# Optimizing a Trainium2 kernel written in Bass

```python
import numpy as np
import jax
import jax.numpy as jnp

def _softmax(x, axis=-1):
    return jax.nn.softmax(x, axis=axis)

def _gelu(x):
    return jax.nn.gelu(x, approximate=True)

def _silu(x):
    return jax.nn.silu(x)

def _sigmoid(x):
    return jax.nn.sigmoid(x)

def _layernorm(x, axis=-1, eps=1e-05):
    m = jnp.mean(x, axis=axis, keepdims=True)
    v = jnp.var(x, axis=axis, keepdims=True)
    return (x - m) / jnp.sqrt(v + eps)

def _scatter_add(tgt, idx, src, axis=0):
    return tgt.at[idx].add(src)

def _segment_sum(src, seg, n):
    return jax.ops.segment_sum(src, seg, n)
kernel_name = 'mk_seq_preln_d2_jaxref_r8_fe4e90'

def setup_inputs(seed: int=0):
    np.random.seed(seed)
    _w = jnp.asarray

    def _L0_attn_setup():
        import jax, jax.numpy as jnp
        import numpy as np
        H, DK, DV, GG = (16, 128, 128, 16)
        NG = DK // GG
        SCALE = DK ** (-0.5)
        EPS = 1e-05

        def _short_conv(x, w):
            K = w.shape[1]
            xp = jnp.pad(x, ((0, 0), (K - 1, 0), (0, 0)))
            y = jax.lax.conv_general_dilated(xp, jnp.transpose(w)[:, None, :], (1,), 'VALID', dimension_numbers=('NWC', 'WIO', 'NWC'), feature_group_count=w.shape[0])
            return jax.nn.silu(y)

        def _l2norm(x, eps=1e-06):
            return x * jax.lax.rsqrt(jnp.sum(x * x, -1, keepdims=True) + eps)

        def _forward(hidden_states, Wq, Wk, Wv, conv_q, conv_k, conv_v, Wf1, Wf2, Wb, A_log, dt_bias, Wg, bg, norm_w, Wo):
            B, T, D = hidden_states.shape
            q = _short_conv(hidden_states @ Wq, conv_q).reshape(B, T, H, DK)
            k = _short_conv(hidden_states @ Wk, conv_k).reshape(B, T, H, DK)
            v = _short_conv(hidden_states @ Wv, conv_v).reshape(B, T, H, DV)
            q = _l2norm(q) * SCALE
            k = _l2norm(k)
            g_grouped = (hidden_states @ Wf1 @ Wf2).reshape(B, T, H, NG)
            g_eff = -jnp.exp(A_log)[:, None] * jax.nn.softplus(g_grouped + dt_bias.reshape(H, NG))
            g_eff = jnp.repeat(g_eff, GG, axis=-1)
            beta = jax.nn.sigmoid(hidden_states @ Wb)

            def step(S, inp):
                qt, kt, vt, gt, bt = inp
                S = S * jnp.exp(gt)[..., None]
                err = jnp.einsum('bhk,bhkv->bhv', kt, S)
                delta = bt[..., None] * (vt - err)
                S = S + kt[..., None] * delta[:, :, None, :]
                ot = jnp.einsum('bhk,bhkv->bhv', qt, S)
                return (S, ot)
            tm = lambda x: jnp.moveaxis(x, 1, 0)
            S0 = jnp.zeros((B, H, DK, DV), hidden_states.dtype)
            _, o = jax.lax.scan(step, S0, (tm(q), tm(k), tm(v), tm(g_eff), tm(beta)))
            o = jnp.moveaxis(o, 0, 1)
            gate = (hidden_states @ Wg + bg).reshape(B, T, H, DV)
            y = o * jax.nn.silu(gate)
            y = y * jax.lax.rsqrt(jnp.mean(y * y, -1, keepdims=True) + EPS) * norm_w
            return y.reshape(B, T, H * DV) @ Wo
        key = jax.random.key(seed)
        ks = jax.random.split(key, 16)
        B, T, D = (2, 128, 256)
        KD, VD = (H * DK, H * DV)
        init = lambda k, sh: jax.random.normal(k, sh, jnp.float32) * 0.02
        return {'hidden_states': jax.random.normal(ks[0], (B, T, D), jnp.float32), 'Wq': init(ks[1], (D, KD)), 'Wk': init(ks[2], (D, KD)), 'Wv': init(ks[3], (D, VD)), 'conv_q': init(ks[4], (KD, 4)), 'conv_k': init(ks[5], (KD, 4)), 'conv_v': init(ks[6], (VD, 4)), 'Wf1': init(ks[7], (D, DV)), 'Wf2': init(ks[8], (DV, H * NG)), 'Wb': init(ks[9], (D, H)), 'A_log': jnp.log(jax.random.uniform(ks[10], (H,), jnp.float32, 1.0, 16.0)), 'dt_bias': jnp.zeros((H * NG,), jnp.float32), 'Wg': init(ks[11], (D, VD)), 'bg': jnp.zeros((VD,), jnp.float32), 'norm_w': jnp.ones((DV,), jnp.float32), 'Wo': init(ks[12], (VD, D))}
    _L0_attn_in = _L0_attn_setup()

    def _L0_ffn_setup():
        import jax, jax.numpy as jnp
        import numpy as np
        SEQ, BS, D, F, E = (128, 2, 256, 256, 8)
        key = jax.random.key(seed)
        ks = jax.random.split(key, 8)
        s = 0.02
        return {'hidden_states': jax.random.normal(ks[0], (SEQ, BS, D), jnp.float32), 'router_w': jax.random.normal(ks[1], (D, E), jnp.float32) * s, 'gate_w': jax.random.normal(ks[2], (E, D, F), jnp.float32) * s, 'up_w': jax.random.normal(ks[3], (E, D, F), jnp.float32) * s, 'down_w': jax.random.normal(ks[4], (E, F, D), jnp.float32) * s, 'shared_gate_w': jax.random.normal(ks[5], (D, F), jnp.float32) * s, 'shared_up_w': jax.random.normal(ks[6], (D, F), jnp.float32) * s, 'shared_down_w': jax.random.normal(ks[7], (F, D), jnp.float32) * s}
    _L0_ffn_in = _L0_ffn_setup()

    def _L1_attn_setup():
        import math
        import jax, jax.numpy as jnp
        import numpy as np
        B, T, E, H = (2, 256, 256, 16)
        D = E // H

        def _alibi_slopes(n):
            start = 2.0 ** (-2.0 ** (-(math.log2(n) - 3)))
            return np.array([start * start ** i for i in range(n)], dtype=np.float32)
        key = jax.random.key(seed)
        ks = jax.random.split(key, 5)
        w_scale = 0.02
        return {'x': jax.random.normal(ks[0], (B, T, E), dtype=jnp.float32), 'Wq': jax.random.normal(ks[1], (E, E), dtype=jnp.float32) * w_scale, 'bq': jnp.zeros((E,), jnp.float32), 'Wk': jax.random.normal(ks[2], (E, E), dtype=jnp.float32) * w_scale, 'bk': jnp.zeros((E,), jnp.float32), 'Wv': jax.random.normal(ks[3], (E, E), dtype=jnp.float32) * w_scale, 'bv': jnp.zeros((E,), jnp.float32), 'Wo': jax.random.normal(ks[4], (E, E), dtype=jnp.float32) * w_scale, 'bo': jnp.zeros((E,), jnp.float32), 'slopes': jnp.asarray(_alibi_slopes(H))}
    _L1_attn_in = _L1_attn_setup()

    def _L1_ffn_setup():
        import jax, jax.numpy as jnp
        import numpy as np
        H = 256
        NH = 16
        NOPE = 128
        ROPE = 64
        VD = 128
        QHD = NOPE + ROPE
        E = 16
        I = 176
        TOPK = 4
        NSH = 2
        SHI = I * NSH
        EPS = 1e-06
        B, S = (2, 128)

        def rmsnorm(x, w):
            return x * jax.lax.rsqrt(jnp.mean(x * x, axis=-1, keepdims=True) + EPS) * w
        key = jax.random.key(seed)
        ks = jax.random.split(key, 12)
        sd = lambda fan_in: 1.0 / np.sqrt(fan_in)
        return {'hidden_states': jax.random.normal(ks[0], (B, S, H), jnp.float32), 'positions': jnp.broadcast_to(jnp.arange(S, dtype=jnp.int32), (B, S)), 'ln1_w': jnp.ones((H,), jnp.float32), 'ln2_w': jnp.ones((H,), jnp.float32), 'q_w': jax.random.normal(ks[1], (NH * QHD, H), jnp.float32) * sd(H), 'kv_w': jax.random.normal(ks[2], (NH * (NOPE + VD) + ROPE, H), jnp.float32) * sd(H), 'o_w': jax.random.normal(ks[3], (H, NH * VD), jnp.float32) * sd(NH * VD), 'gate_w': jax.random.normal(ks[4], (E, H), jnp.float32) * sd(H), 'w1': jax.random.normal(ks[5], (E, 2 * I, H), jnp.float32) * sd(H), 'w2': jax.random.normal(ks[6], (E, H, I), jnp.float32) * sd(I), 'sh_gu_w': jax.random.normal(ks[7], (2 * SHI, H), jnp.float32) * sd(H), 'sh_down_w': jax.random.normal(ks[8], (H, SHI), jnp.float32) * sd(SHI)}
    _L1_ffn_in = _L1_ffn_setup()
    _d = {'L0_attn_hidden_states': _L0_attn_in['hidden_states'], 'L0_attn_Wq': _L0_attn_in['Wq'], 'L0_attn_Wk': _L0_attn_in['Wk'], 'L0_attn_Wv': _L0_attn_in['Wv'], 'L0_attn_conv_q': _L0_attn_in['conv_q'], 'L0_attn_conv_k': _L0_attn_in['conv_k'], 'L0_attn_conv_v': _L0_attn_in['conv_v'], 'L0_attn_Wf1': _L0_attn_in['Wf1'], 'L0_attn_Wf2': _L0_attn_in['Wf2'], 'L0_attn_Wb': _L0_attn_in['Wb'], 'L0_attn_A_log': _L0_attn_in['A_log'], 'L0_attn_dt_bias': _L0_attn_in['dt_bias'], 'L0_attn_Wg': _L0_attn_in['Wg'], 'L0_attn_bg': _L0_attn_in['bg'], 'L0_attn_norm_w': _L0_attn_in['norm_w'], 'L0_attn_Wo': _L0_attn_in['Wo'], 'L0_ffn_router_w': _L0_ffn_in['router_w'], 'L0_ffn_gate_w': _L0_ffn_in['gate_w'], 'L0_ffn_up_w': _L0_ffn_in['up_w'], 'L0_ffn_down_w': _L0_ffn_in['down_w'], 'L0_ffn_shared_gate_w': _L0_ffn_in['shared_gate_w'], 'L0_ffn_shared_up_w': _L0_ffn_in['shared_up_w'], 'L0_ffn_shared_down_w': _L0_ffn_in['shared_down_w'], 'L1_attn_Wq': _L1_attn_in['Wq'], 'L1_attn_bq': _L1_attn_in['bq'], 'L1_attn_Wk': _L1_attn_in['Wk'], 'L1_attn_bk': _L1_attn_in['bk'], 'L1_attn_Wv': _L1_attn_in['Wv'], 'L1_attn_bv': _L1_attn_in['bv'], 'L1_attn_Wo': _L1_attn_in['Wo'], 'L1_attn_bo': _L1_attn_in['bo'], 'L1_attn_slopes': _L1_attn_in['slopes'], 'L1_ffn_positions': _L1_ffn_in['positions'], 'L1_ffn_ln1_w': _L1_ffn_in['ln1_w'], 'L1_ffn_ln2_w': _L1_ffn_in['ln2_w'], 'L1_ffn_q_w': _L1_ffn_in['q_w'], 'L1_ffn_kv_w': _L1_ffn_in['kv_w'], 'L1_ffn_o_w': _L1_ffn_in['o_w'], 'L1_ffn_gate_w': _L1_ffn_in['gate_w'], 'L1_ffn_w1': _L1_ffn_in['w1'], 'L1_ffn_w2': _L1_ffn_in['w2'], 'L1_ffn_sh_gu_w': _L1_ffn_in['sh_gu_w'], 'L1_ffn_sh_down_w': _L1_ffn_in['sh_down_w']}
    _x0 = _d['L0_attn_hidden_states']
    _d['L0_attn_hidden_states'] = jax.random.normal(jax.random.fold_in(jax.random.key(seed), 1), (4, 512, 256), dtype=_x0.dtype)
    del _x0
    return _d

def reference(L0_attn_hidden_states, L0_attn_Wq, L0_attn_Wk, L0_attn_Wv, L0_attn_conv_q, L0_attn_conv_k, L0_attn_conv_v, L0_attn_Wf1, L0_attn_Wf2, L0_attn_Wb, L0_attn_A_log, L0_attn_dt_bias, L0_attn_Wg, L0_attn_bg, L0_attn_norm_w, L0_attn_Wo, L0_ffn_router_w, L0_ffn_gate_w, L0_ffn_up_w, L0_ffn_down_w, L0_ffn_shared_gate_w, L0_ffn_shared_up_w, L0_ffn_shared_down_w, L1_attn_Wq, L1_attn_bq, L1_attn_Wk, L1_attn_bk, L1_attn_Wv, L1_attn_bv, L1_attn_Wo, L1_attn_bo, L1_attn_slopes, L1_ffn_positions, L1_ffn_ln1_w, L1_ffn_ln2_w, L1_ffn_q_w, L1_ffn_kv_w, L1_ffn_o_w, L1_ffn_gate_w, L1_ffn_w1, L1_ffn_w2, L1_ffn_sh_gu_w, L1_ffn_sh_down_w):

    def _L0_attn_ref(hidden_states, Wq, Wk, Wv, conv_q, conv_k, conv_v, Wf1, Wf2, Wb, A_log, dt_bias, Wg, bg, norm_w, Wo):
        import jax, jax.numpy as jnp
        import numpy as np
        H, DK, DV, GG = (16, 128, 128, 16)
        NG = DK // GG
        SCALE = DK ** (-0.5)
        EPS = 1e-05

        def _short_conv(x, w):
            K = w.shape[1]
            xp = jnp.pad(x, ((0, 0), (K - 1, 0), (0, 0)))
            y = jax.lax.conv_general_dilated(xp, jnp.transpose(w)[:, None, :], (1,), 'VALID', dimension_numbers=('NWC', 'WIO', 'NWC'), feature_group_count=w.shape[0])
            return jax.nn.silu(y)

        def _l2norm(x, eps=1e-06):
            return x * jax.lax.rsqrt(jnp.sum(x * x, -1, keepdims=True) + eps)

        def _forward(hidden_states, Wq, Wk, Wv, conv_q, conv_k, conv_v, Wf1, Wf2, Wb, A_log, dt_bias, Wg, bg, norm_w, Wo):
            B, T, D = hidden_states.shape
            q = _short_conv(hidden_states @ Wq, conv_q).reshape(B, T, H, DK)
            k = _short_conv(hidden_states @ Wk, conv_k).reshape(B, T, H, DK)
            v = _short_conv(hidden_states @ Wv, conv_v).reshape(B, T, H, DV)
            q = _l2norm(q) * SCALE
            k = _l2norm(k)
            g_grouped = (hidden_states @ Wf1 @ Wf2).reshape(B, T, H, NG)
            g_eff = -jnp.exp(A_log)[:, None] * jax.nn.softplus(g_grouped + dt_bias.reshape(H, NG))
            g_eff = jnp.repeat(g_eff, GG, axis=-1)
            beta = jax.nn.sigmoid(hidden_states @ Wb)

            def step(S, inp):
                qt, kt, vt, gt, bt = inp
                S = S * jnp.exp(gt)[..., None]
                err = jnp.einsum('bhk,bhkv->bhv', kt, S)
                delta = bt[..., None] * (vt - err)
                S = S + kt[..., None] * delta[:, :, None, :]
                ot = jnp.einsum('bhk,bhkv->bhv', qt, S)
                return (S, ot)
            tm = lambda x: jnp.moveaxis(x, 1, 0)
            S0 = jnp.zeros((B, H, DK, DV), hidden_states.dtype)
            _, o = jax.lax.scan(step, S0, (tm(q), tm(k), tm(v), tm(g_eff), tm(beta)))
            o = jnp.moveaxis(o, 0, 1)
            gate = (hidden_states @ Wg + bg).reshape(B, T, H, DV)
            y = o * jax.nn.silu(gate)
            y = y * jax.lax.rsqrt(jnp.mean(y * y, -1, keepdims=True) + EPS) * norm_w
            return y.reshape(B, T, H * DV) @ Wo
        return _forward(hidden_states, Wq, Wk, Wv, conv_q, conv_k, conv_v, Wf1, Wf2, Wb, A_log, dt_bias, Wg, bg, norm_w, Wo)

    def _L0_ffn_ref(hidden_states, router_w, gate_w, up_w, down_w, shared_gate_w, shared_up_w, shared_down_w):
        import jax, jax.numpy as jnp
        import numpy as np
        SEQ, BS, D, F, E = (128, 2, 256, 256, 8)
        S, B, Dm = hidden_states.shape
        x = hidden_states.reshape(-1, Dm)
        logits = x @ router_w
        expert_idx = jnp.argmax(logits, axis=-1)
        score = jax.nn.sigmoid(jnp.max(logits, axis=-1))
        xs = x * score[:, None]
        n_experts = router_w.shape[1]
        out = jnp.zeros_like(x)
        for e in range(n_experts):
            m = (expert_idx == e)[:, None]
            xe = jnp.where(m, xs, 0.0)
            h = jax.nn.silu(xe @ gate_w[e]) * (xe @ up_w[e])
            out = out + jnp.where(m, h @ down_w[e], 0.0)
        shared = jax.nn.silu(x @ shared_gate_w) * (x @ shared_up_w) @ shared_down_w
        return (out + shared).reshape(S, B, Dm)

    def _L1_attn_ref(x, Wq, bq, Wk, bk, Wv, bv, Wo, bo, slopes):
        import math
        import jax, jax.numpy as jnp
        import numpy as np
        B, T, E, H = (2, 256, 256, 16)
        D = E // H

        def _alibi_slopes(n):
            start = 2.0 ** (-2.0 ** (-(math.log2(n) - 3)))
            return np.array([start * start ** i for i in range(n)], dtype=np.float32)
        b, t, e = x.shape
        h, d = (H, e // H)
        scaling = d ** (-0.5)
        q = (jnp.einsum('bte,fe->btf', x, Wq) + bq) * scaling
        k = jnp.einsum('bte,fe->btf', x, Wk) + bk
        v = jnp.einsum('bte,fe->btf', x, Wv) + bv
        q = q.reshape(b, t, h, d)
        k = k.reshape(b, t, h, d)
        v = v.reshape(b, t, h, d)
        scores = jnp.einsum('bihd,bjhd->bhij', q, k)
        pos = jnp.arange(t)
        alibi = -jnp.abs(pos[None, :] - pos[:, None]).astype(scores.dtype)
        scores = scores + slopes[:, None, None] * alibi
        probs = jax.nn.softmax(scores.astype(jnp.float32), axis=-1).astype(scores.dtype)
        out = jnp.einsum('bhij,bjhd->bihd', probs, v).reshape(b, t, e)
        return jnp.einsum('bte,fe->btf', out, Wo) + bo

    def _L1_ffn_ref(hidden_states, positions, ln1_w, ln2_w, q_w, kv_w, o_w, gate_w, w1, w2, sh_gu_w, sh_down_w):
        import jax, jax.numpy as jnp
        import numpy as np
        H = 256
        NH = 16
        NOPE = 128
        ROPE = 64
        VD = 128
        QHD = NOPE + ROPE
        E = 16
        I = 176
        TOPK = 4
        NSH = 2
        SHI = I * NSH
        EPS = 1e-06
        B, S = (2, 128)

        def rmsnorm(x, w):
            return x * jax.lax.rsqrt(jnp.mean(x * x, axis=-1, keepdims=True) + EPS) * w
        b, s, h = hidden_states.shape
        x = rmsnorm(hidden_states, ln1_w)
        q = jnp.einsum('bsh,dh->bsd', x, q_w).reshape(b, s, NH, QHD)[..., :NOPE]
        kv = jnp.einsum('bsh,dh->bsd', x, kv_w)
        k = kv[..., :NH * NOPE].reshape(b, s, NH, NOPE)
        v = kv[..., NH * NOPE:NH * (NOPE + VD)].reshape(b, s, NH, VD)
        scale = QHD ** (-0.5)
        scores = jnp.einsum('bqnd,bknd->bnqk', q, k) * scale
        causal = jnp.tril(jnp.ones((s, s), bool))
        scores = jnp.where(causal, scores, -1000000000.0)
        p = jax.nn.softmax(scores, axis=-1)
        attn = jnp.einsum('bnqk,bknd->bqnd', p, v).reshape(b, s, NH * VD)
        attn_out = jnp.einsum('bsd,hd->bsh', attn, o_w)
        hid = hidden_states + attn_out
        x2 = rmsnorm(hid, ln2_w).reshape(-1, h)
        logits = x2 @ gate_w.T
        probs = jax.nn.softmax(logits, axis=-1)
        top_w, top_i = jax.lax.top_k(probs, TOPK)
        top_w = top_w / jnp.sum(top_w, axis=-1, keepdims=True)
        wfull = jnp.sum(jax.nn.one_hot(top_i, E, dtype=x2.dtype) * top_w[..., None], axis=1)
        gu = jnp.einsum('th,eih->tei', x2, w1)
        g, u = (gu[..., :I], gu[..., I:])
        act = jax.nn.silu(g) * u
        down = jnp.einsum('tei,ehi->teh', act, w2)
        routed = jnp.einsum('te,teh->th', wfull, down)
        sgu = x2 @ sh_gu_w.T
        sg, su = (sgu[..., :SHI], sgu[..., SHI:])
        shared = jax.nn.silu(sg) * su @ sh_down_w.T
        return hid + (routed + shared).reshape(b, s, h)
    x = L0_attn_hidden_states
    x = x + _L0_attn_ref(_layernorm(x, axis=-1), L0_attn_Wq, L0_attn_Wk, L0_attn_Wv, L0_attn_conv_q, L0_attn_conv_k, L0_attn_conv_v, L0_attn_Wf1, L0_attn_Wf2, L0_attn_Wb, L0_attn_A_log, L0_attn_dt_bias, L0_attn_Wg, L0_attn_bg, L0_attn_norm_w, L0_attn_Wo)
    x = x + _L0_ffn_ref(_layernorm(x, axis=-1), L0_ffn_router_w, L0_ffn_gate_w, L0_ffn_up_w, L0_ffn_down_w, L0_ffn_shared_gate_w, L0_ffn_shared_up_w, L0_ffn_shared_down_w)
    x = x + _L1_attn_ref(_layernorm(x, axis=-1), L1_attn_Wq, L1_attn_bq, L1_attn_Wk, L1_attn_bk, L1_attn_Wv, L1_attn_bv, L1_attn_Wo, L1_attn_bo, L1_attn_slopes)
    x = x + _L1_ffn_ref(_layernorm(x, axis=-1), L1_ffn_positions, L1_ffn_ln1_w, L1_ffn_ln2_w, L1_ffn_q_w, L1_ffn_kv_w, L1_ffn_o_w, L1_ffn_gate_w, L1_ffn_w1, L1_ffn_w2, L1_ffn_sh_gu_w, L1_ffn_sh_down_w)
    return x

_drawn_inputs = setup_inputs


def setup_inputs(seed=0):
    import zlib

    import numpy as np

    out = dict(_drawn_inputs(seed))
    spreads = {'L0_attn_dt_bias': (0.0, 0.8),
     'L0_attn_bg': (0.0, 0.8),
     'L0_attn_norm_w': (1.0, 0.6),
     'L1_attn_bq': (0.0, 2.0),
     'L1_attn_bk': (0.0, 2.0),
     'L1_attn_bv': (0.0, 0.8),
     'L1_attn_bo': (0.0, 0.548),
     'L1_ffn_ln1_w': (1.0, 0.6),
     'L1_ffn_ln2_w': (1.0, 0.555)}
    factors = {'L0_attn_Wq': 8.0,
     'L0_attn_Wk': 8.0,
     'L0_attn_Wv': 8.0,
     'L0_attn_conv_q': 8.0,
     'L0_attn_conv_k': 8.0,
     'L0_attn_conv_v': 8.0,
     'L0_attn_Wf1': 8.0,
     'L0_attn_Wf2': 8.0,
     'L0_attn_Wb': 8.0,
     'L0_attn_A_log': 8.0,
     'L0_attn_Wg': 8.0,
     'L0_attn_Wo': 8.0,
     'L0_ffn_router_w': 6.254,
     'L0_ffn_gate_w': 5.865,
     'L0_ffn_up_w': 5.92,
     'L0_ffn_down_w': 5.991,
     'L1_attn_Wq': 39.907,
     'L1_attn_Wk': 39.38,
     'L0_ffn_shared_gate_w': 8.0,
     'L0_ffn_shared_up_w': 8.0,
     'L0_ffn_shared_down_w': 8.0,
     'L1_attn_Wv': 4.797,
     'L1_attn_Wo': 4.447,
     'L1_attn_slopes': 6.502}
    for name, (base, spread) in spreads.items():
        noise = np.random.default_rng([zlib.crc32(name.encode()), seed]).standard_normal(out[name].shape)
        drawn = base * np.exp(spread * noise) if base else spread * noise
        out[name] = jnp.asarray(drawn.astype(out[name].dtype))
    for name, factor in factors.items():
        out[name] = (out[name] * factor).astype(out[name].dtype)
    return out
```

```python
from contextlib import ExitStack

import numpy as np

import concourse.bass as bass
from concourse import mybir

STAGES = 4

P = 128
F32 = mybir.dt.float32
I32 = mybir.dt.int32
ALU = mybir.AluOpType
ACT = mybir.ActivationFunctionType
AX_X = mybir.AxisListType.X

B, T, D = 4, 512, 256
N = B * T
TILES = N // P
TPB = T // P
KC = D // P
H = 16
BANK = 512
DH = 128
NG = 8
TAPS = 4
LEVELS = 7
HALF = P // 2
E0, F0 = 8, 256
E1, I1, TOPK, NSH = 16, 176, 4, 2
DA = D // H
SLOT = 32
NOPE, ROPE, VD = 128, 64, 128
QHD = NOPE + ROPE
NEG = -1.0e30


def pools(nc, ctx):
    def sb(name, shape, dt=F32):
        return ctx.enter_context(nc.sbuf_tensor(name, shape, dt))

    def ps(name, shape):
        return ctx.enter_context(nc.psum_tensor(name, shape, F32))

    def sem(name):
        return ctx.enter_context(nc.semaphore(name))

    return sb, ps, sem


def rows(ap, n=P):
    return ap.unsqueeze(0).broadcast_to([n, ap.shape[0]])


def load_block(nc, X, x_in, ident, ident_in):
    with ExitStack() as ctx:
        sb, ps, sem = pools(nc, ctx)
        loaded = sem("x_loaded")
        block = ctx.enter_context(nc.Block())

        @block.sync
        def _(sp):
            sp.dma_start(X[:, 0:TILES // 2, :], x_in[:, 0:TILES // 2, :]).then_inc(loaded, 16)
            sp.dma_start(ident[:, :], ident_in).then_inc(loaded, 16)
            sp.wait_ge(loaded, 48)

        @block.scalar
        def _(act):
            act.dma_start(X[:, TILES // 2:, :], x_in[:, TILES // 2:, :]).then_inc(loaded, 16)


def norm_block(nc, tag, X, XT, ident, eps, rms_weight=None, scale_by=None, rows_out=None):
    rms = rms_weight is not None
    with ExitStack() as ctx:
        sb, ps, sem = pools(nc, ctx)
        stats = sb(tag + "stats", [P, TILES, 6])
        mv = sb(tag + "mv", [P, TILES, 2])
        var = sb(tag + "var", [P, TILES])
        std = sb(tag + "std", [P, TILES])
        scale = sb(tag + "scale", [P, TILES])
        shift = sb(tag + "shift", [P, TILES])
        weight = sb(tag + "weight", [P, KC])
        xn = [sb(f"{tag}xn{j}", [P, D]) for j in range(2)]
        bank = [ps(f"{tag}bank{j}", [P, KC, P]) for j in range(2)]
        step = sem(tag + "step")
        var_ready = sem(tag + "var_ready")
        std_ready = sem(tag + "std_ready")
        scale_ready = sem(tag + "scale_ready")
        xn_ready = sem(tag + "xn_ready")
        turned = sem(tag + "turned")
        drained = sem(tag + "drained")
        w_loaded = sem(tag + "w_loaded")
        block = ctx.enter_context(nc.Block())

        @block.sync
        def _(sp):
            if rms:
                sp.dma_start(weight[:, :], rms_weight.rearrange("(c p) -> p c", p=P),
                             allow_slow_non_contiguous=True).then_inc(w_loaded, 16)
                sp.wait_ge(w_loaded, 16)

        @block.vector
        def _(dve):
            for t in range(TILES):
                nc.vector.bn_stats(stats[:, t, :], X[:, t, :]).then_inc(step, 1)
            for t in range(TILES):
                dve.wait_ge(step, t + 1)
                nc.vector.bn_aggr(mv[:, t, :], stats[:, t, :]).then_inc(step, 1)
            dve.wait_ge(step, 2 * TILES)
            if rms:
                nc.vector.tensor_tensor(shift[:, :], mv[:, :, 0], mv[:, :, 0], ALU.mult).then_inc(step, 1)
                dve.wait_ge(step, 2 * TILES + 1)
                nc.vector.scalar_tensor_tensor(var[:, :], mv[:, :, 1], eps, shift[:, :],
                                               ALU.add, ALU.add).then_inc(var_ready, 1)
            else:
                nc.vector.tensor_scalar(var[:, :], mv[:, :, 1], eps, None, ALU.add).then_inc(var_ready, 1)
            dve.wait_ge(std_ready, 1)
            nc.vector.reciprocal(scale[:, :], std[:, :]).then_inc(std_ready, 1)
            dve.wait_ge(std_ready, 2)
            if scale_by is not None:
                nc.vector.tensor_tensor(scale[:, :], scale[:, :], scale_by[:, :], ALU.mult).then_inc(std_ready, 1)
                dve.wait_ge(std_ready, 3)
            nc.vector.scalar_tensor_tensor(shift[:, :], mv[:, :, 0], 0.0 if rms else -1.0, scale[:, :],
                                           ALU.mult, ALU.mult).then_inc(scale_ready, 1)
            if rms:
                dve.wait_ge(w_loaded, 16)
            if rows_out is not None:
                return
            nc.vector.sem_inc(drained, 2)
            with dve.Fori(0, TILES // 2) as i:
                for j in range(2):
                    dve.wait_ge(turned, 2 * i + j + 1)
                    t = 2 * i + j
                    if rms:
                        for c in range(KC):
                            last = nc.vector.tensor_scalar(XT[:, c, bass.ds(t * P, P)], bank[j][:, c, :],
                                                           weight[:, c:c + 1], None, ALU.mult)
                    else:
                        last = nc.vector.tensor_copy(XT[:, :, bass.ds(t * P, P)], bank[j][:, :, :])
                    last.then_inc(drained, 1)

        @block.scalar
        def _(act):
            act.wait_ge(var_ready, 1)
            nc.scalar.activation(std[:, :], var[:, :], ACT.Sqrt).then_inc(std_ready, 1)
            act.wait_ge(scale_ready, 1)
            if rows_out is not None:
                for t in range(TILES):
                    nc.scalar.activation(rows_out[:, t, :], X[:, t, :], ACT.Identity, bias=shift[:, t:t + 1],
                                         scale=scale[:, t:t + 1])
                return
            with act.Fori(0, TILES // 2) as i:
                for j in range(2):
                    act.wait_ge(drained, 2 * i + j + 1)
                    nc.scalar.activation(xn[j][:, :], X[:, bass.ds(2 * i + j, 1), :].rearrange("p a d -> p (a d)"),
                                         ACT.Identity, bias=shift[:, bass.ds(2 * i + j, 1)],
                                         scale=scale[:, bass.ds(2 * i + j, 1)]).then_inc(xn_ready, 1)

        @block.tensor
        def _(pe):
            if rows_out is not None:
                return
            with pe.Fori(0, TILES // 2) as i:
                for j in range(2):
                    pe.wait_ge(drained, 2 * i + j + 1)
                    pe.wait_ge(xn_ready, 2 * i + j + 1)
                    for c in range(KC):
                        last = nc.tensor.transpose(bank[j][:, c, :], xn[j][:, c * P:(c + 1) * P], ident[:, :])
                    last.then_inc(turned, 1)


def decay_block(nc, XT, beta, decay_dram, w):
    with ExitStack() as ctx:
        sb, ps, sem = pools(nc, ctx)
        wf1 = sb("wf1", [P, KC, P])
        wf2 = sb("wf2", [P, P])
        wb = sb("wb", [P, KC, H])
        dtb = sb("dtb", [P, 1])
        alog = sb("alog", [P, 1])
        rate = sb("rate", [P, 1])
        nrate = sb("nrate", [P, 1])
        FT = sb("FT", [P, N])
        z = sb("z", [P, N])
        u = sb("u", [P, N])
        lg = sb("lg", [P, N])
        pol = sb("pol", [P, N])
        pref = sb("pref", [P, N])
        suf = sb("suf", [P, N])
        lev = [sb(f"lev{j}", [P, N]) for j in range(2)]
        acc = ps("dacc", [P, B, T])
        acc_b = ps("dacc_b", [P, TILES, H])
        loaded = sem("d_loaded")
        f_mm = sem("d_f_mm")
        f_sb = sem("d_f_sb")
        g_mm = sem("d_g_mm")
        b_mm = sem("d_b_mm")
        z_ready = sem("d_z")
        act_step = sem("d_act")
        dve_step = sem("d_dve")
        a_ready = sem("d_a")
        lev_ready = sem("d_lev")
        stored = [sem(f"d_stored{j}") for j in range(2)]
        rate_ready = sem("d_rate")
        n_loads = 5
        block = ctx.enter_context(nc.Block())

        @block.sync
        def _(sp):
            sp.dma_start(wf1[:, :, :], w["L0_attn_Wf1"].rearrange("(c p) n -> p c n", p=P)).then_inc(loaded, 16)
            sp.dma_start(wf2[:, :], w["L0_attn_Wf2"]).then_inc(loaded, 16)
            sp.dma_start(wb[:, :, :], w["L0_attn_Wb"].rearrange("(c p) n -> p c n", p=P)).then_inc(loaded, 16)
            sp.dma_start(dtb[:, :], w["L0_attn_dt_bias"].unsqueeze(1)).then_inc(loaded, 16)
            sp.dma_start(alog[:, :], w["L0_attn_A_log"].unsqueeze(1).broadcast_to([H, NG]).unsqueeze(2)
                         ).then_inc(loaded, 16)
            for k in range(LEVELS):
                sp.wait_ge(lev_ready, k + 1)
                sp.dma_start(decay_dram[k], lev[k % 2][:, :]).then_inc(stored[k % 2], 16)
            sp.wait_ge(lev_ready, LEVELS + 1)
            sp.dma_start(decay_dram[LEVELS], pref[:, :]).then_inc(stored[LEVELS % 2], 16)
            sp.dma_start(decay_dram[LEVELS + 1], suf[:, :]).then_inc(stored[(LEVELS + 1) % 2], 16)
            for j in range(2):
                sp.wait_ge(stored[j], 16 * len(range(j, LEVELS + 2, 2)))

        @block.tensor
        def _(pe):
            pe.wait_ge(loaded, 16 * n_loads)
            for b in range(B):
                for c in range(KC):
                    last = nc.tensor.matmul(acc[:, b, :], wf1[:, c, :], XT[:, c, b * T:(b + 1) * T],
                                            start=(c == 0), stop=(c == KC - 1))
                last.then_inc(f_mm, 1)
            for t in range(TILES):
                for c in range(KC):
                    last = nc.tensor.matmul(acc_b[:, t, :], XT[:, c, t * P:(t + 1) * P], wb[:, c, :],
                                            start=(c == 0), stop=(c == KC - 1))
            last.then_inc(b_mm, 1)
            for b in range(B):
                pe.wait_ge(f_sb, b + 1)
                nc.tensor.matmul(acc[:, b, :], wf2[:, :], FT[:, b * T:(b + 1) * T],
                                 start=True, stop=True).then_inc(g_mm, 1)

        @block.scalar
        def _(act):
            for b in range(B):
                act.wait_ge(f_mm, b + 1)
                nc.scalar.activation(FT[:, b * T:(b + 1) * T], acc[:, b, :], ACT.Copy).then_inc(f_sb, 1)
            act.wait_ge(loaded, 16 * n_loads)
            nc.scalar.activation(rate[:, :], alog[:, :], ACT.Exp).then_inc(rate_ready, 1)
            act.wait_ge(z_ready, 1)
            nc.scalar.activation(lg[:, :], z[:, :], ACT.Abs).then_inc(act_step, 1)
            act.wait_ge(act_step, 1)
            nc.scalar.activation(u[:, :], lg[:, :], ACT.Exp, scale=-1.0).then_inc(act_step, 1)
            act.wait_ge(act_step, 2)
            nc.scalar.activation(lg[:, :], u[:, :], ACT.Ln, bias=1.0).then_inc(act_step, 1)
            act.wait_ge(a_ready, 1)
            nc.scalar.activation(pref[:, :], z[:, :], ACT.Exp, scale=nrate[:, 0:1]).then_inc(act_step, 1)
            act.wait_ge(b_mm, 1)
            nc.scalar.activation(beta[:, :, :].rearrange("p h t -> p t h"), acc_b[:, :, :],
                                 ACT.Sigmoid).then_inc(act_step, 1)

        @block.vector
        def _(dve):
            n = [0]

            def then(ins):
                n[0] += 1
                ins.then_inc(dve_step, 1)
                dve.wait_ge(dve_step, n[0])

            dve.wait_ge(loaded, 16 * n_loads)
            for b in range(B):
                dve.wait_ge(g_mm, b + 1)
                last = nc.vector.tensor_scalar(z[:, b * T:(b + 1) * T], acc[:, b, :], dtb[:, 0:1], None, ALU.add)
            last.then_inc(z_ready, 1)
            dve.wait_ge(rate_ready, 1)
            then(nc.vector.tensor_scalar(nrate[:, :], rate[:, :], -1.0, None, ALU.mult))
            dve.wait_ge(act_step, 3)
            then(nc.vector.tensor_scalar(pol[:, :], u[:, :], 1.0 / 5, -1.0 / 4, ALU.mult, ALU.add))
            for k in (3, 2, 1):
                then(nc.vector.tensor_tensor(pol[:, :], pol[:, :], u[:, :], ALU.mult))
                then(nc.vector.tensor_scalar(pol[:, :], pol[:, :], (1.0 if k % 2 else -1.0) / k, None, ALU.add))
            then(nc.vector.tensor_tensor(pol[:, :], pol[:, :], u[:, :], ALU.mult))
            then(nc.vector.tensor_scalar(suf[:, :], u[:, :], 0.03, None, ALU.is_lt))
            then(nc.vector.copy_predicated(lg[:, :], suf[:, :].bitcast(I32), pol[:, :]))
            then(nc.vector.scalar_tensor_tensor(z[:, :], z[:, :], 0.0, lg[:, :], ALU.max, ALU.add))
            nc.vector.memset(suf[:, :], 1.0).then_inc(a_ready, 1)
            dve.wait_ge(a_ready, 1)
            dve.wait_ge(act_step, 4)
            for k in range(LEVELS):
                s = 1 << k
                pv = pref[:, :].rearrange("p (n two s) -> p n two s", two=2, s=s)
                sv = suf[:, :].rearrange("p (n two s) -> p n two s", two=2, s=s)
                lv = lev[k % 2][:, :].rearrange("p (n two s) -> p n two s", two=2, s=s)
                nb = N // (2 * s)
                if k >= 2:
                    dve.wait_ge(stored[k % 2], 16 * (k // 2))
                nc.vector.tensor_copy(lv[:, :, 1, :], pv[:, :, 1, :])
                nc.vector.tensor_copy(lv[:, :, 0, :], sv[:, :, 0, :]).then_inc(lev_ready, 1)
                dve.wait_ge(lev_ready, k + 1)
                then(nc.vector.tensor_tensor(sv[:, :, 0, :], sv[:, :, 0, :],
                                             pv[:, :, 1, s - 1:s].broadcast_to([P, nb, s]), ALU.mult))
                then(nc.vector.tensor_tensor(pv[:, :, 1, :], pv[:, :, 1, :],
                                             pv[:, :, 0, s - 1:s].broadcast_to([P, nb, s]), ALU.mult))
            nc.vector.sem_inc(lev_ready, 1)


def delta_block(nc, X, XT, beta, ident, decay_dram, w, consts):
    PROJ = 3 * B + TPB
    UP = PROJ + 2 * B + 2 * TPB
    UQ = 1 + B + B * LEVELS + (TPB - 1)
    UY = B * LEVELS + (TPB - 1)
    UD = B * LEVELS + TPB
    UT = B * LEVELS + TPB
    assert UP % 2 == 0 and UQ % 2 == 0
    NL = LEVELS + 2
    with ExitStack() as ctx:
        sb, ps, sem = pools(nc, ctx)
        W = sb("W", [P, 4, KC, DH])
        cw = sb("cw", [P, 3, TAPS])
        nw = sb("nw", [P, 1])
        bg = sb("bg", [P, DH])
        wo = sb("wo", [P, D])
        qkv = [sb(nm, [P, N]) for nm in ("QT", "KT", "VT")]
        QT, KT, VT = qkv
        gate = sb("gate", [P, TILES, DH])
        bv = sb("bv", [P, TILES, DH])
        ktm = sb("ktm", [P, TILES, DH])
        dec = sb("dec", [P, 2, N])
        Kl = [sb(f"Kl{j}", [P, N]) for j in range(2)]
        Ql = sb("Ql", [P, 2, N // 2])
        Bl = sb("Bl", [P, LEVELS, 2, 4, P])
        Tm = sb("Tm", [P, TILES, P])
        R = sb("R", [P, TILES, P])
        Aqk = sb("Aqk", [P, TILES, P])
        Ysb = sb("Ysb", [P, 2, 4, HALF])
        S = sb("S", [P, B, DH])
        U = sb("U", [P, B, DH])
        R1 = sb("R1", [P, B, DH])
        y1 = sb("y1", [P, B, DH])
        yT = sb("yT", [P, B, DH])
        junk = sb("junk", [P, DH])
        pend = sb("pend", [P, TILES])
        ones = sb("ones", [P, 1])
        mhalf = sb("mhalf", [P, 2 * TILES])
        ss = sb("ss", [P, 2 * TILES])
        rr = sb("rr", [P, 2 * TILES])
        brk = sb("brk", [P, TILES])
        cc = sb("cc", [P, TILES])
        rq = sb("rq", [P, TILES])
        rq2 = sb("rq2", [P, TILES])
        ysum = sb("ysum", [P, B])
        yms = sb("yms", [P, B])
        yrs = sb("yrs", [P, B])
        yscale = sb("yscale", [P, TPB, B])
        mask = sb("mask", [P, LEVELS, 4 * HALF])
        bankP = [ps(f"bankP{j}", [P, BANK]) for j in range(2)]
        bankQ = [ps(f"bankQ{j}", [P, BANK]) for j in range(2)]
        bankY = ps("bankY", [P, BANK])
        bankD = ps("bankD", [P, BANK])
        bankT = ps("bankT", [P, BANK])
        bankZ = ps("bankZ", [P, BANK])
        P_written, P_drained = sem("P_written"), sem("P_drained")
        Q_written, Q_drained = sem("Q_written"), sem("Q_drained")
        Y_written, Y_drained = sem("Y_written"), sem("Y_drained")
        D_written, D_drained = sem("D_written"), sem("D_drained")
        T_written, T_drained = sem("T_written"), sem("T_drained")
        Z_written, Z_drained = sem("Z_written"), sem("Z_drained")
        const_loaded = sem("const_loaded")
        const_set = sem("const_set")
        w_loaded = sem("a_w_loaded")
        wo_loaded = sem("wo_loaded")
        dec_loaded = [sem(f"dec_loaded{j}") for j in range(2)]
        tap_done = sem("tap_done")
        conv_step = sem("conv_step")
        silu_done = sem("silu_done")
        sq_done = sem("sq_done")
        eye_set = sem("eye_set")
        scaled = sem("scaled")
        ss_ready = sem("ss_ready")
        rr_ready = sem("rr_ready")
        rk_ready = sem("rk_ready")
        R1_ready = sem("R1_ready")
        R1_step = sem("R1_step")
        S_ready = sem("S_ready")
        y1_ready = sem("y1_ready")
        ysq_ready = sem("ysq_ready")
        yms_ready = sem("yms_ready")
        yms_step = sem("yms_step")
        yrs_ready = sem("yrs_ready")
        ysc_ready = sem("ysc_ready")
        pool_turn = sem("pool_turn")
        sp_turn = sem("sp_turn")
        block = ctx.enter_context(nc.Block())

        def up(ap, s):
            return ap.rearrange("p (n two s) -> p n two s", two=2, s=s)[:, :, 1, :]

        def low(ap, s):
            return ap.rearrange("p (n two s) -> p n two s", two=2, s=s)[:, :, 0, :]

        def flat(ap):
            return ap.rearrange("p a b -> p (a b)")

        def blocks(ap, s):
            return ap.rearrange("p (n s) -> p n s", s=s)

        def chunk_of(ap, c):
            return ap.rearrange("p (b c) n -> p c b n", c=TPB)[:, c, :, :]

        def stat_of(ap, c):
            return ap.rearrange("p (b c) -> p c b", c=TPB)[:, c, :]

        @block.sync
        def _(sp):
            sp.dma_start(mask[:, :, :], consts["level_mask"]).then_inc(const_loaded, 16)
            sp.dma_start(nw[:, :], w["L0_attn_norm_w"].unsqueeze(1)).then_inc(const_loaded, 16)
            sp.wait_ge(const_loaded, 32)
            with sp.Fori(0, H) as h:
                sp.wait_ge(P_written, 1 + UP * h)
                sp.sem_inc(sp_turn, 1)
                for k, nm in enumerate(("Wq", "Wk", "Wv", "Wg")):
                    src = w["L0_attn_" + nm].rearrange("(c p) n -> p c n", p=P)
                    sp.dma_start(W[:, k, :, :], src[:, :, bass.ds(h * DH, DH)]).then_inc(w_loaded, 16)
                sp.wait_ge(P_drained, UP * h + 2)
                sp.sem_inc(sp_turn, 1)
                for k, nm in enumerate(("conv_q", "conv_k", "conv_v")):
                    sp.dma_start(cw[:, k, :], w["L0_attn_" + nm][bass.ds(h * DH, DH), :]).then_inc(w_loaded, 16)
                sp.dma_start(bg[:, :], w["L0_attn_bg"].rearrange("(a n) -> a n", a=1)[:, bass.ds(h * DH, DH)]
                             .broadcast_to([P, DH])).then_inc(w_loaded, 16)
                sp.dma_start(wo[:, :], w["L0_attn_Wo"][bass.ds(h * DH, DH), :]).then_inc(wo_loaded, 16)
                for k in range(NL):
                    if k >= 2:
                        sp.wait_ge(scaled, 1 + NL * h + k - 1)
                    else:
                        sp.wait_ge(scaled, 1 + NL * h)
                    sp.sem_inc(sp_turn, 1)
                    src = decay_dram[k][bass.ds(h * NG, NG), :].unsqueeze(1).broadcast_to([NG, P // NG, N])
                    sp.dma_start(dec[:, k % 2, :], src).then_inc(dec_loaded[k % 2], 16)

        @block.gpsimd
        def _(pool):
            nc.gpsimd.sem_inc(scaled, 1)
            nc.gpsimd.memset(ones[:, :], 1.0).then_inc(const_set, 1)
            nc.gpsimd.memset(mhalf[:, :], -0.5).then_inc(const_set, 1)
            nc.gpsimd.memset(Bl[:, :, :, :, :], 0.0).then_inc(const_set, 1)
            pool.wait_ge(const_set, 3)
            with pool.Fori(0, H) as h:
                pool.wait_ge(T_written, 1 + UT * h)
                pool.wait_ge(D_written, 1 + UD * h)
                nc.gpsimd.sem_inc(pool_turn, 1)
                eye = ident[:, :].unsqueeze(1).broadcast_to([P, TILES, P])
                nc.gpsimd.tensor_copy(Tm[:, :, :], eye)
                nc.gpsimd.tensor_copy(R[:, :, :], eye).then_inc(eye_set, 1)
                pool.wait_ge(silu_done, PROJ * h + 2 * B)
                nc.gpsimd.tensor_tensor(Kl[1][:, :], KT[:, :], KT[:, :], ALU.mult)
                nc.gpsimd.tensor_tensor(Kl[0][:, :], QT[:, :], QT[:, :], ALU.mult).then_inc(sq_done, 1)
                pool.wait_ge(ss_ready, h + 1)
                nc.gpsimd.tensor_tensor(rr[:, :], ss[:, :], mhalf[:, :], ALU.pow).then_inc(rr_ready, 1)
                for k in range(NL):
                    s = 1 << k
                    per_head = len(range(k % 2, NL, 2))
                    pool.wait_ge(dec_loaded[k % 2], 16 * (per_head * h + k // 2 + 1))
                    d = dec[:, k % 2, :]
                    if k < LEVELS:
                        pool.wait_ge(Q_written, 1 + UQ * h + (1 if k < 2 else 1 + B + B * (k - 1)))
                        nc.gpsimd.tensor_tensor(Kl[k % 2][:, :], KT[:, :], d, ALU.mult)
                        nc.gpsimd.tensor_tensor(blocks(Ql[:, k % 2, :], s), up(QT[:, :], s), up(d, s),
                                                ALU.mult).then_inc(scaled, 1)
                    elif k == LEVELS:
                        pool.wait_ge(Q_written, 1 + UQ * h + 1 + B + B * LEVELS)
                        nc.gpsimd.tensor_tensor(Kl[1][:, :], KT[:, :], d, ALU.mult)
                        nc.gpsimd.tensor_tensor(flat(Ql[:, :, :]), QT[:, :], d, ALU.mult)
                        nc.gpsimd.tensor_copy(pend[:, :], d.rearrange("p (t n) -> p t n", n=P)[:, :, P - 1]
                                              ).then_inc(scaled, 1)
                    else:
                        nc.gpsimd.tensor_tensor(Kl[0][:, :], KT[:, :], d, ALU.mult).then_inc(scaled, 1)
                for c in range(TPB):
                    pool.wait_ge(yms_ready, TPB * h + c + 1)
                    nc.gpsimd.tensor_tensor(yrs[:, :], yms[:, :], mhalf[:, 0:B], ALU.pow).then_inc(yrs_ready, 1)

        @block.scalar
        def _(act):
            nc.scalar.sem_inc(T_drained, 1)
            nc.scalar.sem_inc(Z_drained, 1)
            act.wait_ge(const_loaded, 32)
            with act.Fori(0, H) as h:
                act.wait_ge(w_loaded, 128 * (h + 1))
                act.wait_ge(scaled, 1 + NL * h)
                act.wait_ge(Q_written, 1 + UQ * h)

                def silu(n):
                    k, b = divmod(n, B)
                    act.wait_ge(conv_step, 3 * (3 * B * h + n + 1))
                    v = qkv[k][:, b * T:(b + 1) * T]
                    nc.scalar.activation(v, v, ACT.Silu).then_inc(silu_done, 1)

                for n in range(3 * B):
                    k, b = divmod(n, B)
                    act.wait_ge(P_written, 1 + UP * h + n + 1)
                    nc.scalar.activation(qkv[k][:, b * T:(b + 1) * T], bankP[n % 2][:, :], ACT.Copy,
                                         scale=cw[:, k, TAPS - 1:TAPS]).then_inc(tap_done, 1)
                    if n >= 1:
                        silu(n - 1)
                silu(3 * B - 1)
                for b in range(TPB):
                    act.wait_ge(P_drained, UP * h + 3 * B + b + 1 + 2)
                    v = gate[:, 4 * b:4 * b + 4, :]
                    nc.scalar.activation(v, v, ACT.Silu).then_inc(silu_done, 1)
                for n in range(B * LEVELS):
                    b = n % B
                    act.wait_ge(T_written, 1 + UT * h + n + 1)
                    nc.scalar.activation(flat(R[:, 4 * b:4 * b + 4, :]), bankT[:, :], ACT.Copy).then_inc(T_drained, 1)
                for c in range(TPB):
                    act.wait_ge(T_written, 1 + UT * h + B * LEVELS + c + 1)
                    nc.scalar.activation(flat(U[:, :, :]), bankT[:, :], ACT.Copy).then_inc(T_drained, 1)
                    act.wait_ge(y1_ready, TPB * h + c + 1)
                    act.wait_ge(yms_step, 1 + TPB * h + c)
                    for b in range(B):
                        if b:
                            act.wait_ge(ysq_ready, B * (TPB * h + c) + b)
                        nc.scalar.activation(junk[:, :], y1[:, b, :], ACT.Square,
                                             accum_out=ysum[:, b:b + 1]).then_inc(ysq_ready, 1)
                    act.wait_ge(Z_written, TPB * h + c + 1)
                    act.wait_ge(P_written, 1 + UP * h + PROJ + 2 * B + 2 * c)
                    nc.scalar.activation(flat(yT[:, :, :]), bankZ[:, :], ACT.Copy,
                                         scale=nw[:, 0:1]).then_inc(Z_drained, 1)

        @block.tensor
        def _(pe):
            for x in (P_written, T_written, D_written, Q_written):
                pe.sem_inc(x, 1)
            pe.wait_ge(const_set, 3)

            def mm(out, lhsT, rhs, first=True, last=True):
                return nc.tensor.matmul(out, lhsT, rhs, start=first, stop=last)

            with pe.Fori(0, H) as h:
                pe.wait_ge(w_loaded, 128 * (h + 1))
                for n in range(3 * B):
                    k, b = divmod(n, B)
                    pe.wait_ge(P_drained, UP * h + n + 1)
                    for c in range(KC):
                        last = mm(bankP[n % 2][:, :], W[:, k, c, :], XT[:, c, b * T:(b + 1) * T], c == 0, c == KC - 1)
                    last.then_inc(P_written, 1)
                for n in range(3 * B, PROJ):
                    pe.wait_ge(P_drained, UP * h + n + 1)
                    for i in range(4):
                        t = 4 * (n - 3 * B) + i
                        for c in range(KC):
                            last = mm(bankP[n % 2][:, i * DH:(i + 1) * DH], XT[:, c, t * P:(t + 1) * P],
                                      W[:, 3, c, :], c == 0, c == KC - 1)
                    last.then_inc(P_written, 1)
                pe.wait_ge(sq_done, h + 1)
                pe.wait_ge(Q_drained, UQ * h + 1)
                for j in range(2):
                    for t in range(TILES):
                        last = mm(bankQ[0][:, j * TILES + t:j * TILES + t + 1], Kl[1 - j][:, t * P:(t + 1) * P],
                                  ones[:, :])
                last.then_inc(Q_written, 1)
                pe.wait_ge(silu_done, PROJ * h + 3 * B)
                for b in range(B):
                    n = PROJ + b
                    pe.wait_ge(P_drained, UP * h + n + 1)
                    for i in range(4):
                        t = 4 * b + i
                        last = nc.tensor.transpose(bankP[n % 2][:, i * P:(i + 1) * P], VT[:, t * P:(t + 1) * P],
                                                   ident[:, :])
                    last.then_inc(P_written, 1)
                for b in range(B):
                    q = 1 + b
                    pe.wait_ge(Q_drained, UQ * h + q + 1)
                    for i in range(4):
                        t = 4 * b + i
                        last = mm(bankQ[q % 2][:, i * P:(i + 1) * P], KT[:, t * P:(t + 1) * P], QT[:, t * P:(t + 1) * P])
                    last.then_inc(Q_written, 1)
                pe.wait_ge(eye_set, h + 1)

                def pairs(n):
                    l, b = divmod(n, B)
                    q, s = 1 + B + n, 1 << l
                    pe.wait_ge(scaled, 1 + NL * h + l + 1)
                    pe.wait_ge(Q_drained, UQ * h + q + 1)
                    for i in range(4):
                        t = 4 * b + i
                        k = Kl[l % 2][:, t * P:(t + 1) * P]
                        mm(blocks(bankQ[q % 2][:, i * HALF:(i + 1) * HALF], s), k, up(k, s))
                        last = mm(bankQ[q % 2][:, (4 + i) * HALF:(5 + i) * HALF], k,
                                  Ql[:, l % 2, t * HALF:(t + 1) * HALF])
                    last.then_inc(Q_written, 1)

                def merge_a(n):
                    l, b = divmod(n, B)
                    s = 1 << l
                    pe.wait_ge(Q_drained, UQ * h + 1 + B + n + 1 + 2)
                    pe.wait_ge(Y_drained, UY * h + n + 1)
                    if l:
                        pe.wait_ge(D_drained, UD * h + n - B + 1 + 1)
                    for i in range(4):
                        t = 4 * b + i
                        last = mm(blocks(bankY[:, i * HALF:(i + 1) * HALF], s), Bl[:, l, b % 2, i, :],
                                  low(Tm[:, t, :], s))
                    last.then_inc(Y_written, 1)

                def merge_b(n):
                    l, b = divmod(n, B)
                    pe.wait_ge(Y_drained, UY * h + n + 1 + 1)
                    pe.wait_ge(D_drained, UD * h + n + 1)
                    if l:
                        pe.wait_ge(T_drained, UT * h + n - B + 1 + 1)
                    for i in range(4):
                        last = mm(bankD[:, i * HALF:(i + 1) * HALF], R[:, 4 * b + i, :], Ysb[:, b % 2, i, :])
                    last.then_inc(D_written, 1)

                def turn(n):
                    b = n % B
                    pe.wait_ge(D_drained, UD * h + n + 1 + 1)
                    pe.wait_ge(T_drained, UT * h + n + 1)
                    for i in range(4):
                        last = nc.tensor.transpose(bankT[:, i * P:(i + 1) * P], Tm[:, 4 * b + i, :], ident[:, :])
                    last.then_inc(T_written, 1)

                for n in range(B * LEVELS + 3):
                    for lag, part in enumerate((pairs, merge_a, merge_b, turn)):
                        if 0 <= n - lag < B * LEVELS:
                            part(n - lag)
                pe.wait_ge(scaled, 1 + NL * (h + 1))
                for b in range(B):
                    n = PROJ + B + b
                    pe.wait_ge(P_drained, UP * h + n + 1)
                    for i in range(4):
                        t = 4 * b + i
                        last = nc.tensor.transpose(bankP[n % 2][:, i * P:(i + 1) * P], Kl[0][:, t * P:(t + 1) * P],
                                                   ident[:, :])
                    last.then_inc(P_written, 1)

                def y_out(c):
                    pe.wait_ge(Z_drained, TPB * h + c + 1)
                    pe.wait_ge(y1_ready, TPB * h + c + 1)
                    for b in range(B):
                        last = nc.tensor.transpose(bankZ[:, b * P:(b + 1) * P], y1[:, b, :], ident[:, :])
                    last.then_inc(Z_written, 1)
                    pe.wait_ge(Z_drained, TPB * h + c + 1 + 1)
                    for g in range(2):
                        n = PROJ + 2 * B + 2 * c + g
                        pe.wait_ge(P_drained, UP * h + n + 1)
                        for i in range(2):
                            last = mm(bankP[n % 2][:, i * D:(i + 1) * D], yT[:, 2 * g + i, :], wo[:, :])
                        last.then_inc(P_written, 1)

                pe.wait_ge(wo_loaded, 16 * (h + 1))
                for c in range(TPB):
                    tok = [slice((b * TPB + c) * P, (b * TPB + c + 1) * P) for b in range(B)]
                    qd = flat(Ql[:, :, :])
                    if c:
                        pe.wait_ge(S_ready, (TPB - 1) * h + c)
                        pe.wait_ge(Y_drained, UY * h + B * LEVELS + c - 1 + 1)
                        for b in range(B):
                            last = mm(bankY[:, b * P:(b + 1) * P], Kl[1][:, tok[b]], S[:, b, :])
                        last.then_inc(Y_written, 1)
                        pe.wait_ge(R1_ready, (TPB - 1) * h + c)
                    pe.wait_ge(T_drained, UT * h + B * LEVELS + c + 1)
                    if c == 0:
                        pe.wait_ge(P_drained, UP * h + PROJ + B + 2)
                    for b in range(B):
                        t = b * TPB + c
                        last = mm(bankT[:, b * P:(b + 1) * P], R[:, t, :], R1[:, b, :] if c else bv[:, t, :])
                    last.then_inc(T_written, 1)
                    if c:
                        y_out(c - 1)
                    pe.wait_ge(T_drained, UT * h + B * LEVELS + c + 1 + 1)
                    pe.wait_ge(D_drained, UD * h + B * LEVELS + c + 1)
                    for b in range(B):
                        t = b * TPB + c
                        if c:
                            mm(bankD[:, b * P:(b + 1) * P], qd[:, tok[b]], S[:, b, :], True, False)
                        last = mm(bankD[:, b * P:(b + 1) * P], Aqk[:, t, :], U[:, b, :], not c, True)
                    last.then_inc(D_written, 1)
                    if c < TPB - 1:
                        q = 1 + B + B * LEVELS + c
                        pe.wait_ge(Q_drained, UQ * h + q + 1)
                        pe.wait_ge(P_drained, UP * h + PROJ + 2 * B + 2)
                        for b in range(B):
                            last = mm(bankQ[q % 2][:, b * P:(b + 1) * P], ktm[:, b * TPB + c, :], U[:, b, :])
                        last.then_inc(Q_written, 1)
                y_out(TPB - 1)

        @block.vector
        def _(dve):
            nc.vector.sem_inc(P_drained, 2)
            nc.vector.sem_inc(Q_drained, 2)
            nc.vector.sem_inc(Y_drained, 1)
            nc.vector.sem_inc(D_drained, 1)
            nc.vector.sem_inc(yms_step, 1)
            dve.wait_ge(const_loaded, 32)
            dve.wait_ge(const_set, 3)
            with dve.Fori(0, H) as h:
                dve.wait_ge(w_loaded, 128 * (h + 1))
                for n in range(3 * B):
                    k, b = divmod(n, B)
                    dve.wait_ge(tap_done, 3 * B * h + n + 1)
                    for j in range(1, TAPS):
                        m = 3 * (3 * B * h + n) + j
                        if j > 1:
                            dve.wait_ge(conv_step, m - 1)
                        v = qkv[k][:, b * T + j:(b + 1) * T]
                        ins = nc.vector.scalar_tensor_tensor(v, bankP[n % 2][:, 0:T - j],
                                                             cw[:, k, TAPS - 1 - j:TAPS - j], v, ALU.mult, ALU.add)
                        ins.then_inc(conv_step, 1)
                    dve.wait_ge(conv_step, 3 * (3 * B * h + n) + 3)
                    nc.vector.sem_inc(P_drained, 1)
                for n in range(3 * B, PROJ):
                    dve.wait_ge(P_written, 1 + UP * h + n + 1)
                    b = n - 3 * B
                    nc.vector.tensor_tensor(gate[:, 4 * b:4 * b + 4, :],
                                            bankP[n % 2][:, :].rearrange("p (i n) -> p i n", n=DH),
                                            bg[:, :].unsqueeze(1).broadcast_to([P, 4, DH]),
                                            ALU.add).then_inc(P_drained, 1)
                dve.wait_ge(Q_written, 1 + UQ * h + 1)
                nc.vector.tensor_scalar(ss[:, :], bankQ[0][:, 0:2 * TILES], 1e-6, None, ALU.add).then_inc(ss_ready, 1)
                dve.wait_ge(ss_ready, h + 1)
                nc.vector.sem_inc(Q_drained, 1)
                dve.wait_ge(rr_ready, h + 1)
                rk = rr[:, 0:TILES]
                nc.vector.tensor_scalar(rq[:, :], rr[:, TILES:2 * TILES], float(DH) ** -0.5, None,
                                        ALU.mult).then_inc(rk_ready, 1)
                nc.vector.tensor_tensor(brk[:, :], rk, beta[:, bass.ds(h, 1), :].rearrange("p a t -> p (a t)"),
                                        ALU.mult).then_inc(rk_ready, 1)
                dve.wait_ge(rk_ready, 4 * h + 2)
                nc.vector.tensor_tensor(cc[:, :], brk[:, :], rk, ALU.mult).then_inc(rk_ready, 1)
                nc.vector.scalar_tensor_tensor(rq2[:, :], rq[:, :], 1.0 / DH, rq[:, :], ALU.mult,
                                               ALU.mult).then_inc(rk_ready, 1)
                dve.wait_ge(rk_ready, 4 * h + 4)
                for b in range(B):
                    n = PROJ + b
                    dve.wait_ge(P_written, 1 + UP * h + n + 1)
                    nc.vector.tensor_tensor(bv[:, 4 * b:4 * b + 4, :],
                                            bankP[n % 2][:, :].rearrange("p (i n) -> p i n", n=DH),
                                            brk[:, 4 * b:4 * b + 4].unsqueeze(2).broadcast_to([P, 4, DH]),
                                            ALU.mult).then_inc(P_drained, 1)
                for b in range(B):
                    q = 1 + b
                    dve.wait_ge(Q_written, 1 + UQ * h + q + 1)
                    nc.vector.tensor_tensor(Aqk[:, 4 * b:4 * b + 4, :],
                                            bankQ[q % 2][:, :].rearrange("p (i n) -> p i n", n=P),
                                            ident[:, :].unsqueeze(1).broadcast_to([P, 4, P]),
                                            ALU.mult).then_inc(Q_drained, 1)

                def take_pairs(n):
                    l, b = divmod(n, B)
                    q, s = 1 + B + n, 1 << l
                    dve.wait_ge(Q_written, 1 + UQ * h + q + 1)
                    if b >= 2:
                        dve.wait_ge(Y_written, UY * h + n - 2 + 1)
                    nc.vector.tensor_tensor(up(flat(Bl[:, l, b % 2, :, :]), s), blocks(bankQ[q % 2][:, 0:4 * HALF], s),
                                            blocks(mask[:, l, :], s), ALU.mult)
                    nc.vector.copy_predicated(up(flat(Aqk[:, 4 * b:4 * b + 4, :]), s),
                                              blocks(mask[:, l, :], s).bitcast(I32),
                                              blocks(bankQ[q % 2][:, 4 * HALF:8 * HALF], s)).then_inc(Q_drained, 1)

                def take_a(n):
                    b = n % B
                    dve.wait_ge(Y_written, UY * h + n + 1)
                    nc.vector.tensor_tensor(Ysb[:, b % 2, :, :],
                                            bankY[:, 0:4 * HALF].rearrange("p (i n) -> p i n", n=HALF),
                                            cc[:, 4 * b:4 * b + 4].unsqueeze(2).broadcast_to([P, 4, HALF]),
                                            ALU.mult).then_inc(Y_drained, 1)

                def take_b(n):
                    l, b = divmod(n, B)
                    s = 1 << l
                    dve.wait_ge(D_written, 1 + UD * h + n + 1)
                    v = low(flat(Tm[:, 4 * b:4 * b + 4, :]), s)
                    nc.vector.tensor_tensor(v, v, blocks(bankD[:, 0:4 * HALF], s), ALU.subtract).then_inc(D_drained, 1)

                for n in range(B * LEVELS + 2):
                    for lag, part in enumerate((take_pairs, take_a, take_b)):
                        if 0 <= n - lag < B * LEVELS:
                            part(n - lag)
                for b in range(B):
                    n = PROJ + B + b
                    dve.wait_ge(P_written, 1 + UP * h + n + 1)
                    nc.vector.tensor_copy(flat(ktm[:, 4 * b:4 * b + 4, :]), bankP[n % 2][:, :]).then_inc(P_drained, 1)

                def add_out(c):
                    dve.wait_ge(yrs_ready, TPB * h + c + 1)
                    nc.vector.tensor_tensor(yscale[:, c, :], yrs[:, :], stat_of(rq[:, :], c),
                                            ALU.mult).then_inc(ysc_ready, 1)
                    dve.wait_ge(ysc_ready, TPB * h + c + 1)
                    for g in range(2):
                        n = PROJ + 2 * B + 2 * c + g
                        dve.wait_ge(P_written, 1 + UP * h + n + 1)
                        for i in range(2):
                            b = 2 * g + i
                            x = X[:, b * TPB + c, :]
                            last = nc.vector.scalar_tensor_tensor(x, bankP[n % 2][:, i * D:(i + 1) * D],
                                                                  yscale[:, c, b:b + 1], x, ALU.mult, ALU.add)
                        last.then_inc(P_drained, 1)

                dve.wait_ge(silu_done, PROJ * (h + 1))
                dve.wait_ge(scaled, 1 + NL * (h + 1))
                for c in range(TPB):
                    if c:
                        k = (TPB - 1) * h + c
                        dve.wait_ge(Y_written, UY * h + B * LEVELS + c)
                        nc.vector.tensor_tensor(R1[:, :, :], bankY[:, :].rearrange("p (b n) -> p b n", n=DH),
                                                stat_of(cc[:, :], c).unsqueeze(2).broadcast_to([P, B, DH]),
                                                ALU.mult).then_inc(Y_drained, 1)
                        dve.wait_ge(Y_drained, UY * h + B * LEVELS + c + 1)
                        nc.vector.tensor_tensor(R1[:, :, :], chunk_of(bv[:, :, :], c), R1[:, :, :],
                                                ALU.subtract).then_inc(R1_ready, 1)
                    dve.wait_ge(D_written, 1 + UD * h + B * LEVELS + c + 1)
                    if c:
                        dve.wait_ge(Z_written, TPB * h + c)
                        dve.wait_ge(ysq_ready, B * (TPB * h + c))
                    nc.vector.tensor_tensor(y1[:, :, :], bankD[:, :].rearrange("p (b n) -> p b n", n=DH),
                                            chunk_of(gate[:, :, :], c), ALU.mult).then_inc(D_drained, 1)
                    dve.wait_ge(D_drained, UD * h + B * LEVELS + c + 1 + 1)
                    nc.vector.sem_inc(y1_ready, 1)
                    if c < TPB - 1:
                        q = 1 + B + B * LEVELS + c
                        dve.wait_ge(Q_written, 1 + UQ * h + q + 1)
                        if c == 0:
                            nc.vector.tensor_copy(flat(S[:, :, :]), bankQ[q % 2][:, :]).then_inc(S_ready, 1)
                        else:
                            for b in range(B):
                                t = b * TPB + c
                                last = nc.vector.scalar_tensor_tensor(S[:, b, :], S[:, b, :], pend[:, t:t + 1],
                                                                      bankQ[q % 2][:, b * P:(b + 1) * P],
                                                                      ALU.mult, ALU.add)
                            last.then_inc(S_ready, 1)
                        dve.wait_ge(S_ready, (TPB - 1) * h + c + 1)
                        nc.vector.sem_inc(Q_drained, 1)
                    if c:
                        add_out(c - 1)
                    dve.wait_ge(ysq_ready, B * (TPB * h + c + 1))
                    nc.vector.tensor_tensor(yms[:, :], ysum[:, :], stat_of(rq2[:, :], c), ALU.mult).then_inc(yms_step, 1)
                    dve.wait_ge(yms_step, 1 + TPB * h + c + 1)
                    nc.vector.tensor_scalar(yms[:, :], yms[:, :], 1e-5, None, ALU.add).then_inc(yms_ready, 1)
                add_out(TPB - 1)


def pick_first_max(nc, link, left, picked, rank, E, tmp, mx):
    link(nc.vector.tensor_reduce(mx[:, :], left, AX_X, ALU.max))
    link(nc.vector.tensor_tensor(tmp, left, mx[:, :].unsqueeze(2).broadcast_to([P, TILES, E]), ALU.is_ge))
    link(nc.vector.tensor_tensor(tmp, tmp, rank, ALU.mult))
    link(nc.vector.tensor_reduce(mx[:, :], tmp, AX_X, ALU.max))
    link(nc.vector.tensor_tensor(picked, tmp, mx[:, :].unsqueeze(2).broadcast_to([P, TILES, E]), ALU.is_equal))


def router_block(nc, tag, XT, router, E, rank_in, weights, score=None):
    with ExitStack() as ctx:
        sb, ps, sem = pools(nc, ctx)
        rw = sb(tag + "rw", [P, KC, E])
        rank = sb(tag + "rank", [P, TILES, E])
        lg = sb(tag + "lg", [P, TILES, E])
        left = sb(tag + "left", [P, TILES, E])
        tmp = sb(tag + "tmp", [P, TILES, E])
        picked = sb(tag + "picked", [P, TILES, E])
        total = sb(tag + "total", [P, TILES, E])
        mx = sb(tag + "mx", [P, TILES])
        bank = ps(tag + "bank", [P, TILES, E])
        loaded = sem(tag + "loaded")
        logits = sem(tag + "logits")
        step = sem(tag + "step")
        for_act = sem(tag + "for_act")
        from_act = sem(tag + "from_act")
        block = ctx.enter_context(nc.Block())

        @block.sync
        def _(sp):
            sp.dma_start(rw[:, :, :], router.rearrange("(c p) n -> p c n", p=P)).then_inc(loaded, 16)
            sp.dma_start(rank[:, :, :], rank_in).then_inc(loaded, 16)
            sp.wait_ge(loaded, 32)

        @block.tensor
        def _(pe):
            pe.wait_ge(loaded, 32)
            for t in range(TILES):
                for c in range(KC):
                    last = nc.tensor.matmul(bank[:, t, :], XT[:, c, t * P:(t + 1) * P], rw[:, c, :],
                                            start=(c == 0), stop=(c == KC - 1))
            last.then_inc(logits, 1)

        @block.scalar
        def _(act):
            act.wait_ge(for_act, 1)
            if score is not None:
                nc.scalar.activation(score[:, :], mx[:, :], ACT.Sigmoid).then_inc(from_act, 1)
            else:
                nc.scalar.activation(lg[:, :, :], lg[:, :, :], ACT.Exp).then_inc(from_act, 1)

        @block.vector
        def _(dve):
            n = [0]

            def link(ins):
                n[0] += 1
                ins.then_inc(step, 1)
                dve.wait_ge(step, n[0])

            dve.wait_ge(loaded, 32)
            dve.wait_ge(logits, 1)
            link(nc.vector.tensor_copy(lg[:, :, :], bank[:, :, :]))
            link(nc.vector.tensor_reduce(mx[:, :], lg[:, :, :], AX_X, ALU.max))
            if score is not None:
                nc.vector.sem_inc(for_act, 1)
                dve.wait_ge(from_act, 1)
                pick_first_max(nc, link, lg[:, :, :], picked[:, :, :], rank[:, :, :], E, tmp[:, :, :], mx)
                link(nc.vector.tensor_copy(weights[:, 0:E, :].rearrange("p e t -> p t e"), picked[:, :, :]))
            else:
                link(nc.vector.tensor_tensor(lg[:, :, :], lg[:, :, :],
                                             mx[:, :].unsqueeze(2).broadcast_to([P, TILES, E]), ALU.subtract))
                nc.vector.sem_inc(for_act, 1)
                dve.wait_ge(from_act, 1)
                link(nc.vector.tensor_copy(left[:, :, :], lg[:, :, :]))
                link(nc.vector.memset(total[:, :, :], 0.0))
                for _ in range(TOPK):
                    pick_first_max(nc, link, left[:, :, :], picked[:, :, :], rank[:, :, :], E, tmp[:, :, :], mx)
                    link(nc.vector.tensor_tensor(total[:, :, :], total[:, :, :], picked[:, :, :], ALU.add))
                    link(nc.vector.scalar_tensor_tensor(left[:, :, :], picked[:, :, :], -4.0, left[:, :, :],
                                                        ALU.mult, ALU.add))
                link(nc.vector.tensor_tensor(lg[:, :, :], lg[:, :, :], total[:, :, :], ALU.mult))
                link(nc.vector.tensor_reduce(mx[:, :], lg[:, :, :], AX_X, ALU.add))
                link(nc.vector.reciprocal(mx[:, :], mx[:, :]))
                link(nc.vector.tensor_tensor(weights[:, 0:E, :].rearrange("p e t -> p t e"), lg[:, :, :],
                                             mx[:, :].unsqueeze(2).broadcast_to([P, TILES, E]), ALU.mult))
            link(nc.vector.memset(weights[:, E:, :], 1.0))


def experts_block(nc, tag, X, runs, weights, gate_up, down, FP):
    FC = 2
    with ExitStack() as ctx:
        sb, ps, sem = pools(nc, ctx)
        gu = [sb(f"{tag}gu{j}", [P, KC, 2, FC, FP]) for j in range(2)]
        dn = [sb(f"{tag}dn{j}", [P, FC, D]) for j in range(2)]
        sg = [sb(f"{tag}sg{j}", [P, T]) for j in range(2)]
        hT = [sb(f"{tag}hT{j}", [P, FC, T]) for j in range(2)]
        bank_g = [ps(f"{tag}bank_g{j}", [P, T]) for j in range(2)]
        bank_u = [ps(f"{tag}bank_u{j}", [P, T]) for j in range(2)]
        bank_d = [ps(f"{tag}bank_d{j}", [P, 2, D]) for j in range(2)]
        loaded = [sem(f"{tag}loaded{j}") for j in range(2)]
        used = sem(tag + "used")
        sp_turn = sem(tag + "sp_turn")
        g_written, u_written = sem(tag + "g_written"), sem(tag + "u_written")
        silu_done = sem(tag + "silu_done")
        h_ready = sem(tag + "h_ready")
        d_written, d_drained = sem(tag + "d_written"), sem(tag + "d_drained")
        block = ctx.enter_context(nc.Block())
        UF = FC * B
        UDN = 2 * B

        def over(eng, body):
            for first, count, xt in runs:
                if count >= 2:
                    assert count % 2 == 0 and first % 2 == 0
                    with eng.Fori(0, count // 2) as i:
                        for j in range(2):
                            body(2 * i + (first + j), j, i + first // 2, xt)
                else:
                    body(first, first % 2, first // 2, xt)

        @block.sync
        def _(sp):
            def body(e, j, pair, xt):
                sp.wait_ge(used, e + 1)
                sp.sem_inc(sp_turn, 1)
                for part in range(2):
                    sp.dma_start(gu[j][:, :, part, :, :].rearrange("p c f n -> p c (f n)"),
                                 gate_up[part][bass.ds(e, 1), :, :].rearrange("e (c p) n -> p c (e n)", p=P)
                                 if not isinstance(e, int) else
                                 gate_up[part][e].rearrange("(c p) n -> p c n", p=P)).then_inc(loaded[j], 16)
                sp.dma_start(dn[j][0:FP, :, :],
                             down[bass.ds(e, 1), :, :].rearrange("e (f q) n -> q f (e n)", q=FP)
                             if not isinstance(e, int) else
                             down[e].rearrange("(f q) n -> q f n", q=FP)).then_inc(loaded[j], 16)
            over(sp, body)

        @block.tensor
        def _(pe):
            pe.sem_inc(d_written, 1)

            def body(e, j, pair, xt):
                def up(b):
                    for f in range(FC):
                        n = FC * b + f
                        for part, bank, written in ((0, bank_g, g_written), (1, bank_u, u_written)):
                            pe.wait_ge(h_ready, UF * e + n + 1)
                            for c in range(KC):
                                last = nc.tensor.matmul(bank[f][0:FP, :], gu[j][:, c, part, f, :],
                                                        xt[:, c, b * T:(b + 1) * T],
                                                        start=(c == 0), stop=(c == KC - 1))
                            last.then_inc(written, 1)

                def down_b(b):
                    pe.wait_ge(h_ready, UF * e + FC * (b + 1) + 2)
                    for g in range(2):
                        pe.wait_ge(d_drained, UDN * e + 2 * b + g + 1)
                        for i in range(2):
                            t = 2 * g + i
                            for f in range(FC):
                                last = nc.tensor.matmul(bank_d[g][:, i, :], hT[b % 2][0:FP, f, t * P:(t + 1) * P],
                                                        dn[j][0:FP, f, :], start=(f == 0), stop=(f == FC - 1))
                        last.then_inc(d_written, 1)

                pe.wait_ge(loaded[j], 48 * (pair + 1))
                for b in range(B + 1):
                    if b < B:
                        up(b)
                    if b >= 1:
                        down_b(b - 1)
            over(pe, body)

        @block.scalar
        def _(act):
            def body(e, j, pair, xt):
                for n in range(UF):
                    f = n % FC
                    act.wait_ge(g_written, UF * e + n + 1)
                    act.wait_ge(h_ready, UF * e + n + 1)
                    nc.scalar.activation(sg[f][0:FP, :], bank_g[f][0:FP, :], ACT.Silu).then_inc(silu_done, 1)
            over(act, body)

        @block.vector
        def _(dve):
            nc.vector.sem_inc(used, 2)
            nc.vector.sem_inc(h_ready, 2)
            nc.vector.sem_inc(d_drained, 2)

            def body(e, j, pair, xt):
                def take_down(b):
                    for g in range(2):
                        dve.wait_ge(d_written, 1 + UDN * e + 2 * b + g + 1)
                        for i in range(2):
                            t = 4 * b + 2 * g + i
                            wt = weights[:, e, t:t + 1] if isinstance(e, int) else \
                                weights[:, bass.ds(e, 1), t:t + 1].rearrange("p a b -> p (a b)")
                            last = nc.vector.scalar_tensor_tensor(X[:, t, :], bank_d[g][:, i, :], wt, X[:, t, :],
                                                                  ALU.mult, ALU.add)
                        last.then_inc(d_drained, 1)

                for b in range(B + 1):
                    if b < B:
                        for f in range(FC):
                            n = FC * b + f
                            dve.wait_ge(u_written, UF * e + n + 1)
                            dve.wait_ge(silu_done, UF * e + n + 1)
                            if b >= 2:
                                dve.wait_ge(d_written, 1 + UDN * e + 2 * (b - 1))
                            else:
                                dve.wait_ge(d_written, 1 + UDN * e)
                            nc.vector.tensor_tensor(hT[b % 2][0:FP, f, :], sg[f][0:FP, :], bank_u[f][0:FP, :],
                                                    ALU.mult).then_inc(h_ready, 1)
                    if b >= 1:
                        take_down(b - 1)
                nc.vector.sem_inc(used, 1)
            over(dve, body)


def alibi_block(nc, X, XT, ident, w, consts):
    HQ = P // SLOT
    TBL = 2 * T - P
    UNITS = TPB * H
    with ExitStack() as ctx:
        sb, ps, sem = pools(nc, ctx)
        wq = sb("c_wq", [P, KC, H, SLOT])
        wk = sb("c_wk", [P, KC, H, SLOT])
        wv = sb("c_wv", [P, KC, D])
        wo = sb("c_wo", [P, KC, D])
        bq = sb("c_bq", [P, H // HQ])
        bk = sb("c_bk", [P, H // HQ])
        bvr = sb("c_bv", [P, D])
        bor = sb("c_bo", [P, D])
        slopes = sb("c_slopes", [P, H])
        dist = sb("c_dist", [P, TBL])
        table = sb("c_table", [P, H, TBL])
        V = sb("c_V", [P, TILES, D])
        Vb = sb("c_Vb", [P, TPB, D])
        Q = sb("c_Q", [P, H // HQ, T])
        K = sb("c_K", [P, H // HQ, T])
        s = [sb(f"c_s{j}", [P, T]) for j in range(2)]
        pr = [sb(f"c_p{j}", [P, T]) for j in range(2)]
        pT = [sb(f"c_pT{j}", [P, T]) for j in range(2)]
        nmax = sb("c_nmax", [P, 2])
        rsum = sb("c_rsum", [P, 2, H])
        rinv = sb("c_rinv", [P, H])
        o = sb("c_o", [P, H, DA])
        oT = sb("c_oT", [P, KC, P])
        bank_s = [ps(f"c_bank_s{j}", [P, T]) for j in range(2)]
        bank_t = [ps(f"c_bank_t{j}", [P, T]) for j in range(2)]
        bank_o = ps("c_bank_o", [P, H, DA])
        bank_p = [ps(f"c_bank_p{j}", [P, T]) for j in range(2)]
        bank_x = ps("c_bank_x", [P, D])
        loaded = sem("c_loaded")
        zeroed = sem("c_zeroed")
        table_ready = sem("c_table_ready")
        p_written, p_drained = sem("c_p_written"), sem("c_p_drained")
        s_written, s_taken = sem("c_s_written"), sem("c_s_taken")
        exp_done = sem("c_exp_done")
        t_written, t_taken = sem("c_t_written"), sem("c_t_taken")
        o_written, o_taken = sem("c_o_written"), sem("c_o_taken")
        rinv_ready = sem("c_rinv_ready")
        oT_written, oT_taken = sem("c_oT_written"), sem("c_oT_taken")
        x_written, x_taken = sem("c_x_written"), sem("c_x_taken")
        x_step = sem("c_x_step")
        vb_ready = sem("c_vb_ready")
        dve_turn = sem("c_dve_turn")
        NLOAD = 2 * KC + 2 + 2 * HQ + 4
        PV = TILES // 2
        PQ = 2 * (H // HQ)
        block = ctx.enter_context(nc.Block())

        @block.gpsimd
        def _(pool):
            for x in (wq, wk):
                nc.gpsimd.memset(x[:, :, :, :], 0.0).then_inc(zeroed, 1)
            nc.gpsimd.memset(bq[:, :], 0.0).then_inc(zeroed, 1)
            nc.gpsimd.memset(bk[:, :], 0.0).then_inc(zeroed, 1)
            pool.wait_ge(loaded, 16 * NLOAD)
            for h in range(H):
                ins = nc.gpsimd.tensor_scalar(table[:, h, :], dist[:, :], slopes[:, h:h + 1], None, ALU.mult)
            ins.then_inc(table_ready, 1)

        @block.sync
        def _(sp):
            def go(dst, src):
                sp.dma_start(dst, src).then_inc(loaded, 16)
            go(wv[:, :, :], w["L1_attn_WvT"].rearrange("(c p) n -> p c n", p=P))
            go(wo[:, :, :], w["L1_attn_WoT"].rearrange("(c p) n -> p c n", p=P))
            go(bvr[:, :], rows(w["L1_attn_bv"]))
            go(bor[:, :], rows(w["L1_attn_bo"]))
            go(slopes[:, :], rows(w["L1_attn_slopes"]))
            go(dist[:, :], consts["dist"])
            sp.wait_ge(zeroed, 4)
            for dst, nm in ((wq, "Wq"), (wk, "Wk")):
                for c in range(KC):
                    go(dst[:, c, :, 0:DA],
                       w[f"L1_attn_{nm}T"][c * P:(c + 1) * P, :].rearrange("p (h d) -> p h d", d=DA))
            for dst, nm in ((bq, "bq"), (bk, "bk")):
                for a in range(HQ):
                    src = w["L1_attn_" + nm].rearrange("(g a d) -> a d g", a=HQ, d=DA)
                    sp.dma_start(dst[a * SLOT:a * SLOT + DA, :], src[a],
                                 allow_slow_non_contiguous=True).then_inc(loaded, 16)
            sp.wait_ge(loaded, 16 * NLOAD)

        @block.tensor
        def _(pe):
            for x in (s_written, t_written, o_written):
                pe.sem_inc(x, 1)
            pe.wait_ge(loaded, 16 * NLOAD)
            for n in range(PV):
                pe.wait_ge(p_drained, n + 1)
                for i in range(2):
                    t = 2 * n + i
                    for c in range(KC):
                        last = nc.tensor.matmul(bank_p[n % 2][:, i * D:(i + 1) * D], XT[:, c, t * P:(t + 1) * P],
                                                wv[:, c, :], start=(c == 0), stop=(c == KC - 1))
                last.then_inc(p_written, 1)
            with pe.Fori(0, B) as b:
                for n in range(PQ):
                    g, which = divmod(n, 2)
                    pe.wait_ge(p_drained, PQ * b + (PV + n + 1))
                    m = (wq, wk)[which]
                    for c in range(KC):
                        last = nc.tensor.matmul(bank_p[n % 2][:, :],
                                                m[:, c, g * HQ:(g + 1) * HQ, :].rearrange("p h d -> p (h d)"),
                                                XT[:, c, bass.ds(b * T, T)], start=(c == 0), stop=(c == KC - 1))
                    last.then_inc(p_written, 1)

                def scores(u):
                    it, h = divmod(u, H)
                    g, a = divmod(h, HQ)
                    if u == 0:
                        pe.wait_ge(p_drained, PQ * b + (PV + PQ + 2))
                    pe.wait_ge(s_taken, UNITS * b + u + 1)
                    r = slice(a * SLOT, (a + 1) * SLOT)
                    nc.tensor.matmul(bank_s[u % 2][:, :], Q[r, g, it * P:(it + 1) * P], K[r, g, :],
                                     start=True, stop=True).then_inc(s_written, 1)

                def turn(u):
                    pe.wait_ge(exp_done, 1 + UNITS * b + u + 1)
                    pe.wait_ge(t_taken, UNITS * b + u + 1)
                    for j in range(TPB):
                        last = nc.tensor.transpose(bank_t[u % 2][:, j * P:(j + 1) * P],
                                                   pr[u % 2][:, j * P:(j + 1) * P], ident[:, :])
                    last.then_inc(t_written, 1)

                def value(u):
                    it, h = divmod(u, H)
                    pe.wait_ge(t_taken, UNITS * b + u + 1 + 2)
                    if u == 0:
                        pe.wait_ge(vb_ready, b + 1)
                    if h == 0:
                        pe.wait_ge(o_taken, TPB * b + it + 1)
                    for j in range(TPB):
                        last = nc.tensor.matmul(bank_o[:, h, :], pT[u % 2][:, j * P:(j + 1) * P],
                                                Vb[:, j, h * DA:(h + 1) * DA],
                                                start=(j == 0), stop=(j == TPB - 1))
                    if h == H - 1:
                        last.then_inc(o_written, 1)

                def project(it):
                    n = TPB * b + it
                    pe.wait_ge(o_taken, n + 1 + 1)
                    pe.wait_ge(x_taken, n + 1)
                    for c in range(KC):
                        last = nc.tensor.transpose(bank_x[:, c * P:(c + 1) * P],
                                                   o[:, :, :].rearrange("p h d -> p (h d)")[:, c * P:(c + 1) * P],
                                                   ident[:, :])
                    last.then_inc(oT_written, 1)
                    pe.wait_ge(oT_taken, n + 1)
                    for c in range(KC):
                        last = nc.tensor.matmul(bank_x[:, :], oT[:, c, :], wo[:, c, :],
                                                start=(c == 0), stop=(c == KC - 1))
                    last.then_inc(x_written, 1)

                for u in range(UNITS + 3):
                    if u < UNITS:
                        scores(u)
                    if 0 <= u - 1 < UNITS:
                        turn(u - 1)
                    if 0 <= u - 2 < UNITS:
                        value(u - 2)
                    if u >= 3 and (u - 3) % H == H - 1:
                        project((u - 3) // H)

        @block.scalar
        def _(act):
            nc.scalar.sem_inc(exp_done, 1)
            with act.Fori(0, B) as b:
                act.wait_ge(p_drained, PV + 2)
                act.wait_ge(o_written, 1 + TPB * b)
                nc.scalar.activation(Vb[:, :, :], V[:, bass.ds(b * TPB, TPB), :], ACT.Copy).then_inc(vb_ready, 1)
                for u in range(UNITS):
                    it, h = divmod(u, H)
                    act.wait_ge(s_taken, UNITS * b + u + 1 + 2)
                    if u >= 2:
                        act.wait_ge(t_written, 1 + UNITS * b + u - 1)
                    else:
                        act.wait_ge(t_written, 1 + UNITS * b)
                    act.wait_ge(rinv_ready, 1 + TPB * b + it - 1) if it else act.wait_ge(rinv_ready, 1 + TPB * b)
                    nc.scalar.activation(pr[u % 2][:, :], s[u % 2][:, :], ACT.Exp, scale=-1.0,
                                         bias=nmax[:, u % 2:u % 2 + 1],
                                         accum_out=rsum[:, it % 2, h:h + 1]).then_inc(exp_done, 1)

        @block.vector
        def _(dve):
            nc.vector.sem_inc(rinv_ready, 1)
            nc.vector.sem_inc(p_drained, 2)
            nc.vector.sem_inc(s_taken, 2)
            nc.vector.sem_inc(t_taken, 2)
            nc.vector.sem_inc(o_taken, 1)
            nc.vector.sem_inc(x_taken, 1)
            dve.wait_ge(loaded, 16 * NLOAD)
            for n in range(PV):
                dve.wait_ge(p_written, n + 1)
                nc.vector.tensor_tensor(V[:, 2 * n:2 * n + 2, :],
                                        bank_p[n % 2][:, :].rearrange("p (i n) -> p i n", n=D),
                                        bvr[:, :].unsqueeze(1).broadcast_to([P, 2, D]), ALU.add).then_inc(p_drained, 1)
            dve.wait_ge(table_ready, 1)
            with dve.Fori(0, B) as b:
                dve.wait_ge(s_written, 1 + UNITS * b)
                for n in range(PQ):
                    g, which = divmod(n, 2)
                    dve.wait_ge(p_written, PQ * b + (PV + n + 1))
                    nc.vector.tensor_scalar((Q, K)[which][:, g, :], bank_p[n % 2][:, :],
                                            (bq, bk)[which][:, g:g + 1], 1.0 if which else -float(DA) ** -0.5,
                                            ALU.add, ALU.mult).then_inc(p_drained, 1)

                def take_scores(u):
                    it, h = divmod(u, H)
                    dve.wait_ge(s_written, 1 + UNITS * b + u + 1)
                    if u >= 2:
                        dve.wait_ge(exp_done, 1 + UNITS * b + u - 1)
                    else:
                        dve.wait_ge(exp_done, 1 + UNITS * b)
                    off = T - P - it * P
                    nc.vector.sem_inc(dve_turn, 1)
                    nc.vector.tensor_tensor_reduce(out=s[u % 2][:, :], in0=bank_s[u % 2][:, :],
                                                   in1=table[:, h, off:off + T], scale=1.0, scalar=3.0e38,
                                                   op0=ALU.add, op1=ALU.min,
                                                   accum_out=nmax[:, u % 2:u % 2 + 1]).then_inc(s_taken, 1)

                def take_turn(u):
                    dve.wait_ge(t_written, 1 + UNITS * b + u + 1)
                    nc.vector.tensor_copy(pT[u % 2][:, :], bank_t[u % 2][:, :]).then_inc(t_taken, 1)

                def finish(it):
                    n = TPB * b + it
                    dve.wait_ge(exp_done, 1 + UNITS * b + H * (it + 1))
                    nc.vector.reciprocal(rinv[:, :], rsum[:, it % 2, :]).then_inc(rinv_ready, 1)
                    dve.wait_ge(rinv_ready, 1 + n + 1)
                    dve.wait_ge(o_written, 1 + n + 1)
                    nc.vector.tensor_tensor(o[:, :, :], bank_o[:, :, :],
                                            rinv[:, :].unsqueeze(2).broadcast_to([P, H, DA]),
                                            ALU.mult).then_inc(o_taken, 1)
                    dve.wait_ge(oT_written, n + 1)
                    nc.vector.tensor_copy(oT[:, :, :].rearrange("p c n -> p (c n)"), bank_x[:, :]).then_inc(oT_taken, 1)
                    x = X[:, bass.ds(b * TPB + it, 1), :].rearrange("p a d -> p (a d)")
                    dve.wait_ge(x_written, n + 1)
                    nc.vector.tensor_tensor(x, bank_x[:, :], x, ALU.add).then_inc(x_step, 1)
                    dve.wait_ge(x_step, n + 1)
                    nc.vector.tensor_tensor(x, x, bor[:, :], ALU.add).then_inc(x_taken, 1)

                for u in range(UNITS + 3):
                    if u < UNITS:
                        take_scores(u)
                    if 0 <= u - 1 < UNITS:
                        take_turn(u - 1)
                    if u >= 3 and (u - 3) % H == H - 1:
                        finish((u - 3) // H)


def latent_block(nc, X, XT, ident, w, consts):
    PROJ = 3 * B
    UNITS = TILES
    UP = PROJ + 2 * B
    with ExitStack() as ctx:
        sb, ps, sem = pools(nc, ctx)
        W = sb("l_W", [P, 3, KC, NOPE])
        wo = sb("l_wo", [P, D])
        Q = sb("l_Q", [P, N])
        K = sb("l_K", [P, N])
        V = sb("l_V", [P, TILES, VD])
        neg = sb("l_neg", [P, P])
        pr = [sb(f"l_p{j}", [P, T]) for j in range(2)]
        pT = [sb(f"l_pT{j}", [P, T]) for j in range(2)]
        nmax = sb("l_nmax", [P, 2])
        rsum = sb("l_rsum", [P, 2, TILES])
        rinv = sb("l_rinv", [P, 2, TILES])
        oT = [sb(f"l_oT{j}", [P, TPB, P]) for j in range(2)]
        bank_p = [ps(f"l_bank_p{j}", [P, T]) for j in range(2)]
        bank_s = [ps(f"l_bank_s{j}", [P, T]) for j in range(2)]
        bank_t = [ps(f"l_bank_t{j}", [P, T]) for j in range(2)]
        bank_o = [ps(f"l_bank_o{j}", [P, TPB, P]) for j in range(2)]
        loaded = sem("l_loaded")
        w_loaded = sem("l_w_loaded")
        sp_turn = sem("l_sp_turn")
        p_written, p_drained = sem("l_p_written"), sem("l_p_drained")
        proj_used = sem("l_proj_used")
        s_written, s_masked, s_max, exp_done = (sem("l_" + x) for x in ("s_written", "s_masked", "s_max", "exp_done"))
        t_written, t_taken = sem("l_t_written"), sem("l_t_taken")
        o_written, o_taken = sem("l_o_written"), sem("l_o_taken")
        rinv_ready = sem("l_rinv_ready")
        block = ctx.enter_context(nc.Block())

        @block.sync
        def _(sp):
            sp.dma_start(neg[:, :], consts["causal"]).then_inc(loaded, 16)
            sp.wait_ge(loaded, 16)
            with sp.Fori(0, H) as h:
                sp.wait_ge(p_written, 1 + UP * h)
                sp.sem_inc(sp_turn, 1)
                for k, (nm, first, step) in enumerate((("q_wT", 0, QHD), ("kv_wT", 0, NOPE), ("kv_wT", H * NOPE, VD))):
                    src = w["L1_ffn_" + nm].rearrange("(c p) n -> p c n", p=P)
                    sp.dma_start(W[:, k, :, :], src[:, :, bass.ds(h * step + first, NOPE)]).then_inc(w_loaded, 16)
                sp.dma_start(wo[:, :], w["L1_ffn_o_wT"][bass.ds(h * VD, VD), :]).then_inc(w_loaded, 16)

        @block.tensor
        def _(pe):
            for x in (s_written, t_written, o_written, p_written):
                pe.sem_inc(x, 1)
            with pe.Fori(0, H) as h:
                pe.wait_ge(w_loaded, 64 * (h + 1))
                for n in range(PROJ):
                    k, b = divmod(n, B)
                    pe.wait_ge(p_drained, UP * h + n + 1)
                    if k < 2:
                        for c in range(KC):
                            last = nc.tensor.matmul(bank_p[n % 2][:, :], W[:, k, c, :], XT[:, c, b * T:(b + 1) * T],
                                                    start=(c == 0), stop=(c == KC - 1))
                    else:
                        for i in range(TPB):
                            t = b * TPB + i
                            for c in range(KC):
                                last = nc.tensor.matmul(bank_p[n % 2][:, i * VD:(i + 1) * VD],
                                                        XT[:, c, t * P:(t + 1) * P], W[:, k, c, :],
                                                        start=(c == 0), stop=(c == KC - 1))
                    last.then_inc(p_written, 1)
                pe.wait_ge(p_drained, UP * h + PROJ + 2)

                def scores(u):
                    b, it = divmod(u, TPB)
                    pe.wait_ge(exp_done, UNITS * h + u + 1)
                    nc.tensor.matmul(bank_s[u % 2][:, 0:(it + 1) * P], Q[:, u * P:(u + 1) * P],
                                     K[:, b * T:b * T + (it + 1) * P], start=True, stop=True).then_inc(s_written, 1)

                def turn(u):
                    it = u % TPB
                    pe.wait_ge(exp_done, UNITS * h + u + 1 + 2)
                    pe.wait_ge(t_taken, UNITS * h + u + 1)
                    for j in range(it + 1):
                        last = nc.tensor.transpose(bank_t[u % 2][:, j * P:(j + 1) * P],
                                                   pr[u % 2][:, j * P:(j + 1) * P], ident[:, :])
                    last.then_inc(t_written, 1)

                def value(u):
                    b, it = divmod(u, TPB)
                    pe.wait_ge(t_taken, UNITS * h + u + 1 + 2)
                    if it == 0:
                        pe.wait_ge(o_taken, B * h + b + 1)
                    for j in range(it + 1):
                        last = nc.tensor.matmul(bank_o[b % 2][:, it, :], V[:, b * TPB + j, :],
                                                pT[u % 2][:, j * P:(j + 1) * P], start=(j == 0), stop=(j == it))
                    if it == TPB - 1:
                        last.then_inc(o_written, 1)

                def project(b):
                    pe.wait_ge(o_taken, B * h + b + 1 + 2)
                    for g in range(2):
                        n = PROJ + 2 * b + g
                        pe.wait_ge(p_drained, UP * h + n + 1)
                        for i in range(2):
                            last = nc.tensor.matmul(bank_p[n % 2][:, i * D:(i + 1) * D], oT[b % 2][:, 2 * g + i, :],
                                                    wo[:, :], start=True, stop=True)
                        last.then_inc(p_written, 1)

                for u in range(UNITS + 3):
                    if u < UNITS:
                        scores(u)
                    if 0 <= u - 1 < UNITS:
                        turn(u - 1)
                    if 0 <= u - 2 < UNITS:
                        value(u - 2)
                    if u >= 3 and (u - 3) % TPB == TPB - 1:
                        project((u - 3) // TPB)

        @block.scalar
        def _(act):
            nc.scalar.sem_inc(exp_done, 2)
            nc.scalar.sem_inc(o_taken, 2)
            with act.Fori(0, H) as h:
                act.wait_ge(s_written, 1 + UNITS * h)
                act.wait_ge(o_written, 1 + B * h)
                for n in range(PROJ):
                    k, b = divmod(n, B)
                    act.wait_ge(p_written, 1 + UP * h + n + 1)
                    if k < 2:
                        nc.scalar.activation((Q, K)[k][:, b * T:(b + 1) * T], bank_p[n % 2][:, :], ACT.Copy,
                                             scale=float(QHD) ** -0.5 if k == 0 else 1.0).then_inc(proj_used, 1)
                    else:
                        nc.scalar.activation(V[:, b * TPB:(b + 1) * TPB, :].rearrange("p t n -> p (t n)"),
                                             bank_p[n % 2][:, :], ACT.Copy).then_inc(proj_used, 1)

                def probabilities(u):
                    w_ = (u % TPB + 1) * P
                    act.wait_ge(s_max, UNITS * h + u + 1)
                    act.wait_ge(t_written, 1 + UNITS * h + max(u - 1, 0))
                    nc.scalar.activation(pr[u % 2][:, 0:w_], bank_s[u % 2][:, 0:w_], ACT.Exp,
                                         bias=nmax[:, u % 2:u % 2 + 1],
                                         accum_out=rsum[:, 0, u:u + 1]).then_inc(exp_done, 1)

                def take_out(b):
                    act.wait_ge(o_written, 1 + B * h + b + 1)
                    act.wait_ge(p_written, 1 + UP * h + (PROJ + 2 * (b - 1) if b >= 2 else 0))
                    nc.scalar.activation(oT[b % 2][:, :, :], bank_o[b % 2][:, :, :], ACT.Copy).then_inc(o_taken, 1)

                act.wait_ge(rinv_ready, 1 + B * h)
                for u in range(UNITS + 3):
                    if u < UNITS:
                        probabilities(u)
                    if u >= 3 and (u - 3) % TPB == TPB - 1:
                        take_out((u - 3) // TPB)

        @block.vector
        def _(dve):
            nc.vector.sem_inc(p_drained, 2)
            nc.vector.sem_inc(rinv_ready, 1)
            nc.vector.sem_inc(t_taken, 2)
            dve.wait_ge(loaded, 16)
            with dve.Fori(0, H) as h:
                dve.wait_ge(p_drained, UP * h + 2)
                for n in range(PROJ):
                    dve.wait_ge(proj_used, PROJ * h + n + 1)
                    nc.vector.sem_inc(p_drained, 1)

                def take_scores(u):
                    it = u % TPB
                    bank = bank_s[u % 2]
                    dve.wait_ge(s_written, 1 + UNITS * h + u + 1)
                    d = bank[:, it * P:(it + 1) * P]
                    nc.vector.tensor_tensor(d, d, neg[:, :], ALU.add).then_inc(s_masked, 1)
                    dve.wait_ge(s_masked, UNITS * h + u + 1)
                    nc.vector.reduce_max(nmax[:, u % 2:u % 2 + 1], bank[:, 0:(it + 1) * P], AX_X,
                                         negate=True).then_inc(s_max, 1)

                def take_turn(u):
                    w_ = (u % TPB + 1) * P
                    dve.wait_ge(t_written, 1 + UNITS * h + u + 1)
                    nc.vector.tensor_copy(pT[u % 2][:, 0:w_], bank_t[u % 2][:, 0:w_]).then_inc(t_taken, 1)

                def add_out(b):
                    dve.wait_ge(exp_done, UNITS * h + TPB * (b + 1) + 2)
                    nc.vector.reciprocal(rinv[:, 0, TPB * b:TPB * (b + 1)],
                                         rsum[:, 0, TPB * b:TPB * (b + 1)]).then_inc(rinv_ready, 1)
                    dve.wait_ge(rinv_ready, 1 + B * h + b + 1)
                    for g in range(2):
                        n = PROJ + 2 * b + g
                        dve.wait_ge(p_written, 1 + UP * h + n + 1)
                        for i in range(2):
                            t = b * TPB + 2 * g + i
                            last = nc.vector.scalar_tensor_tensor(X[:, t, :], bank_p[n % 2][:, i * D:(i + 1) * D],
                                                                  rinv[:, 0, t:t + 1], X[:, t, :], ALU.mult, ALU.add)
                        last.then_inc(p_drained, 1)

                for u in range(UNITS + 3):
                    if u < UNITS:
                        take_scores(u)
                    if 0 <= u - 1 < UNITS:
                        take_turn(u - 1)
                    if u >= 3 and (u - 3) % TPB == TPB - 1:
                        add_out((u - 3) // TPB)


def sum_block(nc, X, Y):
    with ExitStack() as ctx:
        block = ctx.enter_context(nc.Block())

        @block.vector
        def _(dve):
            nc.vector.tensor_tensor(X[:, :, :], X[:, :, :], Y[:, :, :], ALU.add)


def last_part(nc, X, HID, XT, ident, w, consts):
    norm_block(nc, "n4_", X, XT, ident, 1e-5, rows_out=HID)
    norm_block(nc, "n5_", HID, XT, ident, 1e-6, rms_weight=w["L1_ffn_ln1_w"])
    latent_block(nc, HID, XT, ident, w, consts)
    norm_block(nc, "n6_", HID, XT, ident, 1e-6, rms_weight=w["L1_ffn_ln2_w"])
    with ExitStack() as part:
        weights = part.enter_context(nc.sbuf_tensor("e1_weights", [P, E1 + NSH, TILES], F32))
        router_block(nc, "r1_", XT, w["L1_ffn_gate_wT"], E1, consts["rank1"], weights)
        experts_block(nc, "e1_", HID, [(0, E1 + NSH, XT)], weights,
                      (w["L1_ffn_gate"], w["L1_ffn_up"]), w["L1_ffn_down"], I1 // 2)
    sum_block(nc, X, HID)


def clear_block(nc, first):
    used = sorted(n for n in nc.released_uncleared_semaphores if n >= first)
    assert used == list(range(used[0], used[-1] + 1))
    with ExitStack() as ctx:
        block = ctx.enter_context(nc.Block())

        @block.gpsimd
        def _(pool):
            pool.sem_clear(range(used[0], used[-1] + 1))


def store_block(nc, X, out):
    with ExitStack() as ctx:
        sb, ps, sem = pools(nc, ctx)
        stored = sem("x_stored")
        block = ctx.enter_context(nc.Block())

        @block.sync
        def _(sp):
            sp.dma_start(out[:, 0:TILES // 2, :], X[:, 0:TILES // 2, :]).then_inc(stored, 16)
            sp.wait_ge(stored, 32)

        @block.scalar
        def _(act):
            act.dma_start(out[:, TILES // 2:, :], X[:, TILES // 2:, :]).then_inc(stored, 16)


def network(nc, w, consts, decay_dram, out):
    with ExitStack() as ctx:
        sb, ps, sem = pools(nc, ctx)
        X = sb("X", [P, TILES, D])
        XT = sb("XT", [P, KC, N])
        ident = sb("ident", [P, P])
        as_tiles = "b (c p) d -> p (b c) d"
        load_block(nc, X, w["L0_attn_hidden_states"].rearrange(as_tiles, p=P), ident, consts["ident"])
        norm_block(nc, "n0_", X, XT, ident, 1e-5)
        with ExitStack() as part:
            beta = part.enter_context(nc.sbuf_tensor("beta", [P, H, TILES], F32))
            decay_block(nc, XT, beta, decay_dram, w)
            delta_block(nc, X, XT, beta, ident, decay_dram, w, consts)
        if STAGES >= 2:
            norm_block(nc, "n1_", X, XT, ident, 1e-5)
            with ExitStack() as part:
                weights = part.enter_context(nc.sbuf_tensor("e0_weights", [P, E0 + 1, TILES], F32))
                score = part.enter_context(nc.sbuf_tensor("score", [P, TILES], F32))
                XS = part.enter_context(nc.sbuf_tensor("XS", [P, KC, N], F32))
                router_block(nc, "r0_", XT, w["L0_ffn_router_w"], E0, consts["rank0"], weights, score)
                norm_block(nc, "n2_", X, XS, ident, 1e-5, scale_by=score)
                experts_block(nc, "e0_", X, [(0, E0, XS), (E0, 1, XT)], weights,
                              (w["L0_ffn_gate"], w["L0_ffn_up"]), w["L0_ffn_down"], F0 // 2)
        clear_block(nc, 0)
        if STAGES >= 3:
            norm_block(nc, "n3_", X, XT, ident, 1e-5)
            alibi_block(nc, X, XT, ident, w, consts)
        if STAGES >= 4:
            with ExitStack() as part:
                HID = part.enter_context(nc.sbuf_tensor("HID", [P, TILES, D], F32))
                last_part(nc, X, HID, XT, ident, w, consts)
        store_block(nc, X, out.rearrange(as_tiles, p=P))


def constants():
    p = np.arange(P)
    level = np.zeros((P, LEVELS, 4, HALF), np.float32)
    for l in range(LEVELS):
        s = 1 << l
        u = np.arange(HALF)
        level[:, l, :, :] = (((p[:, None] // s) % 2 == 0) & (p[:, None] // (2 * s) == u[None, :] // s))[:, None, :]
    dist = np.abs(np.arange(2 * T - P)[None, :] - (T - P) - p[:, None]).astype(np.float32)

    def rank(E):
        return np.ascontiguousarray(np.broadcast_to((E - np.arange(E)).astype(np.float32), (P, TILES, E)))

    return {
        "ident": np.eye(P, dtype=np.float32),
        "level_mask": level.reshape(P, LEVELS, 4 * HALF),
        "dist": dist,
        "causal": np.where(p[None, :] <= p[:, None], 0.0, NEG).astype(np.float32),
        "rank0": rank(E0),
        "rank1": rank(E1),
    }


def layouts(x):
    out = {k: x[k] for k in (
        "L0_attn_hidden_states", "L0_attn_Wq", "L0_attn_Wk", "L0_attn_Wv", "L0_attn_conv_q", "L0_attn_conv_k",
        "L0_attn_conv_v", "L0_attn_Wf1", "L0_attn_Wf2", "L0_attn_Wb", "L0_attn_A_log", "L0_attn_dt_bias",
        "L0_attn_Wg", "L0_attn_bg", "L0_attn_norm_w", "L0_attn_Wo", "L0_ffn_router_w", "L1_attn_bq", "L1_attn_bk",
        "L1_attn_bv", "L1_attn_bo", "L1_attn_slopes", "L1_ffn_ln1_w", "L1_ffn_ln2_w")}
    for part in ("gate", "up", "down"):
        out[f"L0_ffn_{part}"] = np.concatenate([x[f"L0_ffn_{part}_w"], x[f"L0_ffn_shared_{part}_w"][None]])
    for m in ("Wq", "Wk", "Wv", "Wo"):
        out[f"L1_attn_{m}T"] = x[f"L1_attn_{m}"].T
    for m in ("q_w", "kv_w", "o_w", "gate_w"):
        out[f"L1_ffn_{m}T"] = x[f"L1_ffn_{m}"].T
    w1 = x["L1_ffn_w1"].reshape(E1, 2, I1, D)
    sh = x["L1_ffn_sh_gu_w"].reshape(2, NSH, I1, D)
    for n, part in enumerate(("gate", "up")):
        out[f"L1_ffn_{part}"] = np.concatenate([w1[:, n], sh[n]]).transpose(0, 2, 1)
    down = x["L1_ffn_sh_down_w"].reshape(D, NSH, I1).transpose(1, 2, 0)
    out["L1_ffn_down"] = np.concatenate([x["L1_ffn_w2"].transpose(0, 2, 1), down])
    return {k: np.ascontiguousarray(v) for k, v in out.items()}


def kernel(**inputs):
    import concourse.bacc as _bacc
    from concourse.bass_utils import run_bass_kernel_spmd as _run

    nc = _bacc.Bacc("TRN2", target_bir_lowering=False, num_devices=1)
    arrays = {}

    def dram(name, a):
        arrays[name] = a
        return nc.dram_tensor(name, a.shape, mybir.dt.from_np(a.dtype), kind="ExternalInput").ap()

    x = {k: np.asarray(v) for k, v in inputs.items()}
    w = {k: dram("in_" + k, v) for k, v in layouts(x).items()}
    consts = {k: dram("const_" + k, v) for k, v in constants().items()}
    decay_dram = nc.dram_tensor("decay", (LEVELS + 2, P, N), F32, kind="Internal").ap()
    out = nc.dram_tensor("out_0_dram", (B, T, D), F32, kind="ExternalOutput").ap()
    network(nc, w, consts, decay_dram, out)
    r = _run(nc, [arrays], core_ids=[0])
    return r.results[0]["out_0_dram"]
```

```python
from contextlib import ExitStack

import numpy as np

import concourse.bass as bass
from concourse import mybir

STAGES = 4

P = 128
F32 = mybir.dt.float32
I32 = mybir.dt.int32
ALU = mybir.AluOpType
ACT = mybir.ActivationFunctionType
AX_X = mybir.AxisListType.X

B, T, D = 4, 512, 256
N = B * T
TILES = N // P
TPB = T // P
KC = D // P
H = 16
BANK = 512
DH = 128
NG = 8
TAPS = 4
LEVELS = 7
HALF = P // 2
E0, F0 = 8, 256
E1, I1, TOPK, NSH = 16, 176, 4, 2
DA = D // H
SLOT = 32
NOPE, ROPE, VD = 128, 64, 128
QHD = NOPE + ROPE
NEG = -1.0e30


def pools(nc, ctx):
    def sb(name, shape, dt=F32):
        return ctx.enter_context(nc.sbuf_tensor(name, shape, dt))

    def ps(name, shape):
        return ctx.enter_context(nc.psum_tensor(name, shape, F32))

    def sem(name):
        return ctx.enter_context(nc.semaphore(name))

    return sb, ps, sem


def rows(ap, n=P):
    return ap.unsqueeze(0).broadcast_to([n, ap.shape[0]])


def load_block(nc, X, x_in, ident, ident_in):
    with ExitStack() as ctx:
        sb, ps, sem = pools(nc, ctx)
        loaded = sem("x_loaded")
        block = ctx.enter_context(nc.Block())

        @block.sync
        def _(sp):
            sp.dma_start(X[:, 0:TILES // 2, :], x_in[:, 0:TILES // 2, :]).then_inc(loaded, 16)
            sp.dma_start(ident[:, :], ident_in).then_inc(loaded, 16)
            sp.wait_ge(loaded, 48)

        @block.scalar
        def _(act):
            act.dma_start(X[:, TILES // 2:, :], x_in[:, TILES // 2:, :]).then_inc(loaded, 16)


def norm_block(nc, tag, X, XT, ident, eps, rms_weight=None, scale_by=None, rows_out=None):
    rms = rms_weight is not None
    with ExitStack() as ctx:
        sb, ps, sem = pools(nc, ctx)
        stats = sb(tag + "stats", [P, TILES, 6])
        mv = sb(tag + "mv", [P, TILES, 2])
        var = sb(tag + "var", [P, TILES])
        std = sb(tag + "std", [P, TILES])
        scale = sb(tag + "scale", [P, TILES])
        shift = sb(tag + "shift", [P, TILES])
        weight = sb(tag + "weight", [P, KC])
        xn = [sb(f"{tag}xn{j}", [P, D]) for j in range(2)]
        bank = [ps(f"{tag}bank{j}", [P, KC, P]) for j in range(2)]
        step = sem(tag + "step")
        var_ready = sem(tag + "var_ready")
        std_ready = sem(tag + "std_ready")
        scale_ready = sem(tag + "scale_ready")
        xn_ready = sem(tag + "xn_ready")
        turned = sem(tag + "turned")
        drained = sem(tag + "drained")
        w_loaded = sem(tag + "w_loaded")
        block = ctx.enter_context(nc.Block())

        @block.sync
        def _(sp):
            if rms:
                sp.dma_start(weight[:, :], rms_weight.rearrange("(c p) -> p c", p=P),
                             allow_slow_non_contiguous=True).then_inc(w_loaded, 16)
                sp.wait_ge(w_loaded, 16)

        @block.vector
        def _(dve):
            for t in range(TILES):
                nc.vector.bn_stats(stats[:, t, :], X[:, t, :]).then_inc(step, 1)
            for t in range(TILES):
                dve.wait_ge(step, t + 1)
                nc.vector.bn_aggr(mv[:, t, :], stats[:, t, :]).then_inc(step, 1)
            dve.wait_ge(step, 2 * TILES)
            if rms:
                nc.vector.tensor_tensor(shift[:, :], mv[:, :, 0], mv[:, :, 0], ALU.mult).then_inc(step, 1)
                dve.wait_ge(step, 2 * TILES + 1)
                nc.vector.scalar_tensor_tensor(var[:, :], mv[:, :, 1], eps, shift[:, :],
                                               ALU.add, ALU.add).then_inc(var_ready, 1)
            else:
                nc.vector.tensor_scalar(var[:, :], mv[:, :, 1], eps, None, ALU.add).then_inc(var_ready, 1)
            dve.wait_ge(std_ready, 1)
            nc.vector.reciprocal(scale[:, :], std[:, :]).then_inc(std_ready, 1)
            dve.wait_ge(std_ready, 2)
            if scale_by is not None:
                nc.vector.tensor_tensor(scale[:, :], scale[:, :], scale_by[:, :], ALU.mult).then_inc(std_ready, 1)
                dve.wait_ge(std_ready, 3)
            nc.vector.scalar_tensor_tensor(shift[:, :], mv[:, :, 0], 0.0 if rms else -1.0, scale[:, :],
                                           ALU.mult, ALU.mult).then_inc(scale_ready, 1)
            if rms:
                dve.wait_ge(w_loaded, 16)
            if rows_out is not None:
                return
            nc.vector.sem_inc(drained, 2)
            with dve.Fori(0, TILES // 2) as i:
                for j in range(2):
                    dve.wait_ge(turned, 2 * i + j + 1)
                    t = 2 * i + j
                    if rms:
                        for c in range(KC):
                            last = nc.vector.tensor_scalar(XT[:, c, bass.ds(t * P, P)], bank[j][:, c, :],
                                                           weight[:, c:c + 1], None, ALU.mult)
                    else:
                        last = nc.vector.tensor_copy(XT[:, :, bass.ds(t * P, P)], bank[j][:, :, :])
                    last.then_inc(drained, 1)

        @block.scalar
        def _(act):
            act.wait_ge(var_ready, 1)
            nc.scalar.activation(std[:, :], var[:, :], ACT.Sqrt).then_inc(std_ready, 1)
            act.wait_ge(scale_ready, 1)
            if rows_out is not None:
                for t in range(TILES):
                    nc.scalar.activation(rows_out[:, t, :], X[:, t, :], ACT.Identity, bias=shift[:, t:t + 1],
                                         scale=scale[:, t:t + 1])
                return
            with act.Fori(0, TILES // 2) as i:
                for j in range(2):
                    act.wait_ge(drained, 2 * i + j + 1)
                    nc.scalar.activation(xn[j][:, :], X[:, bass.ds(2 * i + j, 1), :].rearrange("p a d -> p (a d)"),
                                         ACT.Identity, bias=shift[:, bass.ds(2 * i + j, 1)],
                                         scale=scale[:, bass.ds(2 * i + j, 1)]).then_inc(xn_ready, 1)

        @block.tensor
        def _(pe):
            if rows_out is not None:
                return
            with pe.Fori(0, TILES // 2) as i:
                for j in range(2):
                    pe.wait_ge(drained, 2 * i + j + 1)
                    pe.wait_ge(xn_ready, 2 * i + j + 1)
                    for c in range(KC):
                        last = nc.tensor.transpose(bank[j][:, c, :], xn[j][:, c * P:(c + 1) * P], ident[:, :])
                    last.then_inc(turned, 1)


def decay_block(nc, XT, beta, decay_dram, w):
    with ExitStack() as ctx:
        sb, ps, sem = pools(nc, ctx)
        wf1 = sb("wf1", [P, KC, P])
        wf2 = sb("wf2", [P, P])
        wb = sb("wb", [P, KC, H])
        dtb = sb("dtb", [P, 1])
        alog = sb("alog", [P, 1])
        rate = sb("rate", [P, 1])
        nrate = sb("nrate", [P, 1])
        FT = sb("FT", [P, N])
        z = sb("z", [P, N])
        u = sb("u", [P, N])
        lg = sb("lg", [P, N])
        pol = sb("pol", [P, N])
        pref = sb("pref", [P, N])
        suf = sb("suf", [P, N])
        lev = [sb(f"lev{j}", [P, N]) for j in range(2)]
        acc = ps("dacc", [P, B, T])
        acc_b = ps("dacc_b", [P, TILES, H])
        loaded = sem("d_loaded")
        f_mm = sem("d_f_mm")
        f_sb = sem("d_f_sb")
        g_mm = sem("d_g_mm")
        b_mm = sem("d_b_mm")
        z_ready = sem("d_z")
        act_step = sem("d_act")
        dve_step = sem("d_dve")
        a_ready = sem("d_a")
        lev_ready = sem("d_lev")
        stored = [sem(f"d_stored{j}") for j in range(2)]
        rate_ready = sem("d_rate")
        ones_set = sem("d_ones_set")
        n_loads = 5
        block = ctx.enter_context(nc.Block())

        @block.gpsimd
        def _(pool):
            nc.gpsimd.memset(suf[:, :], 1.0).then_inc(ones_set, 1)

        @block.sync
        def _(sp):
            sp.dma_start(wf1[:, :, :], w["L0_attn_Wf1"].rearrange("(c p) n -> p c n", p=P)).then_inc(loaded, 16)
            sp.dma_start(wf2[:, :], w["L0_attn_Wf2"]).then_inc(loaded, 16)
            sp.dma_start(wb[:, :, :], w["L0_attn_Wb"].rearrange("(c p) n -> p c n", p=P)).then_inc(loaded, 16)
            sp.dma_start(dtb[:, :], w["L0_attn_dt_bias"].unsqueeze(1)).then_inc(loaded, 16)
            sp.dma_start(alog[:, :], w["L0_attn_A_log"].unsqueeze(1).broadcast_to([H, NG]).unsqueeze(2)
                         ).then_inc(loaded, 16)
            for k in range(LEVELS):
                sp.wait_ge(lev_ready, k + 1)
                sp.dma_start(decay_dram[k], lev[k % 2][:, :]).then_inc(stored[k % 2], 16)
            sp.wait_ge(lev_ready, LEVELS + 1)
            sp.dma_start(decay_dram[LEVELS], pref[:, :]).then_inc(stored[LEVELS % 2], 16)
            sp.dma_start(decay_dram[LEVELS + 1], suf[:, :]).then_inc(stored[(LEVELS + 1) % 2], 16)
            for j in range(2):
                sp.wait_ge(stored[j], 16 * len(range(j, LEVELS + 2, 2)))

        @block.tensor
        def _(pe):
            pe.wait_ge(loaded, 16 * n_loads)
            for b in range(B):
                for c in range(KC):
                    last = nc.tensor.matmul(acc[:, b, :], wf1[:, c, :], XT[:, c, b * T:(b + 1) * T],
                                            start=(c == 0), stop=(c == KC - 1))
                last.then_inc(f_mm, 1)
            for b in range(B):
                pe.wait_ge(f_sb, b + 1)
                nc.tensor.matmul(acc[:, b, :], wf2[:, :], FT[:, b * T:(b + 1) * T],
                                 start=True, stop=True).then_inc(g_mm, 1)
            for t in range(TILES):
                for c in range(KC):
                    last = nc.tensor.matmul(acc_b[:, t, :], XT[:, c, t * P:(t + 1) * P], wb[:, c, :],
                                            start=(c == 0), stop=(c == KC - 1))
            last.then_inc(b_mm, 1)

        @block.scalar
        def _(act):
            for b in range(B):
                act.wait_ge(f_mm, b + 1)
                nc.scalar.activation(FT[:, b * T:(b + 1) * T], acc[:, b, :], ACT.Copy).then_inc(f_sb, 1)
            act.wait_ge(loaded, 16 * n_loads)
            nc.scalar.activation(rate[:, :], alog[:, :], ACT.Exp).then_inc(rate_ready, 1)
            act.wait_ge(z_ready, 1)
            nc.scalar.activation(lg[:, :], z[:, :], ACT.Abs).then_inc(act_step, 1)
            act.wait_ge(act_step, 1)
            nc.scalar.activation(u[:, :], lg[:, :], ACT.Exp, scale=-1.0).then_inc(act_step, 1)
            act.wait_ge(act_step, 2)
            nc.scalar.activation(lg[:, :], u[:, :], ACT.Ln, bias=1.0).then_inc(act_step, 1)
            act.wait_ge(a_ready, 1)
            nc.scalar.activation(pref[:, :], z[:, :], ACT.Exp, scale=nrate[:, 0:1]).then_inc(act_step, 1)
            act.wait_ge(b_mm, 1)
            nc.scalar.activation(beta[:, :, :].rearrange("p h t -> p t h"), acc_b[:, :, :],
                                 ACT.Sigmoid).then_inc(act_step, 1)

        @block.vector
        def _(dve):
            n = [0]

            def then(ins):
                n[0] += 1
                ins.then_inc(dve_step, 1)
                dve.wait_ge(dve_step, n[0])

            dve.wait_ge(loaded, 16 * n_loads)
            for b in range(B):
                dve.wait_ge(g_mm, b + 1)
                last = nc.vector.tensor_scalar(z[:, b * T:(b + 1) * T], acc[:, b, :], dtb[:, 0:1], None, ALU.add)
            last.then_inc(z_ready, 1)
            dve.wait_ge(rate_ready, 1)
            then(nc.vector.tensor_scalar(nrate[:, :], rate[:, :], -1.0, None, ALU.mult))
            dve.wait_ge(act_step, 3)
            then(nc.vector.tensor_scalar(pol[:, :], u[:, :], 1.0 / 5, None, ALU.mult))
            for k in (4, 3, 2, 1):
                then(nc.vector.scalar_tensor_tensor(pol[:, :], pol[:, :], (1.0 if k % 2 else -1.0) / k, u[:, :],
                                                    ALU.add, ALU.mult))
            then(nc.vector.tensor_scalar(lev[0][:, :], u[:, :], 0.03, None, ALU.is_lt))
            then(nc.vector.copy_predicated(lg[:, :], lev[0][:, :].bitcast(I32), pol[:, :]))
            nc.vector.scalar_tensor_tensor(z[:, :], z[:, :], 0.0, lg[:, :], ALU.max, ALU.add).then_inc(a_ready, 1)
            dve.wait_ge(ones_set, 1)
            dve.wait_ge(act_step, 4)
            for k in range(LEVELS):
                s = 1 << k
                pv = pref[:, :].rearrange("p (n two s) -> p n two s", two=2, s=s)
                sv = suf[:, :].rearrange("p (n two s) -> p n two s", two=2, s=s)
                lv = lev[k % 2][:, :].rearrange("p (n two s) -> p n two s", two=2, s=s)
                nb = N // (2 * s)
                if k >= 2:
                    dve.wait_ge(stored[k % 2], 16 * (k // 2))
                nc.vector.tensor_copy(lv[:, :, 1, :], pv[:, :, 1, :])
                nc.vector.tensor_copy(lv[:, :, 0, :], sv[:, :, 0, :]).then_inc(lev_ready, 1)
                dve.wait_ge(lev_ready, k + 1)
                then(nc.vector.tensor_tensor(sv[:, :, 0, :], sv[:, :, 0, :],
                                             pv[:, :, 1, s - 1:s].broadcast_to([P, nb, s]), ALU.mult))
                then(nc.vector.tensor_tensor(pv[:, :, 1, :], pv[:, :, 1, :],
                                             pv[:, :, 0, s - 1:s].broadcast_to([P, nb, s]), ALU.mult))
            nc.vector.sem_inc(lev_ready, 1)


def delta_block(nc, X, XT, beta, ident, decay_dram, w, consts):
    PRE = 3 * B
    NL = LEVELS + 2
    PAIRS = B * LEVELS
    UQ = B + PAIRS + (TPB - 1)
    UY = PAIRS + (TPB - 1)
    UDD = PAIRS + TPB
    UDW = UDD - B
    UT = B + PAIRS + TPB
    UZ = B + TPB
    V_STEPS = (12, 16, 20, 24)

    def units(more):
        order = [("gate", b) for b in range(TPB)] + [("vt", b) for b in range(B)]
        if more:
            order += [("proj", b) for b in range(B)]
        order += [("kt", b) for b in range(B)]
        for c in range(TPB):
            if c >= 2:
                order += [("out", 2 * (c - 2) + 1)]
            if more:
                order += [("proj", B + 2 * c), ("proj", B + 2 * c + 1)]
            if c:
                order += [("out", 2 * (c - 1))]
        order += [("out", 2 * TPB - 3), ("out", 2 * TPB - 2), ("out", 2 * TPB - 1)]
        return {x: n for n, x in enumerate(order)}

    UP = len(units(True))
    assert UP % 2 == 0 and PRE % 2 == 0
    with ExitStack() as ctx:
        sb, ps, sem = pools(nc, ctx)
        W = sb("W", [P, 4, KC, DH])
        cw = sb("cw", [P, 3, TAPS])
        nw = sb("nw", [P, 1])
        bg = sb("bg", [P, DH])
        wo = sb("wo", [P, D])
        qkv = [sb(nm, [P, N]) for nm in ("VT", "QT", "KT")]
        VT, QT, KT = qkv
        gate = sb("gate", [P, TILES, DH])
        bv = sb("bv", [P, TILES, DH])
        ktm = sb("ktm", [P, TILES, DH])
        dec = sb("dec", [P, 2, N])
        KQ = [sb(f"KQ{j}", [P, 2, N]) for j in range(2)]
        Bl = sb("Bl", [P, LEVELS, 2, 4, P])
        Tm = sb("Tm", [P, TILES, P])
        R = sb("R", [P, TILES, P])
        Aqk = sb("Aqk", [P, TILES, P])
        Ysb = sb("Ysb", [P, 2, 4, HALF])
        S = sb("S", [P, B, DH])
        U = sb("U", [P, B, DH])
        R1 = sb("R1", [P, B, DH])
        y1 = sb("y1", [P, B, DH])
        yT = sb("yT", [P, B, DH])
        ysq_junk = sb("ysq_junk", [P, DH])
        pend = sb("pend", [P, TILES])
        mhalf = sb("mhalf", [P, 2 * TILES])
        sq = sb("sq", [P, 2 * TILES])
        ss = sb("ss", [P, 2 * TILES])
        rr = sb("rr", [P, 2 * TILES])
        brk = sb("brk", [P, TILES])
        cc = sb("cc", [P, TILES])
        rq = sb("rq", [P, TILES])
        rq2 = sb("rq2", [P, TILES])
        ysum = sb("ysum", [P, B])
        yms = sb("yms", [P, B])
        yrs = sb("yrs", [P, B])
        yscale = sb("yscale", [P, TPB, B])
        mask = sb("mask", [P, LEVELS, 4 * HALF])
        bankP = [ps(f"bankP{j}", [P, BANK]) for j in range(2)]
        bankQ = [ps(f"bankQ{j}", [P, BANK]) for j in range(2)]
        bankY = ps("bankY", [P, BANK])
        bankD = ps("bankD", [P, BANK])
        bankT = ps("bankT", [P, BANK])
        bankZ = ps("bankZ", [P, BANK])
        P_written, P_drained = sem("P_written"), sem("P_drained")
        Q_written, Q_drained = sem("Q_written"), sem("Q_drained")
        Y_written, Y_drained = sem("Y_written"), sem("Y_drained")
        D_written, D_drained = sem("D_written"), sem("D_drained")
        T_written, T_drained = sem("T_written"), sem("T_drained")
        Z_written, Z_drained = sem("Z_written"), sem("Z_drained")
        const_loaded = sem("const_loaded")
        const_set = sem("const_set")
        w_loaded = sem("a_w_loaded")
        g_loaded = sem("g_loaded")
        wo_loaded = sem("wo_loaded")
        dec_loaded = [sem(f"dec_loaded{j}") for j in range(2)]
        tap_done = sem("tap_done")
        conv_step = sem("conv_step")
        silu_done = sem("silu_done")
        gate_done = sem("gate_done")
        eye_set = sem("eye_set")
        scaled = sem("scaled")
        ss_ready = sem("ss_ready")
        rr_ready = sem("rr_ready")
        rk_ready = sem("rk_ready")
        R1_ready = sem("R1_ready")
        S_ready = sem("S_ready")
        ysq_ready = sem("ysq_ready")
        yms_ready = sem("yms_ready")
        yms_step = sem("yms_step")
        yrs_ready = sem("yrs_ready")
        ysc_ready = sem("ysc_ready")
        sp_turn = sem("sp_turn")
        block = ctx.enter_context(nc.Block())

        def up(ap, s):
            return ap.rearrange("p (n two s) -> p n two s", two=2, s=s)[:, :, 1, :]

        def low(ap, s):
            return ap.rearrange("p (n two s) -> p n two s", two=2, s=s)[:, :, 0, :]

        def flat(ap):
            return ap.rearrange("p a b -> p (a b)")

        def blocks(ap, s):
            return ap.rearrange("p (n s) -> p n s", s=s)

        def chunk_of(ap, c):
            return ap.rearrange("p (b c) n -> p c b n", c=TPB)[:, c, :, :]

        def stat_of(ap, c):
            return ap.rearrange("p (b c) -> p c b", c=TPB)[:, c, :]

        def heads(eng, body):
            with eng.Fori(0, H - 1) as h:
                body(h, True)
            body(H - 1, False)

        def norm_unit(which, b, h):
            n = (B * which + b) // 2
            if b % 2 == 0:
                return bankT, T_written, T_drained, UT * h + n
            return bankZ, Z_written, Z_drained, UZ * h + n

        def cut(h):
            return bass.ds(h * DH, DH) if not isinstance(h, int) else slice(h * DH, (h + 1) * DH)

        @block.sync
        def _(sp):
            sp.dma_start(mask[:, :, :], consts["level_mask"]).then_inc(const_loaded, 16)
            sp.dma_start(nw[:, :], w["L0_attn_norm_w"].unsqueeze(1)).then_inc(const_loaded, 16)

            def load_qkv(h):
                for k, (nm, cv) in enumerate((("Wv", "conv_v"), ("Wq", "conv_q"), ("Wk", "conv_k"))):
                    src = w["L0_attn_" + nm].rearrange("(c p) n -> p c n", p=P)
                    sp.dma_start(W[:, k, :, :], src[:, :, cut(h)]).then_inc(w_loaded, 16)
                    sp.dma_start(cw[:, k, :], w["L0_attn_" + cv][cut(h), :]).then_inc(w_loaded, 16)

            def load_gate(h):
                src = w["L0_attn_Wg"].rearrange("(c p) n -> p c n", p=P)
                sp.dma_start(W[:, 3, :, :], src[:, :, cut(h)]).then_inc(g_loaded, 16)
                sp.dma_start(bg[:, :], w["L0_attn_bg"].rearrange("(a n) -> a n", a=1)[:, cut(h)]
                             .broadcast_to([P, DH])).then_inc(g_loaded, 16)

            load_qkv(0)
            load_gate(0)
            sp.wait_ge(const_loaded, 32)

            def body(h, more):
                place = units(more)
                base = UP * h + PRE

                def load_decay(k):
                    sp.wait_ge(scaled, NL * h + max(k - 1, 0) + 1)
                    sp.sem_inc(sp_turn, 1)
                    rows_ = bass.ds(h * NG, NG) if more else slice(h * NG, (h + 1) * NG)
                    src = decay_dram[k][rows_, :].unsqueeze(1).broadcast_to([NG, P // NG, N])
                    sp.dma_start(dec[:, k % 2, :], src).then_inc(dec_loaded[k % 2], 16)

                load_decay(0)
                load_decay(1)
                sp.wait_ge(P_drained, base + 2)
                sp.sem_inc(sp_turn, 1)
                sp.dma_start(wo[:, :], w["L0_attn_Wo"][cut(h), :]).then_inc(wo_loaded, 16)
                if more:
                    load_qkv(h + 1)
                    sp.wait_ge(P_drained, base + place["gate", TPB - 1] + 1 + 2)
                    sp.sem_inc(sp_turn, 1)
                    load_gate(h + 1)
                for k in range(2, NL):
                    load_decay(k)
            heads(sp, body)

        @block.gpsimd
        def _(pool):
            nc.gpsimd.sem_inc(scaled, 1)
            nc.gpsimd.memset(mhalf[:, :], -0.5).then_inc(const_set, 1)
            nc.gpsimd.memset(Bl[:, :, :, :, :], 0.0).then_inc(const_set, 1)
            pool.wait_ge(const_set, 2)

            def body(h, more):
                place = units(more)
                base = UP * h + PRE

                def scale(k):
                    s = 1 << k
                    d = dec[:, k % 2, :]
                    per_head = len(range(k % 2, NL, 2))
                    pool.wait_ge(dec_loaded[k % 2], 16 * (per_head * h + k // 2 + 1))
                    if k < LEVELS:
                        if k >= 2:
                            pool.wait_ge(Q_written, UQ * h + B + B * (k - 1) + 1)
                        else:
                            pool.wait_ge(D_written, UDW * h + 1)
                        nc.gpsimd.tensor_tensor(KQ[k % 2][:, 0, :], KT[:, :], d, ALU.mult)
                        nc.gpsimd.tensor_tensor(up(KQ[k % 2][:, 1, :], s), up(QT[:, :], s), up(d, s),
                                                ALU.mult).then_inc(scaled, 1)
                    elif k == LEVELS:
                        pool.wait_ge(Q_written, UQ * h + B + B * (k - 1) + 1)
                        nc.gpsimd.tensor_tensor(KQ[1][:, 0, :], KT[:, :], d, ALU.mult)
                        nc.gpsimd.tensor_tensor(KQ[1][:, 1, :], QT[:, :], d, ALU.mult)
                        nc.gpsimd.tensor_copy(pend[:, :], d.rearrange("p (t n) -> p t n", n=P)[:, :, P - 1]
                                              ).then_inc(scaled, 1)
                    else:
                        pool.wait_ge(Q_written, UQ * h + B + PAIRS + 1)
                        nc.gpsimd.tensor_tensor(KQ[0][:, 0, :], KT[:, :], d, ALU.mult).then_inc(scaled, 1)

                pool.wait_ge(silu_done, 3 * B * (h + 1))
                scale(0)
                for which in range(2):
                    pool.wait_ge(ss_ready, 2 * h + which + 1)
                    v = slice(which * TILES, (which + 1) * TILES)
                    nc.gpsimd.tensor_tensor(rr[:, v], ss[:, v], mhalf[:, v], ALU.pow).then_inc(rr_ready, 1)
                    scale(1 + which)
                for k in range(3, NL):
                    scale(k)
                for c in range(TPB):
                    pool.wait_ge(yms_ready, TPB * h + c + 1)
                    nc.gpsimd.tensor_tensor(yrs[:, :], yms[:, :], mhalf[:, 0:B], ALU.pow).then_inc(yrs_ready, 1)
            heads(pool, body)

        @block.scalar
        def _(act):
            nc.scalar.sem_inc(T_drained, 1)
            nc.scalar.sem_inc(Z_drained, 1)
            act.wait_ge(const_loaded, 32)

            def tap(unit, n, g):
                k, b = divmod(n, B)
                act.wait_ge(P_written, unit + 1 + 1)
                nc.scalar.activation(qkv[k][:, b * T:(b + 1) * T], bankP[n % 2][:, :], ACT.Copy,
                                     scale=cw[:, k, TAPS - 1:TAPS]).then_inc(tap_done, 1)

            def silu(n, g):
                k, b = divmod(n, B)
                act.wait_ge(conv_step, 3 * (3 * B * g + n + 1))
                v = qkv[k][:, b * T:(b + 1) * T]
                nc.scalar.activation(v, v, ACT.Silu).then_inc(silu_done, 1)

            act.wait_ge(w_loaded, 96)
            for n in range(PRE):
                tap(n, n, 0)
                if n:
                    silu(n - 1, 0)
            silu(PRE - 1, 0)

            def body(h, more):
                place = units(more)
                base = UP * h + PRE
                act.wait_ge(P_drained, base + 2)
                for which in range(2):
                    for b in range(B):
                        bank, written, drained, n = norm_unit(which, b, h)
                        act.wait_ge(written, n + 1 + 1)
                        for i in range(4):
                            v = bank[:, i * P:(i + 1) * P]
                            t = which * TILES + 4 * b + i
                            last = nc.scalar.activation(v, v, ACT.Square, accum_out=sq[:, t:t + 1])
                        last.then_inc(drained, 1)
                    if which == 0:
                        nc.scalar.activation(Tm[:, :, :], ident[:, :].unsqueeze(1).broadcast_to([P, TILES, P]),
                                             ACT.Copy).then_inc(eye_set, 1)
                for b in range(TPB):
                    act.wait_ge(P_drained, base + place["gate", b] + 1 + 2)
                    v = gate[:, 4 * b:4 * b + 4, :]
                    nc.scalar.activation(v, v, ACT.Silu).then_inc(gate_done, 1)

                def take_turn(n):
                    b = n % B
                    act.wait_ge(T_written, UT * h + B + n + 1 + 1)
                    nc.scalar.activation(flat(R[:, 4 * b:4 * b + 4, :]), bankT[:, :], ACT.Copy).then_inc(T_drained, 1)

                for n in range(PAIRS + 3):
                    if more and n in V_STEPS:
                        i = V_STEPS.index(n)
                        if i == 0:
                            act.wait_ge(w_loaded, 96 * (h + 2))
                        tap(base + place["proj", i], i, h + 1)
                    if more and n - 2 in V_STEPS:
                        silu(V_STEPS.index(n - 2), h + 1)
                    if n >= 3:
                        take_turn(n - 3)
                act.wait_ge(scaled, NL * (h + 1) + 1)

                def take_y(c):
                    act.wait_ge(Z_written, UZ * h + B + c + 1 + 1)
                    if c:
                        act.wait_ge(P_written, base + place["out", 2 * c - 1] + 1 + 1)
                    nc.scalar.activation(flat(yT[:, :, :]), bankZ[:, :], ACT.Copy,
                                         scale=nw[:, 0:1]).then_inc(Z_drained, 1)

                for c in range(TPB):
                    if more:
                        tap(base + place["proj", B + 2 * c], B + 2 * c, h + 1)
                    act.wait_ge(T_written, UT * h + B + PAIRS + c + 1 + 1)
                    nc.scalar.activation(flat(U[:, :, :]), bankT[:, :], ACT.Copy).then_inc(T_drained, 1)
                    if c:
                        take_y(c - 1)
                    if more:
                        tap(base + place["proj", B + 2 * c + 1], B + 2 * c + 1, h + 1)
                        silu(B + 2 * c, h + 1)
                    act.wait_ge(D_drained, UDD * h + PAIRS + c + 1 + 1)
                    act.wait_ge(yms_step, TPB * h + c + 1)
                    for b in range(B):
                        if b:
                            act.wait_ge(ysq_ready, B * (TPB * h + c) + b)
                        nc.scalar.activation(ysq_junk[:, :], y1[:, b, :], ACT.Square,
                                             accum_out=ysum[:, b:b + 1]).then_inc(ysq_ready, 1)
                    if more:
                        silu(B + 2 * c + 1, h + 1)
                take_y(TPB - 1)
            heads(act, body)

        @block.tensor
        def _(pe):
            for x in (P_written, Y_written, T_written, D_written, Q_written, Z_written):
                pe.sem_inc(x, 1)

            def mm(out, lhsT, rhs, first=True, last=True):
                return nc.tensor.matmul(out, lhsT, rhs, start=first, stop=last)

            def project(unit, n):
                k, b = divmod(n, B)
                pe.wait_ge(P_drained, unit + 1)
                for c in range(KC):
                    last = mm(bankP[n % 2][:, :], W[:, k, c, :], XT[:, c, b * T:(b + 1) * T], c == 0, c == KC - 1)
                last.then_inc(P_written, 1)

            pe.wait_ge(w_loaded, 96)
            for n in range(PRE):
                project(n, n)
            pe.wait_ge(const_set, 2)

            def body(h, more):
                place = units(more)
                base = UP * h + PRE
                pe.wait_ge(g_loaded, 32 * (h + 1))
                for b in range(B):
                    n = place["gate", b]
                    pe.wait_ge(P_drained, base + n + 1)
                    for i in range(4):
                        t = 4 * b + i
                        for c in range(KC):
                            last = mm(bankP[n % 2][:, i * DH:(i + 1) * DH], XT[:, c, t * P:(t + 1) * P],
                                      W[:, 3, c, :], c == 0, c == KC - 1)
                    last.then_inc(P_written, 1)
                    if b == 0:
                        pe.wait_ge(silu_done, 3 * B * (h + 1))
                    for m in (2 * b, 2 * b + 1):
                        which, s = divmod(m, B)
                        bank, written, drained, n = norm_unit(which, s, h)
                        pe.wait_ge(drained, n + 1)
                        for i in range(4):
                            t = 4 * s + i
                            last = nc.tensor.transpose(bank[:, i * P:(i + 1) * P],
                                                       (KT, QT)[which][:, t * P:(t + 1) * P], ident[:, :])
                        last.then_inc(written, 1)
                for b in range(B):
                    pe.wait_ge(Q_drained, UQ * h + max(b + 1, 2))
                    for i in range(4):
                        t = 4 * b + i
                        last = mm(bankQ[b % 2][:, i * P:(i + 1) * P], KT[:, t * P:(t + 1) * P], QT[:, t * P:(t + 1) * P])
                    last.then_inc(Q_written, 1)
                for b in range(B):
                    n = place["vt", b]
                    pe.wait_ge(P_drained, base + n + 1)
                    for i in range(4):
                        t = 4 * b + i
                        last = nc.tensor.transpose(bankP[n % 2][:, i * P:(i + 1) * P], VT[:, t * P:(t + 1) * P],
                                                   ident[:, :])
                    last.then_inc(P_written, 1)
                pe.wait_ge(eye_set, h + 1)

                def pairs(n):
                    l, b = divmod(n, B)
                    q, s = B + n, 1 << l
                    pe.wait_ge(scaled, NL * h + l + 1 + 1)
                    pe.wait_ge(Q_drained, UQ * h + q + 1)
                    for i in range(4):
                        t = 4 * b + i
                        kq = KQ[l % 2][:, :, t * P:(t + 1) * P]
                        last = mm(bankQ[q % 2][:, :].rearrange("p (two i n s) -> p i two n s", two=2, i=4, s=s)[:, i],
                                  kq[:, 0, :], kq.rearrange("p w (n two s) -> p w n two s", two=2, s=s)[:, :, :, 1, :])
                    last.then_inc(Q_written, 1)

                def merge_a(n):
                    l, b = divmod(n, B)
                    s = 1 << l
                    pe.wait_ge(Q_drained, UQ * h + B + n + 1 + 2)
                    pe.wait_ge(Y_drained, UY * h + n + 1)
                    if l:
                        pe.wait_ge(D_drained, UDD * h + n - B + 1 + 1)
                    for i in range(4):
                        t = 4 * b + i
                        if l:
                            last = mm(blocks(bankY[:, i * HALF:(i + 1) * HALF], s), Bl[:, l, b % 2, i, :],
                                      low(Tm[:, t, :], s))
                        else:
                            last = nc.tensor.transpose(bankY[:, i * P:(i + 1) * P], Bl[:, l, b % 2, i, :],
                                                       ident[:, :])
                    last.then_inc(Y_written, 1)

                def merge_b(n):
                    l, b = divmod(n, B)
                    if l == 0:
                        return
                    pe.wait_ge(Y_drained, UY * h + n + 1 + 1)
                    pe.wait_ge(D_drained, UDD * h + n + 1)
                    pe.wait_ge(T_drained, UT * h + B + n - B + 1 + 1)
                    for i in range(4):
                        last = mm(bankD[:, i * HALF:(i + 1) * HALF], R[:, 4 * b + i, :], Ysb[:, b % 2, i, :])
                    last.then_inc(D_written, 1)

                def turn(n):
                    b = n % B
                    pe.wait_ge(D_drained, UDD * h + n + 1 + 1)
                    pe.wait_ge(T_drained, UT * h + B + n + 1)
                    for i in range(4):
                        last = nc.tensor.transpose(bankT[:, i * P:(i + 1) * P], Tm[:, 4 * b + i, :], ident[:, :])
                    last.then_inc(T_written, 1)

                for n in range(PAIRS + 3):
                    if more and n in V_STEPS:
                        i = V_STEPS.index(n)
                        if i == 0:
                            pe.wait_ge(w_loaded, 96 * (h + 2))
                        project(base + place["proj", i], i)
                    for lag, part in enumerate((pairs, merge_a, merge_b, turn)):
                        if 0 <= n - lag < PAIRS:
                            part(n - lag)
                pe.wait_ge(scaled, NL * (h + 1) + 1)
                for b in range(B):
                    n = place["kt", b]
                    pe.wait_ge(P_drained, base + n + 1)
                    for i in range(4):
                        t = 4 * b + i
                        last = nc.tensor.transpose(bankP[n % 2][:, i * P:(i + 1) * P], KQ[0][:, 0, t * P:(t + 1) * P],
                                                   ident[:, :])
                    last.then_inc(P_written, 1)

                def y_turn(c):
                    pe.wait_ge(Z_drained, UZ * h + B + c + 1)
                    pe.wait_ge(D_drained, UDD * h + PAIRS + c + 1 + 1)
                    for b in range(B):
                        last = nc.tensor.transpose(bankZ[:, b * P:(b + 1) * P], y1[:, b, :], ident[:, :])
                    last.then_inc(Z_written, 1)

                def y_out(c, g):
                    if g == 0:
                        pe.wait_ge(Z_drained, UZ * h + B + c + 1 + 1)
                    n = place["out", 2 * c + g]
                    pe.wait_ge(P_drained, base + n + 1)
                    for i in range(2):
                        last = mm(bankP[n % 2][:, i * D:(i + 1) * D], yT[:, 2 * g + i, :], wo[:, :])
                    last.then_inc(P_written, 1)

                pe.wait_ge(wo_loaded, 16 * (h + 1))
                for c in range(TPB):
                    tok = [slice((b * TPB + c) * P, (b * TPB + c + 1) * P) for b in range(B)]
                    if c:
                        pe.wait_ge(S_ready, (TPB - 1) * h + c)
                        pe.wait_ge(Y_drained, UY * h + PAIRS + c - 1 + 1)
                        for b in range(B):
                            last = mm(bankY[:, b * P:(b + 1) * P], KQ[1][:, 0, tok[b]], S[:, b, :])
                        last.then_inc(Y_written, 1)
                    if c >= 2:
                        y_out(c - 2, 1)
                    if more:
                        project(base + place["proj", B + 2 * c], B + 2 * c)
                    if c:
                        pe.wait_ge(R1_ready, (TPB - 1) * h + c)
                    else:
                        pe.wait_ge(P_drained, base + place["vt", B - 1] + 1 + 2)
                    pe.wait_ge(T_drained, UT * h + B + PAIRS + c + 1)
                    for b in range(B):
                        t = b * TPB + c
                        last = mm(bankT[:, b * P:(b + 1) * P], R[:, t, :], R1[:, b, :] if c else bv[:, t, :])
                    last.then_inc(T_written, 1)
                    if c:
                        y_turn(c - 1)
                    if more:
                        project(base + place["proj", B + 2 * c + 1], B + 2 * c + 1)
                    pe.wait_ge(T_drained, UT * h + B + PAIRS + c + 1 + 1)
                    pe.wait_ge(D_drained, UDD * h + PAIRS + c + 1)
                    for b in range(B):
                        t = b * TPB + c
                        if c:
                            mm(bankD[:, b * P:(b + 1) * P], KQ[1][:, 1, tok[b]], S[:, b, :], True, False)
                        last = mm(bankD[:, b * P:(b + 1) * P], Aqk[:, t, :], U[:, b, :], not c, True)
                    last.then_inc(D_written, 1)
                    if c < TPB - 1:
                        q = B + PAIRS + c
                        pe.wait_ge(Q_drained, UQ * h + q + 1)
                        pe.wait_ge(P_drained, base + place["kt", B - 1] + 1 + 2)
                        for b in range(B):
                            last = mm(bankQ[q % 2][:, b * P:(b + 1) * P], ktm[:, b * TPB + c, :], U[:, b, :])
                        last.then_inc(Q_written, 1)
                    if c:
                        y_out(c - 1, 0)
                y_out(TPB - 2, 1)
                y_turn(TPB - 1)
                y_out(TPB - 1, 0)
                y_out(TPB - 1, 1)
            heads(pe, body)

        @block.vector
        def _(dve):
            nc.vector.sem_inc(P_drained, 2)
            nc.vector.sem_inc(Q_drained, 2)
            nc.vector.sem_inc(Y_drained, 1)
            nc.vector.sem_inc(D_drained, 1)
            nc.vector.sem_inc(yms_step, 1)
            dve.wait_ge(const_loaded, 32)
            dve.wait_ge(const_set, 2)

            def conv(n, g):
                k, b = divmod(n, B)
                m = 3 * (3 * B * g + n)
                dve.wait_ge(tap_done, 3 * B * g + n + 1)
                for j in range(1, TAPS):
                    if j > 1:
                        dve.wait_ge(conv_step, m + j - 1)
                    v = qkv[k][:, b * T + j:(b + 1) * T]
                    nc.vector.scalar_tensor_tensor(v, bankP[n % 2][:, 0:T - j], cw[:, k, TAPS - 1 - j:TAPS - j], v,
                                                   ALU.mult, ALU.add).then_inc(conv_step, 1)
                dve.wait_ge(conv_step, m + 3)
                nc.vector.sem_inc(P_drained, 1)

            dve.wait_ge(w_loaded, 96)
            for n in range(PRE):
                conv(n, 0)

            def body(h, more):
                place = units(more)
                base = UP * h + PRE
                dve.wait_ge(g_loaded, 32 * (h + 1))
                def squares(which):
                    dve.wait_ge(T_drained, UT * h + B // 2 * (which + 1) + 1)
                    dve.wait_ge(Z_drained, UZ * h + B // 2 * (which + 1) + 1)
                    v = slice(which * TILES, (which + 1) * TILES)
                    nc.vector.tensor_scalar(ss[:, v], sq[:, v], 1e-6, None, ALU.add).then_inc(ss_ready, 1)

                for b in range(TPB):
                    if b == TPB - 1:
                        squares(0)
                    n = place["gate", b]
                    dve.wait_ge(P_written, base + n + 1 + 1)
                    nc.vector.tensor_tensor(gate[:, 4 * b:4 * b + 4, :],
                                            bankP[n % 2][:, :].rearrange("p (i n) -> p i n", n=DH),
                                            bg[:, :].unsqueeze(1).broadcast_to([P, 4, DH]),
                                            ALU.add).then_inc(P_drained, 1)
                squares(1)
                for b in range(B):
                    dve.wait_ge(Q_written, UQ * h + b + 1 + 1)
                    nc.vector.tensor_tensor(Aqk[:, 4 * b:4 * b + 4, :],
                                            bankQ[b % 2][:, :].rearrange("p (i n) -> p i n", n=P),
                                            ident[:, :].unsqueeze(1).broadcast_to([P, 4, P]),
                                            ALU.mult).then_inc(Q_drained, 1)
                dve.wait_ge(rr_ready, 2 * h + 1)
                rk = rr[:, 0:TILES]
                bt = beta[:, bass.ds(h, 1), :].rearrange("p a t -> p (a t)") if more else beta[:, h, :]
                nc.vector.tensor_tensor(brk[:, :], rk, bt, ALU.mult).then_inc(rk_ready, 1)
                dve.wait_ge(rk_ready, 4 * h + 1)
                nc.vector.tensor_tensor(cc[:, :], brk[:, :], rk, ALU.mult).then_inc(rk_ready, 1)
                dve.wait_ge(rk_ready, 4 * h + 2)
                for b in range(B):
                    n = place["vt", b]
                    dve.wait_ge(P_written, base + n + 1 + 1)
                    nc.vector.tensor_tensor(bv[:, 4 * b:4 * b + 4, :],
                                            bankP[n % 2][:, :].rearrange("p (i n) -> p i n", n=DH),
                                            brk[:, 4 * b:4 * b + 4].unsqueeze(2).broadcast_to([P, 4, DH]),
                                            ALU.mult).then_inc(P_drained, 1)
                dve.wait_ge(eye_set, h + 1)

                def take_pairs(n):
                    l, b = divmod(n, B)
                    q, s = B + n, 1 << l
                    dve.wait_ge(Q_written, UQ * h + q + 1 + 1)
                    if b >= 2:
                        dve.wait_ge(Y_written, UY * h + n - 2 + 1 + 1)
                    nc.vector.tensor_tensor(up(flat(Bl[:, l, b % 2, :, :]), s), blocks(bankQ[q % 2][:, 0:4 * HALF], s),
                                            blocks(mask[:, l, :], s), ALU.mult)
                    nc.vector.copy_predicated(up(flat(Aqk[:, 4 * b:4 * b + 4, :]), s),
                                              blocks(mask[:, l, :], s).bitcast(I32),
                                              blocks(bankQ[q % 2][:, 4 * HALF:8 * HALF], s)).then_inc(Q_drained, 1)

                def take_a(n):
                    l, b = divmod(n, B)
                    dve.wait_ge(Y_written, UY * h + n + 1 + 1)
                    if 2 <= n < B + 2:
                        dve.wait_ge(D_drained, UDD * h + n - 2 + 1 + 1)
                    if l:
                        a = bankY[:, 0:4 * HALF].rearrange("p (i n) -> p i n", n=HALF)
                    else:
                        a = bankY[:, :].rearrange("p (i n two) -> p i n two", i=4, two=2)[:, :, :, 0]
                    nc.vector.tensor_tensor(Ysb[:, b % 2, :, :], a,
                                            cc[:, 4 * b:4 * b + 4].unsqueeze(2).broadcast_to([P, 4, HALF]),
                                            ALU.mult).then_inc(Y_drained, 1)

                def take_b(n):
                    l, b = divmod(n, B)
                    s = 1 << l
                    v = low(flat(Tm[:, 4 * b:4 * b + 4, :]), s)
                    if l:
                        dve.wait_ge(D_written, UDW * h + n - B + 1 + 1)
                        a = blocks(bankD[:, 0:4 * HALF], s)
                    else:
                        dve.wait_ge(Y_drained, UY * h + n + 1 + 1)
                        a = blocks(flat(Ysb[:, b % 2, :, :]), s)
                    nc.vector.tensor_tensor(v, v, a, ALU.subtract).then_inc(D_drained, 1)

                for n in range(PAIRS + 2):
                    for lag, part in enumerate((take_pairs, take_a, take_b)):
                        if 0 <= n - lag < PAIRS:
                            part(n - lag)
                    if more and n in V_STEPS:
                        i = V_STEPS.index(n)
                        if i == 0:
                            dve.wait_ge(w_loaded, 96 * (h + 2))
                        conv(i, h + 1)
                for b in range(B):
                    n = place["kt", b]
                    dve.wait_ge(P_written, base + n + 1 + 1)
                    nc.vector.tensor_copy(flat(ktm[:, 4 * b:4 * b + 4, :]), bankP[n % 2][:, :]).then_inc(P_drained, 1)

                dve.wait_ge(rr_ready, 2 * h + 2)
                nc.vector.tensor_scalar(rq[:, :], rr[:, TILES:2 * TILES], float(DH) ** -0.5, None,
                                        ALU.mult).then_inc(rk_ready, 1)
                dve.wait_ge(rk_ready, 4 * h + 3)
                nc.vector.scalar_tensor_tensor(rq2[:, :], rq[:, :], 1.0 / DH, rq[:, :], ALU.mult,
                                               ALU.mult).then_inc(rk_ready, 1)
                dve.wait_ge(rk_ready, 4 * h + 4)

                def add_out(c, g):
                    if g == 0:
                        dve.wait_ge(yrs_ready, TPB * h + c + 1)
                        nc.vector.tensor_tensor(yscale[:, c, :], yrs[:, :], stat_of(rq[:, :], c),
                                                ALU.mult).then_inc(ysc_ready, 1)
                        dve.wait_ge(ysc_ready, TPB * h + c + 1)
                    n = place["out", 2 * c + g]
                    dve.wait_ge(P_written, base + n + 1 + 1)
                    for i in range(2):
                        b = 2 * g + i
                        x = X[:, b * TPB + c, :]
                        last = nc.vector.scalar_tensor_tensor(x, bankP[n % 2][:, i * D:(i + 1) * D],
                                                              yscale[:, c, b:b + 1], x, ALU.mult, ALU.add)
                    last.then_inc(P_drained, 1)

                dve.wait_ge(gate_done, TPB * (h + 1))
                dve.wait_ge(scaled, NL * (h + 1) + 1)
                for c in range(TPB):
                    if c:
                        dve.wait_ge(Y_written, UY * h + PAIRS + c + 1)
                        nc.vector.tensor_tensor(R1[:, :, :], bankY[:, :].rearrange("p (b n) -> p b n", n=DH),
                                                stat_of(cc[:, :], c).unsqueeze(2).broadcast_to([P, B, DH]),
                                                ALU.mult).then_inc(Y_drained, 1)
                        dve.wait_ge(Y_drained, UY * h + PAIRS + c + 1)
                        nc.vector.tensor_tensor(R1[:, :, :], chunk_of(bv[:, :, :], c), R1[:, :, :],
                                                ALU.subtract).then_inc(R1_ready, 1)
                    if c >= 2:
                        add_out(c - 2, 1)
                    if more:
                        conv(B + 2 * c, h + 1)
                    dve.wait_ge(D_written, UDW * h + PAIRS - B + c + 1 + 1)
                    if c:
                        dve.wait_ge(Z_written, UZ * h + B + c + 1)
                        dve.wait_ge(ysq_ready, B * (TPB * h + c))
                    nc.vector.tensor_tensor(y1[:, :, :], bankD[:, :].rearrange("p (b n) -> p b n", n=DH),
                                            chunk_of(gate[:, :, :], c), ALU.mult).then_inc(D_drained, 1)
                    if c < TPB - 1:
                        q = B + PAIRS + c
                        dve.wait_ge(Q_written, UQ * h + q + 1 + 1)
                        if c == 0:
                            nc.vector.tensor_copy(flat(S[:, :, :]), bankQ[q % 2][:, :]).then_inc(S_ready, 1)
                        else:
                            for b in range(B):
                                t = b * TPB + c
                                last = nc.vector.scalar_tensor_tensor(S[:, b, :], S[:, b, :], pend[:, t:t + 1],
                                                                      bankQ[q % 2][:, b * P:(b + 1) * P],
                                                                      ALU.mult, ALU.add)
                            last.then_inc(S_ready, 1)
                        dve.wait_ge(S_ready, (TPB - 1) * h + c + 1)
                        nc.vector.sem_inc(Q_drained, 1)
                    if more:
                        conv(B + 2 * c + 1, h + 1)
                    if c:
                        add_out(c - 1, 0)
                    dve.wait_ge(ysq_ready, B * (TPB * h + c + 1))
                    nc.vector.tensor_tensor(yms[:, :], ysum[:, :], stat_of(rq2[:, :], c), ALU.mult).then_inc(yms_step, 1)
                    dve.wait_ge(yms_step, TPB * h + c + 1 + 1)
                    nc.vector.tensor_scalar(yms[:, :], yms[:, :], 1e-5, None, ALU.add).then_inc(yms_ready, 1)
                add_out(TPB - 2, 1)
                add_out(TPB - 1, 0)
                add_out(TPB - 1, 1)
            heads(dve, body)


def pick_first_max(nc, link, left, picked, rank, E, tmp, mx):
    link(nc.vector.tensor_reduce(mx[:, :], left, AX_X, ALU.max))
    link(nc.vector.tensor_tensor(tmp, left, mx[:, :].unsqueeze(2).broadcast_to([P, TILES, E]), ALU.is_ge))
    link(nc.vector.tensor_tensor(tmp, tmp, rank, ALU.mult))
    link(nc.vector.tensor_reduce(mx[:, :], tmp, AX_X, ALU.max))
    link(nc.vector.tensor_tensor(picked, tmp, mx[:, :].unsqueeze(2).broadcast_to([P, TILES, E]), ALU.is_equal))


def router_block(nc, tag, XT, router, E, rank_in, weights, score=None):
    with ExitStack() as ctx:
        sb, ps, sem = pools(nc, ctx)
        rw = sb(tag + "rw", [P, KC, E])
        rank = sb(tag + "rank", [P, TILES, E])
        lg = sb(tag + "lg", [P, TILES, E])
        left = sb(tag + "left", [P, TILES, E])
        tmp = sb(tag + "tmp", [P, TILES, E])
        picked = sb(tag + "picked", [P, TILES, E])
        total = sb(tag + "total", [P, TILES, E])
        mx = sb(tag + "mx", [P, TILES])
        bank = ps(tag + "bank", [P, TILES, E])
        loaded = sem(tag + "loaded")
        logits = sem(tag + "logits")
        step = sem(tag + "step")
        for_act = sem(tag + "for_act")
        from_act = sem(tag + "from_act")
        block = ctx.enter_context(nc.Block())

        @block.sync
        def _(sp):
            sp.dma_start(rw[:, :, :], router.rearrange("(c p) n -> p c n", p=P)).then_inc(loaded, 16)
            sp.dma_start(rank[:, :, :], rank_in).then_inc(loaded, 16)
            sp.wait_ge(loaded, 32)

        @block.tensor
        def _(pe):
            pe.wait_ge(loaded, 32)
            for t in range(TILES):
                for c in range(KC):
                    last = nc.tensor.matmul(bank[:, t, :], XT[:, c, t * P:(t + 1) * P], rw[:, c, :],
                                            start=(c == 0), stop=(c == KC - 1))
            last.then_inc(logits, 1)

        @block.scalar
        def _(act):
            act.wait_ge(for_act, 1)
            if score is not None:
                nc.scalar.activation(score[:, :], mx[:, :], ACT.Sigmoid).then_inc(from_act, 1)
            else:
                nc.scalar.activation(lg[:, :, :], lg[:, :, :], ACT.Exp).then_inc(from_act, 1)

        @block.vector
        def _(dve):
            n = [0]

            def link(ins):
                n[0] += 1
                ins.then_inc(step, 1)
                dve.wait_ge(step, n[0])

            dve.wait_ge(loaded, 32)
            dve.wait_ge(logits, 1)
            link(nc.vector.tensor_copy(lg[:, :, :], bank[:, :, :]))
            link(nc.vector.tensor_reduce(mx[:, :], lg[:, :, :], AX_X, ALU.max))
            if score is not None:
                nc.vector.sem_inc(for_act, 1)
                dve.wait_ge(from_act, 1)
                pick_first_max(nc, link, lg[:, :, :], picked[:, :, :], rank[:, :, :], E, tmp[:, :, :], mx)
                link(nc.vector.tensor_copy(weights[:, 0:E, :].rearrange("p e t -> p t e"), picked[:, :, :]))
            else:
                link(nc.vector.tensor_tensor(lg[:, :, :], lg[:, :, :],
                                             mx[:, :].unsqueeze(2).broadcast_to([P, TILES, E]), ALU.subtract))
                nc.vector.sem_inc(for_act, 1)
                dve.wait_ge(from_act, 1)
                link(nc.vector.tensor_copy(left[:, :, :], lg[:, :, :]))
                link(nc.vector.memset(total[:, :, :], 0.0))
                for _ in range(TOPK):
                    pick_first_max(nc, link, left[:, :, :], picked[:, :, :], rank[:, :, :], E, tmp[:, :, :], mx)
                    link(nc.vector.tensor_tensor(total[:, :, :], total[:, :, :], picked[:, :, :], ALU.add))
                    link(nc.vector.scalar_tensor_tensor(left[:, :, :], picked[:, :, :], -4.0, left[:, :, :],
                                                        ALU.mult, ALU.add))
                link(nc.vector.tensor_tensor(lg[:, :, :], lg[:, :, :], total[:, :, :], ALU.mult))
                link(nc.vector.tensor_reduce(mx[:, :], lg[:, :, :], AX_X, ALU.add))
                link(nc.vector.reciprocal(mx[:, :], mx[:, :]))
                link(nc.vector.tensor_tensor(weights[:, 0:E, :].rearrange("p e t -> p t e"), lg[:, :, :],
                                             mx[:, :].unsqueeze(2).broadcast_to([P, TILES, E]), ALU.mult))
            link(nc.vector.memset(weights[:, E:, :], 1.0))


def experts_block(nc, tag, X, runs, weights, gate_up, down, second):
    FC = 2
    small = second <= HALF
    FEATURES = (P, second)
    WIDTH = gate_up.shape[2]
    with ExitStack() as ctx:
        sb, ps, sem = pools(nc, ctx)
        gu = [sb(f"{tag}gu{j}", [P, KC, WIDTH]) for j in range(2)]
        dn = [sb(f"{tag}dn{j}", [P, FC, D]) for j in range(2)]
        sg = [sb(f"{tag}sg{j}", [P, T]) for j in range(2)]
        hT = [sb(f"{tag}hT{j}", [P, FC, T]) for j in range(2)]
        bank_g = [ps(f"{tag}bank_g{j}", [P, T]) for j in range(2)]
        bank_u = [ps(f"{tag}bank_u{j}", [P, T]) for j in range(2)]
        bank_d = [ps(f"{tag}bank_d{j}", [P, 2, D]) for j in range(2)]
        loaded = [sem(f"{tag}loaded{j}") for j in range(2)]
        used = sem(tag + "used")
        sp_turn = sem(tag + "sp_turn")
        g_written, u_written = sem(tag + "g_written"), sem(tag + "u_written")
        silu_done = sem(tag + "silu_done")
        h_ready = sem(tag + "h_ready")
        d_written, d_drained = sem(tag + "d_written"), sem(tag + "d_drained")
        block = ctx.enter_context(nc.Block())
        UF = FC * B
        UU = B if small else UF
        LOADS = 16 * (1 + FC)
        UDN = 2 * B

        def over(eng, body):
            for first, count, xt in runs:
                if count >= 2:
                    assert count % 2 == 0 and first % 2 == 0
                    with eng.Fori(0, count // 2) as i:
                        for j in range(2):
                            body(2 * i + (first + j), j, i + first // 2, xt)
                else:
                    body(first, first % 2, first // 2, xt)

        @block.sync
        def _(sp):
            def body(e, j, pair, xt):
                sp.wait_ge(used, e + 1)
                sp.sem_inc(sp_turn, 1)
                src = gate_up[bass.ds(e, 1), :, :] if not isinstance(e, int) else gate_up[e:e + 1, :, :]
                sp.dma_start(gu[j][:, :, :], src.rearrange("e (c p) n -> p c (e n)", p=P)).then_inc(loaded[j], 16)
                src = down[bass.ds(e, 1), :, :] if not isinstance(e, int) else down[e:e + 1, :, :]
                for f, q in enumerate(FEATURES):
                    sp.dma_start(dn[j][0:q, f, :], src[:, f * P:f * P + q, :].rearrange("e q n -> q (e n)")
                                 ).then_inc(loaded[j], 16)
            over(sp, body)

        def products(f):
            if small and f:
                return [(slice(2 * P, WIDTH), bank_u, g_written)]
            g = slice(f * P, (f + 1) * P)
            u = slice((FC - small) * P + f * P, (FC - small) * P + (f + 1) * P)
            return [(g, bank_g, g_written), (u, bank_u, u_written)]

        @block.tensor
        def _(pe):
            pe.sem_inc(d_written, 1)

            def body(e, j, pair, xt):
                def up(b):
                    for f in range(FC):
                        n = FC * b + f
                        for cols, bank, written in products(f):
                            pe.wait_ge(h_ready, UF * e + n + 1)
                            for c in range(KC):
                                last = nc.tensor.matmul(bank[f][0:cols.stop - cols.start, :], gu[j][:, c, cols],
                                                        xt[:, c, b * T:(b + 1) * T],
                                                        start=(c == 0), stop=(c == KC - 1))
                            last.then_inc(written, 1)

                def down_b(b):
                    pe.wait_ge(h_ready, UF * e + FC * (b + 1) + 2)
                    for g in range(2):
                        pe.wait_ge(d_drained, UDN * e + 2 * b + g + 1)
                        for i in range(2):
                            t = 2 * g + i
                            for f in range(FC):
                                q = FEATURES[f]
                                last = nc.tensor.matmul(bank_d[g][:, i, :], hT[b % 2][0:q, f, t * P:(t + 1) * P],
                                                        dn[j][0:q, f, :], start=(f == 0), stop=(f == FC - 1))
                        last.then_inc(d_written, 1)

                pe.wait_ge(loaded[j], LOADS * (pair + 1))
                for b in range(B + 1):
                    if b < B:
                        up(b)
                    if b >= 1:
                        down_b(b - 1)
            over(pe, body)

        @block.scalar
        def _(act):
            def body(e, j, pair, xt):
                for n in range(UF):
                    f = n % FC
                    act.wait_ge(g_written, UF * e + n + 1)
                    act.wait_ge(h_ready, UF * e + n + 1)
                    q = FEATURES[f]
                    src = bank_u[f][HALF:HALF + q, :] if small and f else bank_g[f][0:q, :]
                    nc.scalar.activation(sg[f][0:q, :], src, ACT.Silu).then_inc(silu_done, 1)
            over(act, body)

        @block.vector
        def _(dve):
            nc.vector.sem_inc(used, 2)
            nc.vector.sem_inc(h_ready, 2)
            nc.vector.sem_inc(d_drained, 2)

            def body(e, j, pair, xt):
                def take_down(b):
                    for g in range(2):
                        dve.wait_ge(d_written, 1 + UDN * e + 2 * b + g + 1)
                        for i in range(2):
                            t = 4 * b + 2 * g + i
                            wt = weights[:, e, t:t + 1] if isinstance(e, int) else \
                                weights[:, bass.ds(e, 1), t:t + 1].rearrange("p a b -> p (a b)")
                            last = nc.vector.scalar_tensor_tensor(X[:, t, :], bank_d[g][:, i, :], wt, X[:, t, :],
                                                                  ALU.mult, ALU.add)
                        last.then_inc(d_drained, 1)

                for b in range(B + 1):
                    if b < B:
                        for f in range(FC):
                            n = FC * b + f
                            if not (small and f):
                                dve.wait_ge(u_written, UU * e + (b if small else n) + 1)
                            dve.wait_ge(silu_done, UF * e + n + 1)
                            if b >= 2:
                                dve.wait_ge(d_written, 1 + UDN * e + 2 * (b - 1))
                            else:
                                dve.wait_ge(d_written, 1 + UDN * e)
                            q = FEATURES[f]
                            nc.vector.tensor_tensor(hT[b % 2][0:q, f, :], sg[f][0:q, :], bank_u[f][0:q, :],
                                                    ALU.mult).then_inc(h_ready, 1)
                    if b >= 1:
                        take_down(b - 1)
                nc.vector.sem_inc(used, 1)
            over(dve, body)


def alibi_block(nc, X, XT, ident, w, consts):
    HQ = P // SLOT
    G = H // HQ
    GU = HQ * TPB
    TBL = 2 * T - P
    UNITS = TPB * H
    R = 4
    TURN, VALUE = 2, 2 + TPB
    SPREAD = VALUE + 2
    PV = TILES // 2
    FIRST = PV + 2 * G
    RING = [x for g in range(G) for x in (("q", g), ("k", g), ("sum", g))] + [("out", i) for i in range(TPB // 2)]
    with ExitStack() as ctx:
        sb, ps, sem = pools(nc, ctx)
        wq = sb("c_wq", [P, KC, H * SLOT])
        wk = sb("c_wk", [P, KC, H * SLOT])
        wv = sb("c_wv", [P, KC, D])
        wo = sb("c_wo", [P, G, D])
        bq = sb("c_bq", [P, G])
        bk = sb("c_bk", [P, G])
        bvr = sb("c_bv", [P, D])
        bor = sb("c_bo", [P, D])
        slopes = sb("c_slopes", [P, H])
        dist = sb("c_dist", [P, TBL])
        spread = sb("c_spread", [P, P])
        table = sb("c_table", [P, H, TBL])
        V = sb("c_V", [P, TILES, H, DA])
        Vb = sb("c_Vb", [P, TPB, H, SLOT])
        Q = sb("c_Q", [P, G, T])
        K = sb("c_K", [P, G, T])
        s = [sb(f"c_s{j}", [P, T]) for j in range(R)]
        pr = [sb(f"c_p{j}", [P, T]) for j in range(R)]
        pT = [sb(f"c_pT{j}", [P, TPB, T]) for j in range(2)]
        nmax = sb("c_nmax", [P, R])
        oraw = [sb(f"c_oraw{j}", [P, T]) for j in range(2)]
        rinv = sb("c_rinv", [P, T])
        oT = sb("c_oT", [P, G, T])
        bank_s = [ps(f"c_bank_s{j}", [P, T]) for j in range(2)]
        bank_t = [ps(f"c_bank_t{j}", [P, T]) for j in range(2)]
        bank_o = [ps(f"c_bank_o{j}", [P, T]) for j in range(2)]
        bank_p = [ps(f"c_bank_p{j}", [P, T]) for j in range(2)]
        proj_loaded, rest_loaded = sem("c_proj_loaded"), sem("c_rest_loaded")
        table_loaded = sem("c_table_loaded")
        ones_ready, x_biased = sem("c_ones_ready"), sem("c_x_biased")
        table_ready = sem("c_table_ready")
        p_written, p_drained = sem("c_p_written"), sem("c_p_drained")
        s_written, s_taken = sem("c_s_written"), sem("c_s_taken")
        exp_done = sem("c_exp_done")
        t_written, t_taken = sem("c_t_written"), sem("c_t_taken")
        o_written, o_taken = sem("c_o_written"), sem("c_o_taken")
        rinv_ready, oT_ready = sem("c_rinv_ready"), sem("c_oT_ready")
        vb_ready = sem("c_vb_ready")
        dve_turn = sem("c_dve_turn")
        block = ctx.enter_context(nc.Block())

        def unit(b, what, i, last):
            order = [x for x in RING if not last or x[0] in ("sum", "out")]
            n = order.index((what, i))
            return len(RING) * b + (FIRST + n), (FIRST + n) % 2

        @block.gpsimd
        def _(pool):
            nc.gpsimd.memset(Vb[:, :, :, :], 1.0).then_inc(ones_ready, 1)
            pool.wait_ge(table_loaded, 16 * 3)
            nc.gpsimd.tensor_scalar(table[:, 0, :], dist[:, :], slopes[:, 0:1], None, ALU.mult).then_inc(table_ready, 1)
            nc.gpsimd.tensor_tensor(X[:, :, :], X[:, :, :], bor[:, :].unsqueeze(1).broadcast_to([P, TILES, D]),
                                    ALU.add).then_inc(x_biased, 1)
            for h in range(1, H):
                nc.gpsimd.tensor_scalar(table[:, h, :], dist[:, :], slopes[:, h:h + 1], None,
                                        ALU.mult).then_inc(table_ready, 1)

        @block.sync
        def _(sp):
            chunks = "(c p) n -> p c n"
            for dst, src in ((wv[:, :, :], w["L1_attn_WvT"].rearrange(chunks, p=P)),
                             (bvr[:, :], rows(w["L1_attn_bv"])),
                             (wq[:, :, :], w["L1_attn_WqT"].rearrange(chunks, p=P)),
                             (bq[:, :], w["L1_attn_bq"]), (bk[:, :], w["L1_attn_bk"]),
                             (wk[:, :, :], w["L1_attn_WkT"].rearrange(chunks, p=P))):
                sp.dma_start(dst, src).then_inc(proj_loaded, 16)
            for dst, src in ((wo[:, :, :], w["L1_attn_WoT"].rearrange(chunks, p=P)),
                             (spread[:, :], consts["spread"])):
                sp.dma_start(dst, src).then_inc(rest_loaded, 16)
            sp.wait_ge(proj_loaded, 16 * 6)
            sp.wait_ge(rest_loaded, 16 * 2)

        @block.tensor
        def _(pe):
            pe.sem_inc(s_written, 1)
            pe.sem_inc(t_written, R)
            pe.sem_inc(o_written, 1)

            def project_head_group(n, g, which, b):
                m = (wq, wk)[which]
                for c in range(KC):
                    last = nc.tensor.matmul(bank_p[n % 2][:, :], m[:, c, g * P:(g + 1) * P],
                                            XT[:, c, bass.ds(b * T, T)], start=(c == 0), stop=(c == KC - 1))
                last.then_inc(p_written, 1)

            pe.wait_ge(proj_loaded, 16 * 6)
            for n in range(2 * G):
                pe.wait_ge(p_drained, n + 1)
                project_head_group(n, n // 2, n % 2, 0)
            for n in range(PV):
                pe.wait_ge(p_drained, 2 * G + n + 1)
                for i in range(2):
                    t = 2 * n + i
                    for c in range(KC):
                        last = nc.tensor.matmul(bank_p[n % 2][:, i * D:(i + 1) * D], XT[:, c, t * P:(t + 1) * P],
                                                wv[:, c, :], start=(c == 0), stop=(c == KC - 1))
                last.then_inc(p_written, 1)
            pe.wait_ge(rest_loaded, 16 * 2)

            def scores(u, b):
                h, it = divmod(u, TPB)
                g, a = divmod(h, HQ)
                if u % GU == 0:
                    if isinstance(b, int) and b == 0:
                        pe.wait_ge(p_drained, FIRST + 2)
                    else:
                        pe.wait_ge(p_drained, len(RING) * b + (FIRST - len(RING) + RING.index(("k", g)) + 1 + 2))
                pe.wait_ge(s_taken, UNITS * b + u + 1)
                r = slice(a * SLOT, (a + 1) * SLOT)
                nc.tensor.matmul(bank_s[u % 2][:, :], Q[r, g, it * P:(it + 1) * P], K[r, g, :],
                                 start=True, stop=True).then_inc(s_written, 1)

            def turn(u, b):
                pe.wait_ge(exp_done, UNITS * b + u + 1 + R)
                pe.wait_ge(t_taken, UNITS * b + u + 1)
                for j in range(TPB):
                    last = nc.tensor.transpose(bank_t[u % 2][:, j * P:(j + 1) * P],
                                               pr[u % R][:, j * P:(j + 1) * P], ident[:, :])
                last.then_inc(t_written, 1)

            def value(u, b):
                h, j = divmod(u, TPB)
                g, a = divmod(h, HQ)
                if j == 0:
                    pe.wait_ge(t_taken, UNITS * b + TPB * (h + 1) + 2)
                if u == 0:
                    pe.wait_ge(vb_ready, b + 1)
                if u % GU == 0:
                    pe.wait_ge(o_taken, G * b + g + 1)
                last = nc.tensor.matmul(bank_o[g % 2][a * SLOT:(a + 1) * SLOT, :], Vb[:, j, h, :],
                                        pT[h % 2][:, j, :], start=(j == 0), stop=(j == TPB - 1))
                if u % GU == GU - 1:
                    last.then_inc(o_written, 1)

            def sums(g, b, last_b):
                n, bank = unit(b, "sum", g, last_b)
                pe.wait_ge(o_taken, G * b + g + 1 + 2)
                pe.wait_ge(p_drained, n + 1)
                nc.tensor.matmul(bank_p[bank][:, :], spread[:, :], oraw[g % 2][:, :],
                                 start=True, stop=True).then_inc(p_written, 1)

            def sequence(b, last_b):
                for u in range(UNITS + SPREAD):
                    if u < UNITS:
                        scores(u, b)
                    if 0 <= u - TURN < UNITS:
                        turn(u - TURN, b)
                    if 0 <= u - VALUE < UNITS:
                        value(u - VALUE, b)
                    if not last_b and u % GU == 0 and u > 0:
                        g = u // GU - 1
                        for which, nm in enumerate("qk"):
                            n, bank = unit(b, nm, g, last_b)
                            pe.wait_ge(p_drained, n + 1)
                            project_head_group(bank, g, which, b + 1)
                    v = u - SPREAD + 1
                    if v >= 0 and v % GU == GU - 1:
                        sums(v // GU, b, last_b)
                pe.wait_ge(oT_ready, G * b + G + 2)
                for i in range(TPB // 2):
                    n, bank = unit(b, "out", i, last_b)
                    pe.wait_ge(p_drained, n + 1)
                    for k in range(2):
                        t = 2 * i + k
                        for g in range(G):
                            last = nc.tensor.matmul(bank_p[bank][:, k * D:(k + 1) * D], oT[:, g, t * P:(t + 1) * P],
                                                    wo[:, g, :], start=(g == 0), stop=(g == G - 1))
                    last.then_inc(p_written, 1)

            with pe.Fori(0, B - 1) as b:
                sequence(b, False)
            sequence(B - 1, True)

        @block.scalar
        def _(act):
            for dst, src in ((dist[:, :], consts["dist"]), (slopes[:, :], rows(w["L1_attn_slopes"])),
                             (bor[:, :], rows(w["L1_attn_bo"]))):
                act.dma_start(dst, src).then_inc(table_loaded, 16)
            nc.scalar.sem_inc(exp_done, R)
            nc.scalar.sem_inc(o_taken, 2)

            def sequence(b):
                for u in range(UNITS + SPREAD - 1):
                    if u < UNITS:
                        act.wait_ge(s_taken, UNITS * b + u + 1 + 2)
                        act.wait_ge(t_written, UNITS * b + u + 1)
                        nc.scalar.activation(pr[u % R][:, :], s[u % R][:, :], ACT.Exp, scale=-1.0,
                                             bias=nmax[:, u % R:u % R + 1]).then_inc(exp_done, 1)
                    if u == 1:
                        act.wait_ge(o_written, 1 + G * b)
                        nc.scalar.activation(Vb[:, :, :, 0:DA], V[:, bass.ds(b * TPB, TPB), :, :],
                                             ACT.Copy).then_inc(vb_ready, 1)
                    v = u - VALUE
                    if v >= 0 and v % GU == GU - 1:
                        g = v // GU
                        act.wait_ge(o_written, 1 + G * b + g + 1)
                        act.wait_ge(oT_ready, G * b + g + 1)
                        nc.scalar.activation(oraw[g % 2][:, :], bank_o[g % 2][:, :], ACT.Copy).then_inc(o_taken, 1)

            act.wait_ge(ones_ready, 1)
            act.wait_ge(p_drained, FIRST + 2)
            with act.Fori(0, B) as b:
                sequence(b)

        @block.vector
        def _(dve):
            nc.vector.sem_inc(rinv_ready, 1)
            nc.vector.sem_inc(p_drained, 2)
            nc.vector.sem_inc(s_taken, 2)
            nc.vector.sem_inc(t_taken, 2)
            nc.vector.sem_inc(oT_ready, 2)

            def drain_head_group(bank, g, which):
                nc.vector.tensor_scalar((Q, K)[which][:, g, :], bank_p[bank][:, :], (bq, bk)[which][:, g:g + 1],
                                        1.0 if which else -float(DA) ** -0.5, ALU.add, ALU.mult).then_inc(p_drained, 1)

            dve.wait_ge(proj_loaded, 16 * 6)
            for n in range(2 * G):
                dve.wait_ge(p_written, n + 1)
                drain_head_group(n % 2, n // 2, n % 2)
            for n in range(PV):
                dve.wait_ge(p_written, 2 * G + n + 1)
                nc.vector.tensor_tensor(V[:, 2 * n:2 * n + 2, :, :].rearrange("p i h d -> p i (h d)"),
                                        bank_p[n % 2][:, :].rearrange("p (i n) -> p i n", n=D),
                                        bvr[:, :].unsqueeze(1).broadcast_to([P, 2, D]), ALU.add).then_inc(p_drained, 1)
            dve.wait_ge(x_biased, 1)

            def take_scores(u, b):
                h, it = divmod(u, TPB)
                dve.wait_ge(s_written, 1 + UNITS * b + u + 1)
                dve.wait_ge(exp_done, UNITS * b + u + 1)
                if it == 0:
                    dve.wait_ge(table_ready, h + 1)
                off = T - P - it * P
                nc.vector.sem_inc(dve_turn, 1)
                nc.vector.tensor_tensor_reduce(out=s[u % R][:, :], in0=bank_s[u % 2][:, :],
                                               in1=table[:, h, off:off + T], scale=1.0, scalar=3.0e38,
                                               op0=ALU.add, op1=ALU.min,
                                               accum_out=nmax[:, u % R:u % R + 1]).then_inc(s_taken, 1)

            def take_turn(u, b):
                h, it = divmod(u, TPB)
                dve.wait_ge(t_written, UNITS * b + u + 1 + R)
                nc.vector.tensor_copy(pT[h % 2][:, :, it * P:(it + 1) * P],
                                      bank_t[u % 2][:, :].rearrange("p (j q) -> p j q", q=P)).then_inc(t_taken, 1)

            def normalise(g, b, last_b):
                n, bank = unit(b, "sum", g, last_b)
                dve.wait_ge(p_written, n + 1)
                nc.vector.reciprocal(rinv[:, :], bank_p[bank][:, :]).then_inc(rinv_ready, 1)
                dve.wait_ge(rinv_ready, 1 + G * b + g + 1)
                nc.vector.sem_inc(p_drained, 1)
                nc.vector.tensor_tensor(oT[:, g, :], oraw[g % 2][:, :], rinv[:, :], ALU.mult).then_inc(oT_ready, 1)

            def sequence(b, last_b):
                for u in range(UNITS + SPREAD):
                    if u < UNITS:
                        take_scores(u, b)
                    if 0 <= u - TURN < UNITS:
                        take_turn(u - TURN, b)
                    if not last_b and u % GU == 0 and u > 0:
                        for which, nm in enumerate("qk"):
                            n, bank = unit(b, nm, u // GU - 1, last_b)
                            dve.wait_ge(p_written, n + 1)
                            drain_head_group(bank, u // GU - 1, which)
                    v = u - SPREAD + 1
                    if v >= 0 and v % GU == GU - 1:
                        normalise(v // GU, b, last_b)
                for i in range(TPB // 2):
                    n, bank = unit(b, "out", i, last_b)
                    dve.wait_ge(p_written, n + 1)
                    x = X[:, bass.ds(b * TPB + 2 * i, 2), :]
                    nc.vector.tensor_tensor(x, bank_p[bank][:, :].rearrange("p (i n) -> p i n", n=D), x,
                                            ALU.add).then_inc(p_drained, 1)

            with dve.Fori(0, B - 1) as b:
                sequence(b, False)
            sequence(B - 1, True)


def latent_block(nc, X, XT, ident, w, consts):
    UNITS = TILES
    R = 4
    TURN, VALUE = 2, 3
    PROJ = 3 * B
    OUT = 2 * B
    STEPS = UNITS + VALUE + 2
    ring = {u: [] for u in range(STEPS)}
    for b in range(B):
        u = TPB * (b + 1)
        ring[u].append(("proj", b, 0))
        ring[u + 1].append(("proj", b, 1))
        ring[u + VALUE].append(("proj", b, 2))
        ring[u + VALUE + 1].append(("out", b, 0))
        ring[min(u + VALUE + 2, STEPS - 1)].append(("out", b, 1))
    with ExitStack() as ctx:
        sb, ps, sem = pools(nc, ctx)
        W = sb("l_W", [P, 3, KC, NOPE])
        wo = sb("l_wo", [P, D])
        Q = sb("l_Q", [P, N])
        K = sb("l_K", [P, N])
        V = sb("l_V", [P, TILES, VD])
        mask = sb("l_mask", [P, T])
        s = [sb(f"l_s{j}", [P, T]) for j in range(R)]
        pr = [sb(f"l_p{j}", [P, T]) for j in range(R)]
        pT = [sb(f"l_pT{j}", [P, T]) for j in range(2)]
        nmax = sb("l_nmax", [P, R])
        rsum = sb("l_rsum", [P, TILES])
        rinv = sb("l_rinv", [P, TILES])
        oT = sb("l_oT", [P, TILES, P])
        bank_p = [ps(f"l_bank_p{j}", [P, T]) for j in range(2)]
        bank_s = [ps(f"l_bank_s{j}", [P, T]) for j in range(2)]
        bank_t = [ps(f"l_bank_t{j}", [P, T]) for j in range(2)]
        bank_o = [ps(f"l_bank_o{j}", [P, TPB, P]) for j in range(2)]
        mask_loaded = sem("l_mask_loaded")
        w_loaded = [sem(f"l_w_loaded_{x}") for x in "qkvo"]
        sp_turn, dve_turn = sem("l_sp_turn"), sem("l_dve_turn")
        p_written = sem("l_p_written")
        copied, added = sem("l_copied"), sem("l_added")
        s_written, s_taken, exp_done = (sem("l_" + x) for x in ("s_written", "s_taken", "exp_done"))
        t_written, t_taken = sem("l_t_written"), sem("l_t_taken")
        o_written, o_taken = sem("l_o_written"), sem("l_o_taken")
        rinv_ready = sem("l_rinv_ready")
        block = ctx.enter_context(nc.Block())

        def order(last):
            return [x for u in range(STEPS) for x in ring[u] if not last or x[0] == "out"]

        def written(h, x, last):
            return (PROJ + OUT) * h + (PROJ + order(last).index(x) + 1)

        def bank_of(x, last):
            return bank_p[order(last).index(x) % 2]

        @block.sync
        def _(sp):
            def load(k, h):
                nm, first, step = (("q_wT", 0, QHD), ("kv_wT", 0, NOPE), ("kv_wT", H * NOPE, VD))[k]
                src = w["L1_ffn_" + nm].rearrange("(c p) n -> p c n", p=P)
                sp.dma_start(W[:, k, :, :], src[:, :, bass.ds(h * step + first, NOPE)]).then_inc(w_loaded[k], 16)

            def load_out(h):
                sp.dma_start(wo[:, :], w["L1_ffn_o_wT"][bass.ds(h * VD, VD), :]).then_inc(w_loaded[3], 16)

            for k in range(3):
                load(k, 0)
            sp.dma_start(mask[:, :], consts["causal"]).then_inc(mask_loaded, 16)
            sp.wait_ge(mask_loaded, 16)
            with sp.Fori(1, H) as h:
                for k in range(3):
                    sp.wait_ge(copied, PROJ * h + (k - 2))
                    sp.sem_inc(sp_turn, 1)
                    load(k, h)
                sp.wait_ge(added, OUT * h)
                sp.sem_inc(sp_turn, 1)
                load_out(h - 1)
            sp.wait_ge(added, OUT * H)
            load_out(H - 1)

        @block.tensor
        def _(pe):
            pe.sem_inc(t_written, R)
            pe.sem_inc(s_written, 1)
            pe.sem_inc(o_written, 1)

            def project(bank, b, k):
                if k < 2:
                    for c in range(KC):
                        last = nc.tensor.matmul(bank[:, :], W[:, k, c, :], XT[:, c, b * T:(b + 1) * T],
                                                start=(c == 0), stop=(c == KC - 1))
                else:
                    for i in range(TPB):
                        t = b * TPB + i
                        for c in range(KC):
                            last = nc.tensor.matmul(bank[:, i * VD:(i + 1) * VD], XT[:, c, t * P:(t + 1) * P],
                                                    W[:, k, c, :], start=(c == 0), stop=(c == KC - 1))
                last.then_inc(p_written, 1)

            for n in range(PROJ):
                b, k = divmod(n, 3)
                if b == 0:
                    pe.wait_ge(w_loaded[k], 16)
                if n >= 2:
                    pe.wait_ge(copied, n - 1)
                project(bank_p[n % 2], b, k)
            pe.wait_ge(copied, PROJ)

            def scores(u, h):
                b, it = divmod(u, TPB)
                if it == 0:
                    pe.wait_ge(copied, PROJ * h + 3 * b + 2)
                pe.wait_ge(s_taken, UNITS * h + u + 1)
                nc.tensor.matmul(bank_s[u % 2][:, 0:(it + 1) * P], Q[:, u * P:(u + 1) * P],
                                 K[:, b * T:b * T + (it + 1) * P], start=True, stop=True).then_inc(s_written, 1)

            def turn(u, h):
                pe.wait_ge(exp_done, UNITS * h + u + 1 + R)
                pe.wait_ge(t_taken, UNITS * h + u + 1)
                for j in range(u % TPB + 1):
                    last = nc.tensor.transpose(bank_t[u % 2][:, j * P:(j + 1) * P],
                                               pr[u % R][:, j * P:(j + 1) * P], ident[:, :])
                last.then_inc(t_written, 1)

            def value(u, h):
                b, it = divmod(u, TPB)
                if it == 0:
                    pe.wait_ge(copied, PROJ * h + 3 * b + 3)
                    pe.wait_ge(o_taken, B * h + b + 1)
                pe.wait_ge(t_taken, UNITS * h + u + 1 + 2)
                for j in range(it + 1):
                    last = nc.tensor.matmul(bank_o[b % 2][:, it, :], V[:, b * TPB + j, :],
                                            pT[u % 2][:, j * P:(j + 1) * P], start=(j == 0), stop=(j == it))
                if it == TPB - 1:
                    last.then_inc(o_written, 1)

            def wait_for_bank(x, h, last_h):
                units = order(last_h)
                n = units.index(x)
                if n >= 2 or not last_h:
                    kind, b, k = units[n - 2]
                else:
                    kind, b, k = order(False)[n - 2]
                before = 0 if n >= 2 else 1
                if kind == "proj":
                    pe.wait_ge(copied, PROJ * h + (PROJ * (1 - before) + 3 * b + k + 1))
                else:
                    pe.wait_ge(added, OUT * h + (OUT * (1 - before) + 2 * b + k + 1))

            def head(h, last_h):
                for u in range(STEPS):
                    if u < UNITS:
                        scores(u, h)
                    if 0 <= u - TURN < UNITS:
                        turn(u - TURN, h)
                    if 0 <= u - VALUE < UNITS:
                        value(u - VALUE, h)
                    for x in ring[u]:
                        kind, b, k = x
                        if last_h and kind == "proj":
                            continue
                        wait_for_bank(x, h, last_h)
                        bank = bank_of(x, last_h)
                        if kind == "proj":
                            if b == 0:
                                pe.wait_ge(w_loaded[k], 16 * h + 32)
                            project(bank, b, k)
                            continue
                        if (b, k) == (0, 0):
                            pe.wait_ge(w_loaded[3], 16 * h + 16)
                        if k == 0:
                            pe.wait_ge(o_taken, B * h + b + 1 + 2)
                        for i in range(2):
                            last = nc.tensor.matmul(bank[:, i * D:(i + 1) * D], oT[:, b * TPB + 2 * k + i, :],
                                                    wo[:, :], start=True, stop=True)
                        last.then_inc(p_written, 1)

            with pe.Fori(0, H - 1) as h:
                head(h, False)
            head(H - 1, True)

        @block.scalar
        def _(act):
            nc.scalar.sem_inc(exp_done, R)
            nc.scalar.sem_inc(o_taken, 2)

            def copy(bank, b, k):
                if k < 2:
                    nc.scalar.activation((Q, K)[k][:, b * T:(b + 1) * T], bank[:, :], ACT.Copy,
                                         scale=-float(QHD) ** -0.5 if k == 0 else 1.0).then_inc(copied, 1)
                else:
                    nc.scalar.activation(V[:, b * TPB:(b + 1) * TPB, :].rearrange("p t n -> p (t n)"),
                                         bank[:, :], ACT.Copy).then_inc(copied, 1)

            for n in range(PROJ):
                act.wait_ge(p_written, n + 1)
                copy(bank_p[n % 2], *divmod(n, 3))

            def head(h, last_h):
                for u in range(STEPS):
                    if u < UNITS:
                        w_ = (u % TPB + 1) * P
                        act.wait_ge(s_taken, UNITS * h + u + 1 + 2)
                        act.wait_ge(t_written, UNITS * h + u + 1)
                        if u % TPB == 0:
                            act.wait_ge(rinv_ready, B * h + u // TPB + 1)
                        nc.scalar.activation(pr[u % R][:, 0:w_], s[u % R][:, 0:w_], ACT.Exp, scale=-1.0,
                                             bias=nmax[:, u % R:u % R + 1],
                                             accum_out=rsum[:, u:u + 1]).then_inc(exp_done, 1)
                    v = u - VALUE
                    if v >= 0 and v % TPB == TPB - 1:
                        b = v // TPB
                        act.wait_ge(o_written, 1 + B * h + b + 1)
                        act.wait_ge(added, OUT * h + 2 * b + 2)
                        nc.scalar.activation(oT[:, b * TPB:(b + 1) * TPB, :], bank_o[b % 2][:, :, :],
                                             ACT.Copy).then_inc(o_taken, 1)
                    for x in ring[u]:
                        if x[0] == "proj" and not last_h:
                            act.wait_ge(p_written, written(h, x, last_h))
                            copy(bank_of(x, last_h), *x[1:])

            with act.Fori(0, H - 1) as h:
                head(h, False)
            head(H - 1, True)

        @block.vector
        def _(dve):
            nc.vector.sem_inc(added, OUT)
            nc.vector.sem_inc(rinv_ready, B)
            nc.vector.sem_inc(s_taken, 2)
            nc.vector.sem_inc(t_taken, 2)
            dve.wait_ge(mask_loaded, 16)

            def take_scores(u, h):
                w_ = (u % TPB + 1) * P
                dve.wait_ge(s_written, 1 + UNITS * h + u + 1)
                dve.wait_ge(exp_done, UNITS * h + u + 1)
                nc.vector.sem_inc(dve_turn, 1)
                nc.vector.tensor_tensor_reduce(out=s[u % R][:, 0:w_], in0=bank_s[u % 2][:, 0:w_],
                                               in1=mask[:, T - w_:T], scale=1.0, scalar=3.0e38,
                                               op0=ALU.add, op1=ALU.min,
                                               accum_out=nmax[:, u % R:u % R + 1]).then_inc(s_taken, 1)

            def take_turn(u, h):
                w_ = (u % TPB + 1) * P
                dve.wait_ge(t_written, UNITS * h + u + 1 + R)
                nc.vector.tensor_copy(pT[u % 2][:, 0:w_], bank_t[u % 2][:, 0:w_]).then_inc(t_taken, 1)

            def head(h, last_h):
                for u in range(STEPS):
                    if u < UNITS:
                        take_scores(u, h)
                    if 0 <= u - TURN < UNITS:
                        take_turn(u - TURN, h)
                    for x in ring[u]:
                        kind, b, k = x
                        if kind != "out":
                            continue
                        if k == 0:
                            dve.wait_ge(exp_done, UNITS * h + TPB * (b + 1) + R)
                            nc.vector.reciprocal(rinv[:, TPB * b:TPB * (b + 1)],
                                                 rsum[:, TPB * b:TPB * (b + 1)]).then_inc(rinv_ready, 1)
                            dve.wait_ge(rinv_ready, B * h + b + 1 + B)
                        dve.wait_ge(p_written, written(h, x, last_h))
                        for i in range(2):
                            t = b * TPB + 2 * k + i
                            last = nc.vector.scalar_tensor_tensor(X[:, t, :], bank_of(x, last_h)[:, i * D:(i + 1) * D],
                                                                  rinv[:, t:t + 1], X[:, t, :], ALU.mult, ALU.add)
                        last.then_inc(added, 1)

            with dve.Fori(0, H - 1) as h:
                head(h, False)
            head(H - 1, True)


def sum_block(nc, X, Y):
    with ExitStack() as ctx:
        block = ctx.enter_context(nc.Block())

        @block.vector
        def _(dve):
            nc.vector.tensor_tensor(X[:, :, :], X[:, :, :], Y[:, :, :], ALU.add)


def last_part(nc, X, HID, XT, ident, w, consts):
    norm_block(nc, "n4_", X, XT, ident, 1e-5, rows_out=HID)
    norm_block(nc, "n5_", HID, XT, ident, 1e-6, rms_weight=w["L1_ffn_ln1_w"])
    latent_block(nc, HID, XT, ident, w, consts)
    norm_block(nc, "n6_", HID, XT, ident, 1e-6, rms_weight=w["L1_ffn_ln2_w"])
    with ExitStack() as part:
        weights = part.enter_context(nc.sbuf_tensor("e1_weights", [P, E1 + NSH, TILES], F32))
        router_block(nc, "r1_", XT, w["L1_ffn_gate_wT"], E1, consts["rank1"], weights)
        experts_block(nc, "e1_", HID, [(0, E1 + NSH, XT)], weights,
                      w["L1_ffn_gate_up"], w["L1_ffn_down"], I1 - P)
    sum_block(nc, X, HID)


def clear_block(nc):
    used = sorted(nc.released_uncleared_semaphores)
    assert used == list(range(used[0], used[-1] + 1))
    with ExitStack() as ctx:
        block = ctx.enter_context(nc.Block())

        @block.gpsimd
        def _(pool):
            pool.sem_clear(range(used[0], used[-1] + 1))


def store_block(nc, X, out):
    with ExitStack() as ctx:
        sb, ps, sem = pools(nc, ctx)
        stored = sem("x_stored")
        block = ctx.enter_context(nc.Block())

        @block.sync
        def _(sp):
            sp.dma_start(out[:, 0:TILES // 2, :], X[:, 0:TILES // 2, :]).then_inc(stored, 16)
            sp.wait_ge(stored, 32)

        @block.scalar
        def _(act):
            act.dma_start(out[:, TILES // 2:, :], X[:, TILES // 2:, :]).then_inc(stored, 16)


def network(nc, w, consts, decay_dram, out):
    with ExitStack() as ctx:
        sb, ps, sem = pools(nc, ctx)
        X = sb("X", [P, TILES, D])
        XT = sb("XT", [P, KC, N])
        ident = sb("ident", [P, P])
        as_tiles = "b (c p) d -> p (b c) d"
        load_block(nc, X, w["L0_attn_hidden_states"].rearrange(as_tiles, p=P), ident, consts["ident"])
        norm_block(nc, "n0_", X, XT, ident, 1e-5)
        with ExitStack() as part:
            beta = part.enter_context(nc.sbuf_tensor("beta", [P, H, TILES], F32))
            decay_block(nc, XT, beta, decay_dram, w)
            delta_block(nc, X, XT, beta, ident, decay_dram, w, consts)
        if STAGES >= 2:
            norm_block(nc, "n1_", X, XT, ident, 1e-5)
            with ExitStack() as part:
                weights = part.enter_context(nc.sbuf_tensor("e0_weights", [P, E0 + 1, TILES], F32))
                score = part.enter_context(nc.sbuf_tensor("score", [P, TILES], F32))
                XS = part.enter_context(nc.sbuf_tensor("XS", [P, KC, N], F32))
                router_block(nc, "r0_", XT, w["L0_ffn_router_w"], E0, consts["rank0"], weights, score)
                norm_block(nc, "n2_", X, XS, ident, 1e-5, scale_by=score)
                experts_block(nc, "e0_", X, [(0, E0, XS), (E0, 1, XT)], weights,
                              w["L0_ffn_gate_up"], w["L0_ffn_down"], F0 - P)
        clear_block(nc)
        if STAGES >= 3:
            norm_block(nc, "n3_", X, XT, ident, 1e-5)
            alibi_block(nc, X, XT, ident, w, consts)
        if STAGES >= 4:
            with ExitStack() as part:
                HID = part.enter_context(nc.sbuf_tensor("HID", [P, TILES, D], F32))
                last_part(nc, X, HID, XT, ident, w, consts)
        store_block(nc, X, out.rearrange(as_tiles, p=P))


def constants():
    p = np.arange(P)
    level = np.zeros((P, LEVELS, 4, HALF), np.float32)
    for l in range(LEVELS):
        s = 1 << l
        u = np.arange(HALF)
        level[:, l, :, :] = (((p[:, None] // s) % 2 == 0) & (p[:, None] // (2 * s) == u[None, :] // s))[:, None, :]
    dist = np.abs(np.arange(2 * T - P)[None, :] - (T - P) - p[:, None]).astype(np.float32)

    spread = (p[:, None] == SLOT * (p[None, :] // SLOT) + DA).astype(np.float32)

    def rank(E):
        return np.ascontiguousarray(np.broadcast_to((E - np.arange(E)).astype(np.float32), (P, TILES, E)))

    return {
        "ident": np.eye(P, dtype=np.float32),
        "level_mask": level.reshape(P, LEVELS, 4 * HALF),
        "dist": dist,
        "spread": spread,
        "causal": np.where(np.arange(T)[None, :] - (T - P) <= p[:, None], 0.0, -NEG).astype(np.float32),
        "rank0": rank(E0),
        "rank1": rank(E1),
    }


def packed(gate, up):
    if gate.shape[2] == 2 * P:
        return np.concatenate([gate, up], axis=2)
    second = gate.shape[2] - P
    pad = np.zeros(gate.shape[:2] + (HALF - second,), gate.dtype)
    return np.concatenate([gate[:, :, :P], up[:, :, :P], up[:, :, P:], pad, gate[:, :, P:]], axis=2)


def layouts(x):
    out = {k: x[k] for k in (
        "L0_attn_hidden_states", "L0_attn_Wq", "L0_attn_Wk", "L0_attn_Wv", "L0_attn_conv_q", "L0_attn_conv_k",
        "L0_attn_conv_v", "L0_attn_Wf1", "L0_attn_Wf2", "L0_attn_Wb", "L0_attn_A_log", "L0_attn_dt_bias",
        "L0_attn_Wg", "L0_attn_bg", "L0_attn_norm_w", "L0_attn_Wo", "L0_ffn_router_w", "L1_attn_bv", "L1_attn_bo", "L1_attn_slopes", "L1_ffn_ln1_w", "L1_ffn_ln2_w")}
    gate, up, down = (np.concatenate([x[f"L0_ffn_{part}_w"], x[f"L0_ffn_shared_{part}_w"][None]])
                      for part in ("gate", "up", "down"))
    out["L0_ffn_gate_up"], out["L0_ffn_down"] = packed(gate, up), down
    out["L1_attn_WvT"] = x["L1_attn_Wv"].T
    for m in ("Wq", "Wk", "Wo"):
        wide = np.zeros((D, H, SLOT), x[f"L1_attn_{m}"].dtype)
        wide[:, :, :DA] = (x["L1_attn_Wo"] if m == "Wo" else x[f"L1_attn_{m}"].T).reshape(D, H, DA)
        wide = wide.reshape(D, H * SLOT)
        out[f"L1_attn_{m}T"] = wide.T if m == "Wo" else wide
    for m in ("bq", "bk"):
        wide = np.zeros((H, SLOT), x[f"L1_attn_{m}"].dtype)
        wide[:, :DA] = x[f"L1_attn_{m}"].reshape(H, DA)
        out[f"L1_attn_{m}"] = wide.reshape(-1, P).T
    for m in ("q_w", "kv_w", "o_w", "gate_w"):
        out[f"L1_ffn_{m}T"] = x[f"L1_ffn_{m}"].T
    w1 = x["L1_ffn_w1"].reshape(E1, 2, I1, D)
    sh = x["L1_ffn_sh_gu_w"].reshape(2, NSH, I1, D)
    gate, up = (np.concatenate([w1[:, n], sh[n]]).transpose(0, 2, 1) for n in range(2))
    out["L1_ffn_gate_up"] = packed(gate, up)
    down = x["L1_ffn_sh_down_w"].reshape(D, NSH, I1).transpose(1, 2, 0)
    out["L1_ffn_down"] = np.concatenate([x["L1_ffn_w2"].transpose(0, 2, 1), down])
    return {k: np.ascontiguousarray(v) for k, v in out.items()}


def kernel(**inputs):
    import concourse.bacc as _bacc
    from concourse.bass_utils import run_bass_kernel_spmd as _run

    nc = _bacc.Bacc("TRN2", target_bir_lowering=False, num_devices=1)
    arrays = {}

    def dram(name, a):
        arrays[name] = a
        return nc.dram_tensor(name, a.shape, mybir.dt.from_np(a.dtype), kind="ExternalInput").ap()

    x = {k: np.asarray(v) for k, v in inputs.items()}
    w = {k: dram("in_" + k, v) for k, v in layouts(x).items()}
    consts = {k: dram("const_" + k, v) for k, v in constants().items()}
    decay_dram = nc.dram_tensor("decay", (LEVELS + 2, P, N), F32, kind="Internal").ap()
    out = nc.dram_tensor("out_0_dram", (B, T, D), F32, kind="ExternalOutput").ap()
    network(nc, w, consts, decay_dram, out)
    r = _run(nc, [arrays], core_ids=[0])
    return r.results[0]["out_0_dram"]
```

```python
from contextlib import ExitStack

import numpy as np

import concourse.bass as bass
from concourse import mybir

P = 128
F32 = mybir.dt.float32
BF16 = mybir.dt.bfloat16
I32 = mybir.dt.int32
ALU = mybir.AluOpType
ACT = mybir.ActivationFunctionType
AX_X = mybir.AxisListType.X

B, T, D = 4, 512, 256
N = B * T
TILES = N // P
TPB = T // P
KC = D // P
H = 16
BANK = 512
DH = 128
NG = 8
TAPS = 4
LEVELS = 7
HALF = P // 2
E0, F0 = 8, 256
E1, I1, TOPK, NSH = 16, 176, 4, 2
DA = D // H
SLOT = 32
NOPE, ROPE, VD = 128, 64, 128
QHD = NOPE + ROPE
NEG = -1.0e30


def pools(nc, ctx):
    def sb(name, shape, dt=F32):
        return ctx.enter_context(nc.sbuf_tensor(name, shape, dt))

    def ps(name, shape):
        return ctx.enter_context(nc.psum_tensor(name, shape, F32))

    def sem(name):
        return ctx.enter_context(nc.semaphore(name))

    return sb, ps, sem


def rows(ap, n=P):
    return ap.unsqueeze(0).broadcast_to([n, ap.shape[0]])


def load_block(nc, X, x_in, ident, ident_in):
    with ExitStack() as ctx:
        sb, ps, sem = pools(nc, ctx)
        loaded = sem("x_loaded")
        block = ctx.enter_context(nc.Block())

        @block.sync
        def _(sp):
            sp.dma_start(X[:, 0:TILES // 2, :], x_in[:, 0:TILES // 2, :]).then_inc(loaded, 16)
            sp.dma_start(ident[:, :], ident_in).then_inc(loaded, 16)
            sp.wait_ge(loaded, 48)

        @block.scalar
        def _(act):
            act.dma_start(X[:, TILES // 2:, :], x_in[:, TILES // 2:, :]).then_inc(loaded, 16)


def norm_block(nc, tag, X, XT, ident, eps, rms_weight=None, scale_by=None, kept=None, rows_out=None, rms_eps=None):
    rms = rms_weight is not None
    DEPTH = 4
    with ExitStack() as ctx:
        sb, ps, sem = pools(nc, ctx)
        stats = sb(tag + "stats", [P, TILES, 6])
        mv = sb(tag + "mv", [P, TILES, 2])
        var = sb(tag + "var", [P, TILES])
        std = sb(tag + "std", [P, TILES])
        scale = sb(tag + "scale", [P, TILES])
        shift = sb(tag + "shift", [P, TILES])
        scale_x = sb(tag + "scale_x", [P, TILES])
        shift_x = sb(tag + "shift_x", [P, TILES])
        if kept is not None:
            scale, shift = kept
        weight = sb(tag + "weight", [P, KC])
        xn = [sb(f"{tag}xn{j}", [P, D]) for j in range(DEPTH)]
        bank = [ps(f"{tag}bank{j}", [P, KC, P]) for j in range(DEPTH)]
        step = sem(tag + "step")
        var_ready = sem(tag + "var_ready")
        std_ready = sem(tag + "std_ready")
        rows_ready = sem(tag + "rows_ready")
        scale_ready = sem(tag + "scale_ready")
        xn_ready = sem(tag + "xn_ready")
        turned = sem(tag + "turned")
        drained = sem(tag + "drained")
        w_loaded = sem(tag + "w_loaded")
        block = ctx.enter_context(nc.Block())
        own = rows_out is not None or scale_by is not None
        f_scale, f_shift = (scale_x, shift_x) if own else (scale, shift)

        @block.sync
        def _(sp):
            if rms:
                sp.dma_start(weight[:, :], rms_weight.rearrange("(c p) -> p c", p=P),
                             allow_slow_non_contiguous=True).then_inc(w_loaded, 16)
                sp.wait_ge(w_loaded, 16)

        @block.vector
        def _(dve):
            n = [0]

            def then(ins):
                n[0] += 1
                ins.then_inc(step, 1)
                dve.wait_ge(step, n[0])

            if scale_by is not None:
                nc.vector.tensor_tensor(scale_x[:, :], scale[:, :], scale_by[:, :], ALU.mult)
                nc.vector.tensor_tensor(shift_x[:, :], shift[:, :], scale_by[:, :], ALU.mult).then_inc(scale_ready, 1)
            else:
                for t in range(TILES):
                    nc.vector.bn_stats(stats[:, t, :], X[:, t, :]).then_inc(step, 1)
                for t in range(TILES):
                    dve.wait_ge(step, t + 1)
                    nc.vector.bn_aggr(mv[:, t, :], stats[:, t, :]).then_inc(step, 1)
                n[0] = 2 * TILES
                dve.wait_ge(step, n[0])
                if rms and rows_out is None:
                    then(nc.vector.tensor_tensor(shift[:, :], mv[:, :, 0], mv[:, :, 0], ALU.mult))
                    nc.vector.scalar_tensor_tensor(var[:, :], mv[:, :, 1], eps, shift[:, :],
                                                   ALU.add, ALU.add).then_inc(var_ready, 1)
                else:
                    nc.vector.tensor_scalar(var[:, :], mv[:, :, 1], eps, None, ALU.add).then_inc(var_ready, 1)
                dve.wait_ge(std_ready, 1)
                then(nc.vector.reciprocal(scale[:, :], std[:, :]))
                nc.vector.scalar_tensor_tensor(shift[:, :], mv[:, :, 0], 0.0 if rms and rows_out is None else -1.0,
                                               scale[:, :], ALU.mult, ALU.mult
                                               ).then_inc(rows_ready if rows_out is not None else scale_ready, 1)
                if rows_out is not None:
                    then(nc.vector.tensor_tensor(scale_x[:, :], mv[:, :, 1], scale[:, :], ALU.mult))
                    then(nc.vector.tensor_tensor(scale_x[:, :], scale_x[:, :], scale[:, :], ALU.mult))
                    nc.vector.tensor_scalar(var[:, :], scale_x[:, :], rms_eps, None, ALU.add).then_inc(var_ready, 1)
                    dve.wait_ge(std_ready, 2)
                    then(nc.vector.reciprocal(var[:, :], std[:, :]))
                    nc.vector.tensor_tensor(scale_x[:, :], scale[:, :], var[:, :], ALU.mult)
                    dve.wait_ge(rows_ready, 1)
                    nc.vector.tensor_tensor(shift_x[:, :], shift[:, :], var[:, :], ALU.mult).then_inc(scale_ready, 1)
            if rms:
                dve.wait_ge(w_loaded, 16)
            nc.vector.sem_inc(drained, DEPTH)
            with dve.Fori(0, TILES // DEPTH) as i:
                for j in range(DEPTH):
                    dve.wait_ge(turned, DEPTH * i + j + 1)
                    t = DEPTH * i + j
                    if rms:
                        for c in range(KC):
                            last = nc.vector.tensor_scalar(XT[:, c, bass.ds(t * P, P)], bank[j][:, c, :],
                                                           weight[:, c:c + 1], None, ALU.mult)
                    else:
                        last = nc.vector.tensor_copy(XT[:, :, bass.ds(t * P, P)], bank[j][:, :, :])
                    last.then_inc(drained, 1)

        @block.gpsimd
        def _(pool):
            if rows_out is None:
                return
            pool.wait_ge(rows_ready, 1)
            for t in range(TILES):
                nc.gpsimd.tensor_scalar(rows_out[:, t, :], X[:, t, :], scale[:, t:t + 1], shift[:, t:t + 1],
                                        ALU.mult, ALU.add)

        @block.scalar
        def _(act):
            if scale_by is None:
                for k in range(1 if rows_out is None else 2):
                    act.wait_ge(var_ready, k + 1)
                    nc.scalar.activation(std[:, :], var[:, :], ACT.Sqrt).then_inc(std_ready, 1)
            act.wait_ge(scale_ready, 1)
            with act.Fori(0, TILES // DEPTH) as i:
                for j in range(DEPTH):
                    t = DEPTH * i + j
                    act.wait_ge(drained, DEPTH * i + j + 1)
                    nc.scalar.activation(xn[j][:, :], X[:, bass.ds(t, 1), :].rearrange("p a d -> p (a d)"),
                                         ACT.Identity, bias=f_shift[:, bass.ds(t, 1)],
                                         scale=f_scale[:, bass.ds(t, 1)]).then_inc(xn_ready, 1)

        @block.tensor
        def _(pe):
            with pe.Fori(0, TILES // DEPTH) as i:
                for j in range(DEPTH):
                    pe.wait_ge(drained, DEPTH * i + j + 1)
                    pe.wait_ge(xn_ready, DEPTH * i + j + 1)
                    for c in range(KC):
                        last = nc.tensor.transpose(bank[j][:, c, :], xn[j][:, c * P:(c + 1) * P], ident[:, :])
                    last.then_inc(turned, 1)


def decay_block(nc, XT, beta, decay_dram, w):
    with ExitStack() as ctx:
        sb, ps, sem = pools(nc, ctx)
        wf1 = sb("wf1", [P, KC, P])
        wf2 = sb("wf2", [P, P])
        wb = sb("wb", [P, KC, H])
        dtb = sb("dtb", [P, 1])
        alog = sb("alog", [P, 1])
        rate = sb("rate", [P, 1])
        nrate = sb("nrate", [P, 1])
        FT = sb("FT", [P, N])
        z = sb("z", [P, N])
        u = sb("u", [P, N])
        lg = sb("lg", [P, N])
        pol = sb("pol", [P, N])
        pref = sb("pref", [P, N])
        suf = sb("suf", [P, N])
        lev = [sb(f"lev{j}", [P, N]) for j in range(2)]
        acc = ps("dacc", [P, B, T])
        acc_b = ps("dacc_b", [P, TILES, H])
        loaded = sem("d_loaded")
        f_mm = sem("d_f_mm")
        f_sb = sem("d_f_sb")
        g_mm = sem("d_g_mm")
        b_mm = sem("d_b_mm")
        z_ready = sem("d_z")
        act_step = sem("d_act")
        dve_step = sem("d_dve")
        a_ready = sem("d_a")
        lev_ready = sem("d_lev")
        stored = [sem(f"d_stored{j}") for j in range(2)]
        rate_ready = sem("d_rate")
        ones_set = sem("d_ones_set")
        n_loads = 5
        block = ctx.enter_context(nc.Block())

        @block.gpsimd
        def _(pool):
            nc.gpsimd.memset(suf[:, :], 1.0).then_inc(ones_set, 1)

        @block.sync
        def _(sp):
            sp.dma_start(wf1[:, :, :], w["L0_attn_Wf1"].rearrange("(c p) n -> p c n", p=P)).then_inc(loaded, 16)
            sp.dma_start(wf2[:, :], w["L0_attn_Wf2"]).then_inc(loaded, 16)
            sp.dma_start(wb[:, :, :], w["L0_attn_Wb"].rearrange("(c p) n -> p c n", p=P)).then_inc(loaded, 16)
            sp.dma_start(dtb[:, :], w["L0_attn_dt_bias"].unsqueeze(1)).then_inc(loaded, 16)
            sp.dma_start(alog[:, :], w["L0_attn_A_log"].unsqueeze(1).broadcast_to([H, NG]).unsqueeze(2)
                         ).then_inc(loaded, 16)
            for k in range(LEVELS):
                sp.wait_ge(lev_ready, k + 1)
                sp.dma_start(decay_dram[k], lev[k % 2][:, :]).then_inc(stored[k % 2], 16)
            sp.wait_ge(lev_ready, LEVELS + 1)
            sp.dma_start(decay_dram[LEVELS], pref[:, :]).then_inc(stored[LEVELS % 2], 16)
            sp.dma_start(decay_dram[LEVELS + 1], suf[:, :]).then_inc(stored[(LEVELS + 1) % 2], 16)
            for j in range(2):
                sp.wait_ge(stored[j], 16 * len(range(j, LEVELS + 2, 2)))

        @block.tensor
        def _(pe):
            pe.wait_ge(loaded, 16 * n_loads)
            for b in range(B):
                for c in range(KC):
                    last = nc.tensor.matmul(acc[:, b, :], wf1[:, c, :], XT[:, c, b * T:(b + 1) * T],
                                            start=(c == 0), stop=(c == KC - 1))
                last.then_inc(f_mm, 1)
            for b in range(B):
                pe.wait_ge(f_sb, b + 1)
                nc.tensor.matmul(acc[:, b, :], wf2[:, :], FT[:, b * T:(b + 1) * T],
                                 start=True, stop=True).then_inc(g_mm, 1)
            for t in range(TILES):
                for c in range(KC):
                    last = nc.tensor.matmul(acc_b[:, t, :], XT[:, c, t * P:(t + 1) * P], wb[:, c, :],
                                            start=(c == 0), stop=(c == KC - 1))
            last.then_inc(b_mm, 1)

        @block.scalar
        def _(act):
            for b in range(B):
                act.wait_ge(f_mm, b + 1)
                nc.scalar.activation(FT[:, b * T:(b + 1) * T], acc[:, b, :], ACT.Copy).then_inc(f_sb, 1)
            act.wait_ge(loaded, 16 * n_loads)
            nc.scalar.activation(rate[:, :], alog[:, :], ACT.Exp).then_inc(rate_ready, 1)
            act.wait_ge(z_ready, 1)
            nc.scalar.activation(lg[:, :], z[:, :], ACT.Abs).then_inc(act_step, 1)
            act.wait_ge(act_step, 1)
            nc.scalar.activation(u[:, :], lg[:, :], ACT.Exp, scale=-1.0).then_inc(act_step, 1)
            act.wait_ge(act_step, 2)
            nc.scalar.activation(lg[:, :], u[:, :], ACT.Ln, bias=1.0).then_inc(act_step, 1)
            act.wait_ge(a_ready, 1)
            nc.scalar.activation(pref[:, :], z[:, :], ACT.Exp, scale=nrate[:, 0:1]).then_inc(act_step, 1)
            act.wait_ge(b_mm, 1)
            nc.scalar.activation(beta[:, :, :].rearrange("p h t -> p t h"), acc_b[:, :, :],
                                 ACT.Sigmoid).then_inc(act_step, 1)

        @block.vector
        def _(dve):
            n = [0]

            def then(ins):
                n[0] += 1
                ins.then_inc(dve_step, 1)
                dve.wait_ge(dve_step, n[0])

            dve.wait_ge(loaded, 16 * n_loads)
            for b in range(B):
                dve.wait_ge(g_mm, b + 1)
                last = nc.vector.tensor_scalar(z[:, b * T:(b + 1) * T], acc[:, b, :], dtb[:, 0:1], None, ALU.add)
            last.then_inc(z_ready, 1)
            dve.wait_ge(rate_ready, 1)
            then(nc.vector.tensor_scalar(nrate[:, :], rate[:, :], -1.0, None, ALU.mult))
            dve.wait_ge(act_step, 3)
            then(nc.vector.tensor_scalar(pol[:, :], u[:, :], 1.0 / 5, None, ALU.mult))
            for k in (4, 3, 2, 1):
                then(nc.vector.scalar_tensor_tensor(pol[:, :], pol[:, :], (1.0 if k % 2 else -1.0) / k, u[:, :],
                                                    ALU.add, ALU.mult))
            then(nc.vector.tensor_scalar(lev[0][:, :], u[:, :], 0.03, None, ALU.is_lt))
            then(nc.vector.copy_predicated(lg[:, :], lev[0][:, :].bitcast(I32), pol[:, :]))
            nc.vector.scalar_tensor_tensor(z[:, :], z[:, :], 0.0, lg[:, :], ALU.max, ALU.add).then_inc(a_ready, 1)
            dve.wait_ge(ones_set, 1)
            dve.wait_ge(act_step, 4)
            for k in range(LEVELS):
                s = 1 << k
                pv = pref[:, :].rearrange("p (n two s) -> p n two s", two=2, s=s)
                sv = suf[:, :].rearrange("p (n two s) -> p n two s", two=2, s=s)
                lv = lev[k % 2][:, :].rearrange("p (n two s) -> p n two s", two=2, s=s)
                nb = N // (2 * s)
                if k >= 2:
                    dve.wait_ge(stored[k % 2], 16 * (k // 2))
                nc.vector.tensor_copy(lv[:, :, 1, :], pv[:, :, 1, :])
                nc.vector.tensor_copy(lv[:, :, 0, :], sv[:, :, 0, :]).then_inc(lev_ready, 1)
                dve.wait_ge(lev_ready, k + 1)
                then(nc.vector.tensor_tensor(sv[:, :, 0, :], sv[:, :, 0, :],
                                             pv[:, :, 1, s - 1:s].broadcast_to([P, nb, s]), ALU.mult))
                then(nc.vector.tensor_tensor(pv[:, :, 1, :], pv[:, :, 1, :],
                                             pv[:, :, 0, s - 1:s].broadcast_to([P, nb, s]), ALU.mult))
            nc.vector.sem_inc(lev_ready, 1)


def delta_block(nc, X, XT, beta, ident, decay_dram, w, consts):
    PRE = 3 * B
    NL = LEVELS + 2
    PAIRS = B * LEVELS
    UQ = B + PAIRS + (TPB - 1)
    UY = PAIRS + (TPB - 1)
    UDD = PAIRS + TPB
    UDW = UDD - B
    UT = B + PAIRS + TPB
    UZ = B + TPB
    LOWER, UPPER = slice(0, HALF), slice(HALF, P)
    V_STEPS = (12, 16, 20, 24)

    def units(more):
        order = [("gate", b) for b in range(TPB)] + [("vt", b) for b in range(B)]
        if more:
            order += [("proj", b) for b in range(B)]
        order += [("kt", b) for b in range(B)]
        for c in range(TPB):
            if c >= 2:
                order += [("out", 2 * (c - 2)), ("out", 2 * (c - 2) + 1)]
            if more:
                order += [("proj", B + 2 * c), ("proj", B + 2 * c + 1)]
        order += [("out", n) for n in range(2 * TPB - 4, 2 * TPB)]
        return {x: n for n, x in enumerate(order)}

    UP = len(units(True))
    assert UP % 2 == 0 and PRE % 2 == 0
    with ExitStack() as ctx:
        sb, ps, sem = pools(nc, ctx)
        W = sb("W", [P, 4, KC, DH])
        cw = sb("cw", [P, 3, TAPS])
        nw = sb("nw", [P, 1])
        bg = sb("bg", [P, DH])
        wo = sb("wo", [P, D])
        qkv = [sb(nm, [P, N]) for nm in ("VT", "QT", "KT")]
        VT, QT, KT = qkv
        gate = sb("gate", [P, TILES, DH])
        bv = sb("bv", [P, TILES, DH])
        ktm = sb("ktm", [P, TILES, DH])
        dec = sb("dec", [P, 2, N])
        KQ = [sb(f"KQ{j}", [P, 2, N]) for j in range(2)]
        Bl = sb("Bl", [P, LEVELS, 2, 4, P])
        Tm = sb("Tm", [P, TILES, P])
        R = sb("R", [P, TILES, P])
        Aqk = sb("Aqk", [P, TILES, P])
        Ysb = sb("Ysb", [P, 2, 4, HALF])
        S = sb("S", [P, B, DH])
        U = sb("U", [P, B, DH])
        R1 = U
        y1 = sb("y1", [P, B, DH])
        yT = [sb(f"yT{j}", [P, B, DH]) for j in range(2)]
        ysq_junk = sb("ysq_junk", [P, DH])
        pend = sb("pend", [P, TILES])
        mhalf = sb("mhalf", [P, 2 * TILES])
        sq = sb("sq", [P, 2 * TILES])
        ss = sb("ss", [P, 2 * TILES])
        rr = sb("rr", [P, 2 * TILES])
        brk = sb("brk", [P, TILES])
        cc = sb("cc", [P, TILES])
        rq = sb("rq", [P, TILES])
        rq2 = sb("rq2", [P, TILES])
        ysum = sb("ysum", [P, B])
        yms = sb("yms", [P, B])
        yrs = sb("yrs", [P, B])
        yscale = sb("yscale", [P, TPB, B])
        mask = sb("mask", [P, LEVELS, 4 * HALF])
        bankP = [ps(f"bankP{j}", [P, BANK]) for j in range(2)]
        bankQ = [ps(f"bankQ{j}", [P, BANK]) for j in range(2)]
        bankY = ps("bankY", [P, BANK])
        bankD = ps("bankD", [P, BANK])
        bankT = ps("bankT", [P, BANK])
        bankZ = ps("bankZ", [P, BANK])
        P_written, P_drained = sem("P_written"), sem("P_drained")
        Q_written, Q_drained = sem("Q_written"), sem("Q_drained")
        Y_written, Y_drained = sem("Y_written"), sem("Y_drained")
        D_written, D_drained = sem("D_written"), sem("D_drained")
        T_written, T_drained = sem("T_written"), sem("T_drained")
        Z_written, Z_drained = sem("Z_written"), sem("Z_drained")
        const_loaded = sem("const_loaded")
        const_set = sem("const_set")
        w_loaded = sem("a_w_loaded")
        g_loaded = sem("g_loaded")
        wo_loaded = sem("wo_loaded")
        dec_loaded = [sem(f"dec_loaded{j}") for j in range(2)]
        tap_done = sem("tap_done")
        conv_step = sem("conv_step")
        silu_done = sem("silu_done")
        gate_done = sem("gate_done")
        eye_set = sem("eye_set")
        scaled = sem("scaled")
        ss_ready = sem("ss_ready")
        rr_ready = sem("rr_ready")
        rk_ready = sem("rk_ready")
        R1_ready = sem("R1_ready")
        S_ready = sem("S_ready")
        ysq_ready = sem("ysq_ready")
        yms_ready = sem("yms_ready")
        yms_step = sem("yms_step")
        yrs_ready = sem("yrs_ready")
        ysc_ready = sem("ysc_ready")
        sp_turn, pe_turn = sem("sp_turn"), sem("pe_turn")
        block = ctx.enter_context(nc.Block())

        def up(ap, s):
            return ap.rearrange("p (n two s) -> p n two s", two=2, s=s)[:, :, 1, :]

        def low(ap, s):
            return ap.rearrange("p (n two s) -> p n two s", two=2, s=s)[:, :, 0, :]

        def rows_of(l):
            return UPPER if l == LEVELS - 1 else slice(0, P)

        def flat(ap):
            return ap.rearrange("p a b -> p (a b)")

        def blocks(ap, s):
            return ap.rearrange("p (n s) -> p n s", s=s)

        def chunk_of(ap, c):
            return ap.rearrange("p (b c) n -> p c b n", c=TPB)[:, c, :, :]

        def stat_of(ap, c):
            return ap.rearrange("p (b c) -> p c b", c=TPB)[:, c, :]

        def heads(eng, body):
            with eng.Fori(0, H - 1) as h:
                body(h, True)
            body(H - 1, False)

        def norm_unit(which, b, h):
            n = (B * which + b) // 2
            if b % 2 == 0:
                return bankT, T_written, T_drained, UT * h + n
            return bankZ, Z_written, Z_drained, UZ * h + n

        def cut(h):
            return bass.ds(h * DH, DH) if not isinstance(h, int) else slice(h * DH, (h + 1) * DH)

        @block.sync
        def _(sp):
            sp.dma_start(mask[:, :, :], consts["level_mask"]).then_inc(const_loaded, 16)
            sp.dma_start(nw[:, :], w["L0_attn_norm_w"].unsqueeze(1)).then_inc(const_loaded, 16)

            def load_qkv(h):
                for k, (nm, cv) in enumerate((("Wv", "conv_v"), ("Wq", "conv_q"), ("Wk", "conv_k"))):
                    src = w["L0_attn_" + nm].rearrange("(c p) n -> p c n", p=P)
                    sp.dma_start(W[:, k, :, :], src[:, :, cut(h)]).then_inc(w_loaded, 16)
                    sp.dma_start(cw[:, k, :], w["L0_attn_" + cv][cut(h), :]).then_inc(w_loaded, 16)

            def load_gate(h):
                src = w["L0_attn_Wg"].rearrange("(c p) n -> p c n", p=P)
                sp.dma_start(W[:, 3, :, :], src[:, :, cut(h)]).then_inc(g_loaded, 16)
                sp.dma_start(bg[:, :], w["L0_attn_bg"].rearrange("(a n) -> a n", a=1)[:, cut(h)]
                             .broadcast_to([P, DH])).then_inc(g_loaded, 16)

            load_qkv(0)
            load_gate(0)
            sp.wait_ge(const_loaded, 32)

            def body(h, more):
                place = units(more)
                base = UP * h + PRE

                def load_decay(k):
                    sp.wait_ge(scaled, NL * h + max(k - 1, 0) + 1)
                    sp.sem_inc(sp_turn, 1)
                    rows_ = bass.ds(h * NG, NG) if more else slice(h * NG, (h + 1) * NG)
                    src = decay_dram[k][rows_, :].unsqueeze(1).broadcast_to([NG, P // NG, N])
                    sp.dma_start(dec[:, k % 2, :], src).then_inc(dec_loaded[k % 2], 16)

                load_decay(0)
                load_decay(1)
                sp.wait_ge(P_drained, base + 2)
                sp.sem_inc(sp_turn, 1)
                sp.dma_start(wo[:, :], w["L0_attn_Wo"][cut(h), :]).then_inc(wo_loaded, 16)
                if more:
                    load_qkv(h + 1)
                    sp.wait_ge(P_drained, base + place["gate", TPB - 1] + 1 + 2)
                    sp.sem_inc(sp_turn, 1)
                    load_gate(h + 1)
                for k in range(2, NL):
                    load_decay(k)
            heads(sp, body)

        @block.gpsimd
        def _(pool):
            nc.gpsimd.sem_inc(scaled, 1)
            nc.gpsimd.memset(mhalf[:, :], -0.5).then_inc(const_set, 1)
            nc.gpsimd.memset(Bl[:, :, :, :, :], 0.0).then_inc(const_set, 1)
            pool.wait_ge(const_set, 2)

            def body(h, more):
                place = units(more)
                base = UP * h + PRE

                def scale(k):
                    s = 1 << k
                    d = dec[:, k % 2, :]
                    per_head = len(range(k % 2, NL, 2))
                    pool.wait_ge(dec_loaded[k % 2], 16 * (per_head * h + k // 2 + 1))
                    if k < LEVELS:
                        if k >= 2:
                            pool.wait_ge(Q_written, UQ * h + B + B * (k - 1) + 1)
                        else:
                            pool.wait_ge(D_written, UDW * h + 1)
                        nc.gpsimd.tensor_tensor(KQ[k % 2][:, 0, :], KT[:, :], d, ALU.mult)
                        nc.gpsimd.tensor_tensor(up(KQ[k % 2][:, 1, :], s), up(QT[:, :], s), up(d, s),
                                                ALU.mult).then_inc(scaled, 1)
                    elif k == LEVELS:
                        pool.wait_ge(Q_written, UQ * h + B + B * (k - 1) + 1)
                        nc.gpsimd.tensor_tensor(KQ[1][:, 0, :], KT[:, :], d, ALU.mult)
                        nc.gpsimd.tensor_tensor(KQ[1][:, 1, :], QT[:, :], d, ALU.mult)
                        nc.gpsimd.tensor_copy(pend[:, :], d.rearrange("p (t n) -> p t n", n=P)[:, :, P - 1]
                                              ).then_inc(scaled, 1)
                    else:
                        pool.wait_ge(Q_written, UQ * h + B + PAIRS + 1)
                        nc.gpsimd.tensor_tensor(KQ[0][:, 0, :], KT[:, :], d, ALU.mult).then_inc(scaled, 1)

                pool.wait_ge(silu_done, 3 * B * (h + 1))
                scale(0)
                for which in range(2):
                    pool.wait_ge(ss_ready, 2 * h + which + 1)
                    v = slice(which * TILES, (which + 1) * TILES)
                    nc.gpsimd.tensor_tensor(rr[:, v], ss[:, v], mhalf[:, v], ALU.pow).then_inc(rr_ready, 1)
                    scale(1 + which)
                for k in range(3, NL):
                    scale(k)
                for c in range(TPB):
                    pool.wait_ge(yms_ready, TPB * h + c + 1)
                    nc.gpsimd.tensor_tensor(yrs[:, :], yms[:, :], mhalf[:, 0:B], ALU.pow).then_inc(yrs_ready, 1)
            heads(pool, body)

        @block.scalar
        def _(act):
            nc.scalar.sem_inc(T_drained, 1)
            nc.scalar.sem_inc(Z_drained, 1)
            act.wait_ge(const_loaded, 32)

            def tap(unit, n, g):
                k, b = divmod(n, B)
                act.wait_ge(P_written, unit + 1 + 1)
                nc.scalar.activation(qkv[k][:, b * T:(b + 1) * T], bankP[n % 2][:, :], ACT.Copy,
                                     scale=cw[:, k, TAPS - 1:TAPS]).then_inc(tap_done, 1)

            def silu(n, g):
                k, b = divmod(n, B)
                act.wait_ge(conv_step, 3 * (3 * B * g + n + 1))
                v = qkv[k][:, b * T:(b + 1) * T]
                nc.scalar.activation(v, v, ACT.Silu).then_inc(silu_done, 1)

            act.wait_ge(w_loaded, 96)
            for n in range(PRE):
                tap(n, n, 0)
                if n:
                    silu(n - 1, 0)
            silu(PRE - 1, 0)

            def body(h, more):
                place = units(more)
                base = UP * h + PRE
                act.wait_ge(P_drained, base + 2)
                for which in range(2):
                    for b in range(B):
                        bank, written, drained, n = norm_unit(which, b, h)
                        act.wait_ge(written, n + 1 + 1)
                        for i in range(4):
                            v = bank[:, i * P:(i + 1) * P]
                            t = which * TILES + 4 * b + i
                            last = nc.scalar.activation(v, v, ACT.Square, accum_out=sq[:, t:t + 1])
                        last.then_inc(drained, 1)
                    if which == 0:
                        nc.scalar.activation(Tm[:, :, :], ident[:, :].unsqueeze(1).broadcast_to([P, TILES, P]),
                                             ACT.Copy).then_inc(eye_set, 1)
                for b in range(TPB):
                    act.wait_ge(P_drained, base + place["gate", b] + 1 + 2)
                    v = gate[:, 4 * b:4 * b + 4, :]
                    nc.scalar.activation(v, v, ACT.Silu).then_inc(gate_done, 1)

                def take_turn(n):
                    l, b = divmod(n, B)
                    act.wait_ge(T_written, UT * h + B + n + 1 + 1)
                    if l == LEVELS - 1:
                        nc.scalar.activation(R[LOWER, 4 * b:4 * b + 4, UPPER],
                                             bankT[LOWER, 0:4 * HALF].rearrange("p (i n) -> p i n", n=HALF),
                                             ACT.Copy).then_inc(T_drained, 1)
                        return
                    nc.scalar.activation(flat(R[:, 4 * b:4 * b + 4, :]), bankT[:, :], ACT.Copy).then_inc(T_drained, 1)

                for n in range(PAIRS + 3):
                    if more and n in V_STEPS:
                        i = V_STEPS.index(n)
                        if i == 0:
                            act.wait_ge(w_loaded, 96 * (h + 2))
                        tap(base + place["proj", i], i, h + 1)
                    if more and n - 2 in V_STEPS:
                        silu(V_STEPS.index(n - 2), h + 1)
                    if n >= 3:
                        take_turn(n - 3)
                act.wait_ge(scaled, NL * (h + 1) + 1)

                def take_y(c):
                    act.wait_ge(Z_written, UZ * h + B + c + 1 + 1)
                    if c >= 2:
                        act.wait_ge(P_written, base + place["out", 2 * c - 3] + 1 + 1)
                    nc.scalar.activation(flat(yT[c % 2][:, :, :]), bankZ[:, :], ACT.Copy,
                                         scale=nw[:, 0:1]).then_inc(Z_drained, 1)

                def next_tap(i):
                    if more:
                        tap(base + place["proj", B + i], B + i, h + 1)

                def next_silu(i):
                    if more:
                        silu(B + i, h + 1)

                for c in range(TPB):
                    if c:
                        take_y(c - 1)
                    else:
                        next_tap(0)
                    act.wait_ge(T_written, UT * h + B + PAIRS + c + 1 + 1)
                    nc.scalar.activation(flat(U[:, :, :]), bankT[:, :], ACT.Copy,
                                         scale=-1.0 if c else 1.0).then_inc(T_drained, 1)
                    if c:
                        next_silu(2 * c - 1)
                    else:
                        next_tap(1)
                    act.wait_ge(D_drained, UDD * h + PAIRS + c + 1 + 1)
                    act.wait_ge(yms_step, TPB * h + c + 1)
                    for b in range(B):
                        if b:
                            act.wait_ge(ysq_ready, B * (TPB * h + c) + b)
                        nc.scalar.activation(ysq_junk[:, :], y1[:, b, :], ACT.Square,
                                             accum_out=ysum[:, b:b + 1]).then_inc(ysq_ready, 1)
                    if c:
                        next_tap(2 * c)
                        next_tap(2 * c + 1)
                    if c < TPB - 1:
                        next_silu(2 * c)
                take_y(TPB - 1)
                next_silu(2 * TPB - 2)
                next_silu(2 * TPB - 1)
            heads(act, body)

        @block.tensor
        def _(pe):
            for x in (P_written, Y_written, T_written, D_written, Q_written, Z_written):
                pe.sem_inc(x, 1)

            def mm(out, lhsT, rhs, first=True, last=True):
                return nc.tensor.matmul(out, lhsT, rhs, start=first, stop=last)

            def project(unit, n):
                k, b = divmod(n, B)
                pe.wait_ge(P_drained, unit + 1)
                for c in range(KC):
                    last = mm(bankP[n % 2][:, :], W[:, k, c, :], XT[:, c, b * T:(b + 1) * T], c == 0, c == KC - 1)
                last.then_inc(P_written, 1)

            pe.wait_ge(w_loaded, 96)
            for n in range(PRE):
                project(n, n)
            pe.wait_ge(const_set, 2)

            def body(h, more):
                place = units(more)
                base = UP * h + PRE
                pe.wait_ge(g_loaded, 32 * (h + 1))
                for b in range(B):
                    n = place["gate", b]
                    pe.wait_ge(P_drained, base + n + 1)
                    for i in range(4):
                        t = 4 * b + i
                        for c in range(KC):
                            last = mm(bankP[n % 2][:, i * DH:(i + 1) * DH], XT[:, c, t * P:(t + 1) * P],
                                      W[:, 3, c, :], c == 0, c == KC - 1)
                    last.then_inc(P_written, 1)
                    if b == 0:
                        pe.wait_ge(silu_done, 3 * B * (h + 1))
                    for m in (2 * b, 2 * b + 1):
                        which, s = divmod(m, B)
                        bank, written, drained, n = norm_unit(which, s, h)
                        pe.wait_ge(drained, n + 1)
                        for i in range(4):
                            t = 4 * s + i
                            last = nc.tensor.transpose(bank[:, i * P:(i + 1) * P],
                                                       (KT, QT)[which][:, t * P:(t + 1) * P], ident[:, :])
                        last.then_inc(written, 1)
                for b in range(B):
                    pe.wait_ge(Q_drained, UQ * h + max(b + 1, 2))
                    for i in range(4):
                        t = 4 * b + i
                        last = mm(bankQ[b % 2][:, i * P:(i + 1) * P], KT[:, t * P:(t + 1) * P], QT[:, t * P:(t + 1) * P])
                    last.then_inc(Q_written, 1)
                for b in range(B):
                    n = place["vt", b]
                    pe.wait_ge(P_drained, base + n + 1)
                    for i in range(4):
                        t = 4 * b + i
                        last = nc.tensor.transpose(bankP[n % 2][:, i * P:(i + 1) * P], VT[:, t * P:(t + 1) * P],
                                                   ident[:, :])
                    last.then_inc(P_written, 1)
                pe.wait_ge(eye_set, h + 1)

                def pairs(n):
                    l, b = divmod(n, B)
                    q, s = B + n, 1 << l
                    pe.wait_ge(scaled, NL * h + l + 1 + 1)
                    pe.wait_ge(Q_drained, UQ * h + q + 1)
                    for i in range(4):
                        t = 4 * b + i
                        kq = KQ[l % 2][:, :, t * P:(t + 1) * P]
                        last = mm(bankQ[q % 2][:, :].rearrange("p (two i n s) -> p i two n s", two=2, i=4, s=s)[:, i],
                                  kq[:, 0, :], kq.rearrange("p w (n two s) -> p w n two s", two=2, s=s)[:, :, :, 1, :])
                    last.then_inc(Q_written, 1)

                def merge_a(n):
                    l, b = divmod(n, B)
                    s = 1 << l
                    pe.wait_ge(Q_drained, UQ * h + B + n + 1 + 2)
                    pe.wait_ge(Y_drained, UY * h + n + 1)
                    if l:
                        pe.wait_ge(D_drained, UDD * h + n - B + 1 + 1)
                    if l == LEVELS - 1:
                        pe.sem_inc(pe_turn, 1)
                    for i in range(4):
                        t = 4 * b + i
                        if l == LEVELS - 1:
                            last = mm(bankY[UPPER, i * HALF:(i + 1) * HALF], Bl[LOWER, l, b % 2, i, UPPER],
                                      Tm[LOWER, t, LOWER])
                        elif l:
                            last = mm(blocks(bankY[:, i * HALF:(i + 1) * HALF], s), Bl[:, l, b % 2, i, :],
                                      low(Tm[:, t, :], s))
                        else:
                            last = nc.tensor.transpose(bankY[:, i * P:(i + 1) * P], Bl[:, l, b % 2, i, :],
                                                       ident[:, :])
                    last.then_inc(Y_written, 1)

                def merge_b(n):
                    l, b = divmod(n, B)
                    if l == 0:
                        return
                    pe.wait_ge(Y_drained, UY * h + n + 1 + 1)
                    pe.wait_ge(D_drained, UDD * h + n + 1)
                    pe.wait_ge(T_drained, UT * h + B + n - B + 1 + 1)
                    r = rows_of(l)
                    if l == LEVELS - 1:
                        pe.sem_inc(pe_turn, 1)
                    for i in range(4):
                        last = mm(bankD[r, i * HALF:(i + 1) * HALF], R[r, 4 * b + i, r], Ysb[r, b % 2, i, :])
                    last.then_inc(D_written, 1)

                def turn(n):
                    l, b = divmod(n, B)
                    pe.wait_ge(D_drained, UDD * h + n + 1 + 1)
                    pe.wait_ge(T_drained, UT * h + B + n + 1)
                    if l == LEVELS - 1:
                        pe.sem_inc(pe_turn, 1)
                    for i in range(4):
                        if l == LEVELS - 1:
                            last = nc.tensor.transpose(bankT[LOWER, i * HALF:(i + 1) * HALF],
                                                       Tm[UPPER, 4 * b + i, LOWER], ident[UPPER, UPPER])
                        else:
                            last = nc.tensor.transpose(bankT[:, i * P:(i + 1) * P], Tm[:, 4 * b + i, :], ident[:, :])
                    last.then_inc(T_written, 1)

                for n in range(PAIRS + 3):
                    if more and n in V_STEPS:
                        i = V_STEPS.index(n)
                        if i == 0:
                            pe.wait_ge(w_loaded, 96 * (h + 2))
                        project(base + place["proj", i], i)
                    for lag, part in enumerate((pairs, merge_a, merge_b, turn)):
                        if 0 <= n - lag < PAIRS:
                            part(n - lag)
                pe.wait_ge(scaled, NL * (h + 1) + 1)
                for b in range(B):
                    n = place["kt", b]
                    pe.wait_ge(P_drained, base + n + 1)
                    for i in range(4):
                        t = 4 * b + i
                        last = nc.tensor.transpose(bankP[n % 2][:, i * P:(i + 1) * P], KQ[0][:, 0, t * P:(t + 1) * P],
                                                   ident[:, :])
                    last.then_inc(P_written, 1)

                def y_turn(c):
                    pe.wait_ge(Z_drained, UZ * h + B + c + 1)
                    pe.wait_ge(D_drained, UDD * h + PAIRS + c + 1 + 1)
                    for b in range(B):
                        last = nc.tensor.transpose(bankZ[:, b * P:(b + 1) * P], y1[:, b, :], ident[:, :])
                    last.then_inc(Z_written, 1)

                def y_out(c, g):
                    if g == 0:
                        pe.wait_ge(Z_drained, UZ * h + B + c + 1 + 1)
                    n = place["out", 2 * c + g]
                    pe.wait_ge(P_drained, base + n + 1)
                    for i in range(2):
                        last = mm(bankP[n % 2][:, i * D:(i + 1) * D], yT[c % 2][:, 2 * g + i, :], wo[:, :])
                    last.then_inc(P_written, 1)

                pe.wait_ge(wo_loaded, 16 * (h + 1))
                for c in range(TPB):
                    tok = [slice((b * TPB + c) * P, (b * TPB + c + 1) * P) for b in range(B)]
                    if c:
                        pe.wait_ge(S_ready, (TPB - 1) * h + c)
                        pe.wait_ge(Y_drained, UY * h + PAIRS + c - 1 + 1)
                        for b in range(B):
                            last = mm(bankY[:, b * P:(b + 1) * P], KQ[1][:, 0, tok[b]], S[:, b, :])
                        last.then_inc(Y_written, 1)
                        y_turn(c - 1)
                    elif more:
                        project(base + place["proj", B], B)
                    if c >= 2:
                        y_out(c - 2, 0)
                    if c:
                        pe.wait_ge(R1_ready, (TPB - 1) * h + c)
                    else:
                        pe.wait_ge(P_drained, base + place["vt", B - 1] + 1 + 2)
                    pe.wait_ge(T_drained, UT * h + B + PAIRS + c + 1)
                    for b in range(B):
                        t = b * TPB + c
                        last = mm(bankT[:, b * P:(b + 1) * P], R[:, t, :], R1[:, b, :] if c else bv[:, t, :])
                    last.then_inc(T_written, 1)
                    if not c and more:
                        project(base + place["proj", B + 1], B + 1)
                    pe.wait_ge(T_drained, UT * h + B + PAIRS + c + 1 + 1)
                    pe.wait_ge(D_drained, UDD * h + PAIRS + c + 1)
                    for b in range(B):
                        t = b * TPB + c
                        if c:
                            mm(bankD[:, b * P:(b + 1) * P], KQ[1][:, 1, tok[b]], S[:, b, :], True, False)
                        last = mm(bankD[:, b * P:(b + 1) * P], Aqk[:, t, :], U[:, b, :], not c, True)
                    last.then_inc(D_written, 1)
                    if c < TPB - 1:
                        q = B + PAIRS + c
                        pe.wait_ge(Q_drained, UQ * h + q + 1)
                        pe.wait_ge(P_drained, base + place["kt", B - 1] + 1 + 2)
                        for b in range(B):
                            last = mm(bankQ[q % 2][:, b * P:(b + 1) * P], ktm[:, b * TPB + c, :], U[:, b, :])
                        last.then_inc(Q_written, 1)
                    if c >= 2:
                        y_out(c - 2, 1)
                    if c and more:
                        project(base + place["proj", B + 2 * c], B + 2 * c)
                        project(base + place["proj", B + 2 * c + 1], B + 2 * c + 1)
                y_turn(TPB - 1)
                y_out(TPB - 2, 0)
                y_out(TPB - 2, 1)
                y_out(TPB - 1, 0)
                y_out(TPB - 1, 1)
            heads(pe, body)

        @block.vector
        def _(dve):
            nc.vector.sem_inc(P_drained, 2)
            nc.vector.sem_inc(Q_drained, 2)
            nc.vector.sem_inc(Y_drained, 1)
            nc.vector.sem_inc(D_drained, 1)
            nc.vector.sem_inc(yms_step, 1)
            dve.wait_ge(const_loaded, 32)
            dve.wait_ge(const_set, 2)

            def conv(n, g):
                k, b = divmod(n, B)
                m = 3 * (3 * B * g + n)
                dve.wait_ge(tap_done, 3 * B * g + n + 1)
                for j in range(1, TAPS):
                    if j > 1:
                        dve.wait_ge(conv_step, m + j - 1)
                    v = qkv[k][:, b * T + j:(b + 1) * T]
                    nc.vector.scalar_tensor_tensor(v, bankP[n % 2][:, 0:T - j], cw[:, k, TAPS - 1 - j:TAPS - j], v,
                                                   ALU.mult, ALU.add).then_inc(conv_step, 1)
                dve.wait_ge(conv_step, m + 3)
                nc.vector.sem_inc(P_drained, 1)

            dve.wait_ge(w_loaded, 96)
            for n in range(PRE):
                conv(n, 0)

            def body(h, more):
                place = units(more)
                base = UP * h + PRE
                dve.wait_ge(g_loaded, 32 * (h + 1))
                def squares(which):
                    dve.wait_ge(T_drained, UT * h + B // 2 * (which + 1) + 1)
                    dve.wait_ge(Z_drained, UZ * h + B // 2 * (which + 1) + 1)
                    v = slice(which * TILES, (which + 1) * TILES)
                    nc.vector.tensor_scalar(ss[:, v], sq[:, v], 1e-6, None, ALU.add).then_inc(ss_ready, 1)

                for b in range(TPB):
                    if b == TPB - 1:
                        squares(0)
                    n = place["gate", b]
                    dve.wait_ge(P_written, base + n + 1 + 1)
                    nc.vector.tensor_tensor(gate[:, 4 * b:4 * b + 4, :],
                                            bankP[n % 2][:, :].rearrange("p (i n) -> p i n", n=DH),
                                            bg[:, :].unsqueeze(1).broadcast_to([P, 4, DH]),
                                            ALU.add).then_inc(P_drained, 1)
                squares(1)
                for b in range(B):
                    dve.wait_ge(Q_written, UQ * h + b + 1 + 1)
                    nc.vector.tensor_tensor(Aqk[:, 4 * b:4 * b + 4, :],
                                            bankQ[b % 2][:, :].rearrange("p (i n) -> p i n", n=P),
                                            ident[:, :].unsqueeze(1).broadcast_to([P, 4, P]),
                                            ALU.mult).then_inc(Q_drained, 1)
                dve.wait_ge(rr_ready, 2 * h + 1)
                rk = rr[:, 0:TILES]
                bt = beta[:, bass.ds(h, 1), :].rearrange("p a t -> p (a t)") if more else beta[:, h, :]
                nc.vector.tensor_tensor(brk[:, :], rk, bt, ALU.mult).then_inc(rk_ready, 1)
                dve.wait_ge(rk_ready, 4 * h + 1)
                nc.vector.tensor_tensor(cc[:, :], brk[:, :], rk, ALU.mult).then_inc(rk_ready, 1)
                dve.wait_ge(rk_ready, 4 * h + 2)
                for b in range(B):
                    n = place["vt", b]
                    dve.wait_ge(P_written, base + n + 1 + 1)
                    nc.vector.tensor_tensor(bv[:, 4 * b:4 * b + 4, :],
                                            bankP[n % 2][:, :].rearrange("p (i n) -> p i n", n=DH),
                                            brk[:, 4 * b:4 * b + 4].unsqueeze(2).broadcast_to([P, 4, DH]),
                                            ALU.mult).then_inc(P_drained, 1)
                dve.wait_ge(eye_set, h + 1)

                def take_pairs(n):
                    l, b = divmod(n, B)
                    q, s = B + n, 1 << l
                    dve.wait_ge(Q_written, UQ * h + q + 1 + 1)
                    if b >= 2:
                        dve.wait_ge(Y_written, UY * h + n - 2 + 1 + 1)
                    nc.vector.tensor_tensor(up(flat(Bl[:, l, b % 2, :, :]), s), blocks(bankQ[q % 2][:, 0:4 * HALF], s),
                                            blocks(mask[:, l, :], s), ALU.mult)
                    nc.vector.copy_predicated(up(flat(Aqk[:, 4 * b:4 * b + 4, :]), s),
                                              blocks(mask[:, l, :], s).bitcast(I32),
                                              blocks(bankQ[q % 2][:, 4 * HALF:8 * HALF], s)).then_inc(Q_drained, 1)

                def take_a(n):
                    l, b = divmod(n, B)
                    dve.wait_ge(Y_written, UY * h + n + 1 + 1)
                    if 2 <= n < B + 2:
                        dve.wait_ge(D_drained, UDD * h + n - 2 + 1 + 1)
                    r = rows_of(l)
                    if l:
                        a = bankY[r, 0:4 * HALF].rearrange("p (i n) -> p i n", n=HALF)
                    else:
                        a = bankY[:, :].rearrange("p (i n two) -> p i n two", i=4, two=2)[:, :, :, 0]
                    nc.vector.tensor_tensor(Ysb[r, b % 2, :, :], a,
                                            cc[r, 4 * b:4 * b + 4].unsqueeze(2)
                                            .broadcast_to([r.stop - r.start, 4, HALF]),
                                            ALU.mult).then_inc(Y_drained, 1)

                def take_b(n):
                    l, b = divmod(n, B)
                    s = 1 << l
                    r = rows_of(l)
                    v = low(flat(Tm[r, 4 * b:4 * b + 4, :]), s)
                    if l:
                        dve.wait_ge(D_written, UDW * h + n - B + 1 + 1)
                        a = blocks(bankD[r, 0:4 * HALF], s)
                    else:
                        dve.wait_ge(Y_drained, UY * h + n + 1 + 1)
                        a = blocks(flat(Ysb[:, b % 2, :, :]), s)
                    nc.vector.tensor_tensor(v, v, a, ALU.subtract).then_inc(D_drained, 1)

                for n in range(PAIRS + 2):
                    for lag, part in enumerate((take_pairs, take_a, take_b)):
                        if 0 <= n - lag < PAIRS:
                            part(n - lag)
                    if more and n in V_STEPS:
                        i = V_STEPS.index(n)
                        if i == 0:
                            dve.wait_ge(w_loaded, 96 * (h + 2))
                        conv(i, h + 1)
                for b in range(B):
                    n = place["kt", b]
                    dve.wait_ge(P_written, base + n + 1 + 1)
                    nc.vector.tensor_copy(flat(ktm[:, 4 * b:4 * b + 4, :]), bankP[n % 2][:, :]).then_inc(P_drained, 1)

                dve.wait_ge(rr_ready, 2 * h + 2)
                nc.vector.tensor_scalar(rq[:, :], rr[:, TILES:2 * TILES], float(DH) ** -0.5, None,
                                        ALU.mult).then_inc(rk_ready, 1)
                dve.wait_ge(rk_ready, 4 * h + 3)
                nc.vector.scalar_tensor_tensor(rq2[:, :], rq[:, :], 1.0 / DH, rq[:, :], ALU.mult,
                                               ALU.mult).then_inc(rk_ready, 1)
                dve.wait_ge(rk_ready, 4 * h + 4)

                def scale_out(c):
                    dve.wait_ge(yrs_ready, TPB * h + c + 1)
                    nc.vector.tensor_tensor(yscale[:, c, :], yrs[:, :], stat_of(rq[:, :], c),
                                            ALU.mult).then_inc(ysc_ready, 1)

                def add_out(c, g):
                    dve.wait_ge(ysc_ready, TPB * h + c + 1)
                    n = place["out", 2 * c + g]
                    dve.wait_ge(P_written, base + n + 1 + 1)
                    for i in range(2):
                        b = 2 * g + i
                        x = X[:, b * TPB + c, :]
                        last = nc.vector.scalar_tensor_tensor(x, bankP[n % 2][:, i * D:(i + 1) * D],
                                                              yscale[:, c, b:b + 1], x, ALU.mult, ALU.add)
                    last.then_inc(P_drained, 1)

                dve.wait_ge(gate_done, TPB * (h + 1))
                dve.wait_ge(scaled, NL * (h + 1) + 1)
                for c in range(TPB):
                    if c:
                        dve.wait_ge(Y_written, UY * h + PAIRS + c + 1)
                        for b in range(B):
                            t = b * TPB + c
                            last = nc.vector.scalar_tensor_tensor(R1[:, b, :], bankY[:, b * P:(b + 1) * P],
                                                                  cc[:, t:t + 1], bv[:, t, :],
                                                                  ALU.mult, ALU.subtract)
                        last.then_inc(R1_ready, 1)
                        dve.wait_ge(R1_ready, (TPB - 1) * h + c)
                        nc.vector.sem_inc(Y_drained, 1)
                        if more:
                            conv(B + 2 * c - 1, h + 1)
                        scale_out(c - 1)
                    elif more:
                        conv(B, h + 1)
                    if c >= 2:
                        add_out(c - 2, 0)
                    dve.wait_ge(D_written, UDW * h + PAIRS - B + c + 1 + 1)
                    if c:
                        dve.wait_ge(Z_written, UZ * h + B + c + 1)
                        dve.wait_ge(ysq_ready, B * (TPB * h + c))
                    nc.vector.tensor_tensor(y1[:, :, :], bankD[:, :].rearrange("p (b n) -> p b n", n=DH),
                                            chunk_of(gate[:, :, :], c), ALU.mult).then_inc(D_drained, 1)
                    if c < TPB - 1:
                        q = B + PAIRS + c
                        dve.wait_ge(Q_written, UQ * h + q + 1 + 1)
                        if c == 0:
                            nc.vector.tensor_copy(flat(S[:, :, :]), bankQ[q % 2][:, :]).then_inc(S_ready, 1)
                        else:
                            for b in range(B):
                                t = b * TPB + c
                                last = nc.vector.scalar_tensor_tensor(S[:, b, :], S[:, b, :], pend[:, t:t + 1],
                                                                      bankQ[q % 2][:, b * P:(b + 1) * P],
                                                                      ALU.mult, ALU.add)
                            last.then_inc(S_ready, 1)
                        dve.wait_ge(S_ready, (TPB - 1) * h + c + 1)
                        nc.vector.sem_inc(Q_drained, 1)
                    if c >= 2:
                        add_out(c - 2, 1)
                    if c and more:
                        conv(B + 2 * c, h + 1)
                    dve.wait_ge(ysq_ready, B * (TPB * h + c + 1))
                    nc.vector.tensor_tensor(yms[:, :], ysum[:, :], stat_of(rq2[:, :], c), ALU.mult).then_inc(yms_step, 1)
                    dve.wait_ge(yms_step, TPB * h + c + 1 + 1)
                    nc.vector.tensor_scalar(yms[:, :], yms[:, :], 1e-5, None, ALU.add).then_inc(yms_ready, 1)
                if more:
                    conv(B + 2 * TPB - 1, h + 1)
                scale_out(TPB - 1)
                for c in (TPB - 2, TPB - 1):
                    add_out(c, 0)
                    add_out(c, 1)
            heads(dve, body)


def pick_first_max(nc, link, left, picked, rank, E, tmp, mx):
    link(nc.vector.tensor_reduce(mx[:, :], left, AX_X, ALU.max))
    link(nc.vector.tensor_tensor(tmp, left, mx[:, :].unsqueeze(2).broadcast_to([P, TILES, E]), ALU.is_ge))
    link(nc.vector.tensor_tensor(tmp, tmp, rank, ALU.mult))
    link(nc.vector.tensor_reduce(mx[:, :], tmp, AX_X, ALU.max))
    link(nc.vector.tensor_tensor(picked, tmp, mx[:, :].unsqueeze(2).broadcast_to([P, TILES, E]), ALU.is_equal))


def router_block(nc, tag, XT, router, E, rank_in, weights, score=None):
    with ExitStack() as ctx:
        sb, ps, sem = pools(nc, ctx)
        rw = sb(tag + "rw", [P, KC, E])
        rank = sb(tag + "rank", [P, TILES, E])
        lg = sb(tag + "lg", [P, TILES, E])
        left = sb(tag + "left", [P, TILES, E])
        tmp = sb(tag + "tmp", [P, TILES, E])
        picked = sb(tag + "picked", [P, TILES, E])
        total = sb(tag + "total", [P, TILES, E])
        mx = sb(tag + "mx", [P, TILES])
        bank = ps(tag + "bank", [P, TILES, E])
        loaded = sem(tag + "loaded")
        logits = sem(tag + "logits")
        step = sem(tag + "step")
        for_act = sem(tag + "for_act")
        from_act = sem(tag + "from_act")
        block = ctx.enter_context(nc.Block())

        @block.sync
        def _(sp):
            sp.dma_start(rw[:, :, :], router.rearrange("(c p) n -> p c n", p=P)).then_inc(loaded, 16)
            sp.dma_start(rank[:, :, :], rank_in).then_inc(loaded, 16)
            sp.wait_ge(loaded, 32)

        @block.tensor
        def _(pe):
            pe.wait_ge(loaded, 32)
            for t in range(TILES):
                for c in range(KC):
                    last = nc.tensor.matmul(bank[:, t, :], XT[:, c, t * P:(t + 1) * P], rw[:, c, :],
                                            start=(c == 0), stop=(c == KC - 1))
            last.then_inc(logits, 1)

        @block.scalar
        def _(act):
            act.wait_ge(for_act, 1)
            if score is not None:
                nc.scalar.activation(score[:, :], mx[:, :], ACT.Sigmoid).then_inc(from_act, 1)
            else:
                nc.scalar.activation(lg[:, :, :], lg[:, :, :], ACT.Exp).then_inc(from_act, 1)

        @block.vector
        def _(dve):
            n = [0]

            def link(ins):
                n[0] += 1
                ins.then_inc(step, 1)
                dve.wait_ge(step, n[0])

            dve.wait_ge(loaded, 32)
            dve.wait_ge(logits, 1)
            link(nc.vector.tensor_copy(lg[:, :, :], bank[:, :, :]))
            link(nc.vector.tensor_reduce(mx[:, :], lg[:, :, :], AX_X, ALU.max))
            if score is not None:
                nc.vector.sem_inc(for_act, 1)
                dve.wait_ge(from_act, 1)
                pick_first_max(nc, link, lg[:, :, :], picked[:, :, :], rank[:, :, :], E, tmp[:, :, :], mx)
                link(nc.vector.tensor_copy(weights[:, 0:E, :].rearrange("p e t -> p t e"), picked[:, :, :]))
            else:
                link(nc.vector.tensor_tensor(lg[:, :, :], lg[:, :, :],
                                             mx[:, :].unsqueeze(2).broadcast_to([P, TILES, E]), ALU.subtract))
                nc.vector.sem_inc(for_act, 1)
                dve.wait_ge(from_act, 1)
                link(nc.vector.tensor_copy(left[:, :, :], lg[:, :, :]))
                link(nc.vector.memset(total[:, :, :], 0.0))
                for _ in range(TOPK):
                    pick_first_max(nc, link, left[:, :, :], picked[:, :, :], rank[:, :, :], E, tmp[:, :, :], mx)
                    link(nc.vector.tensor_tensor(total[:, :, :], total[:, :, :], picked[:, :, :], ALU.add))
                    link(nc.vector.scalar_tensor_tensor(left[:, :, :], picked[:, :, :], -4.0, left[:, :, :],
                                                        ALU.mult, ALU.add))
                link(nc.vector.tensor_tensor(lg[:, :, :], lg[:, :, :], total[:, :, :], ALU.mult))
                link(nc.vector.tensor_reduce(mx[:, :], lg[:, :, :], AX_X, ALU.add))
                link(nc.vector.reciprocal(mx[:, :], mx[:, :]))
                link(nc.vector.tensor_tensor(weights[:, 0:E, :].rearrange("p e t -> p t e"), lg[:, :, :],
                                             mx[:, :].unsqueeze(2).broadcast_to([P, TILES, E]), ALU.mult))
            link(nc.vector.memset(weights[:, E:, :], 1.0))


def experts_block(nc, tag, X, runs, weights, gate_up, down, second):
    FC = 2
    small = second <= HALF
    FEATURES = (P, second)
    WIDTH = gate_up.shape[2]
    with ExitStack() as ctx:
        sb, ps, sem = pools(nc, ctx)
        gu = [sb(f"{tag}gu{j}", [P, KC, WIDTH]) for j in range(2)]
        dn = [sb(f"{tag}dn{j}", [P, FC, D]) for j in range(2)]
        sg = [sb(f"{tag}sg{j}", [P, T]) for j in range(2)]
        hT = [sb(f"{tag}hT{j}", [P, FC, T]) for j in range(2)]
        bank_g = [ps(f"{tag}bank_g{j}", [P, T]) for j in range(2)]
        bank_u = [ps(f"{tag}bank_u{j}", [P, T]) for j in range(2)]
        bank_d = [ps(f"{tag}bank_d{j}", [P, 2, D]) for j in range(2)]
        loaded = [sem(f"{tag}loaded{j}") for j in range(2)]
        used = sem(tag + "used")
        sp_turn = sem(tag + "sp_turn")
        g_written, u_written = sem(tag + "g_written"), sem(tag + "u_written")
        silu_done = sem(tag + "silu_done")
        h_ready = sem(tag + "h_ready")
        d_written, d_drained = sem(tag + "d_written"), sem(tag + "d_drained")
        block = ctx.enter_context(nc.Block())
        UF = FC * B
        UU = B if small else UF
        LOADS = 16 * (1 + FC)
        UDN = 2 * B

        def over(eng, body):
            for first, count, xt in runs:
                if count >= 2:
                    assert count % 2 == 0 and first % 2 == 0
                    with eng.Fori(0, count // 2) as i:
                        for j in range(2):
                            body(2 * i + (first + j), j, i + first // 2, xt)
                else:
                    body(first, first % 2, first // 2, xt)

        @block.sync
        def _(sp):
            def body(e, j, pair, xt):
                sp.wait_ge(used, e + 1)
                sp.sem_inc(sp_turn, 1)
                src = gate_up[bass.ds(e, 1), :, :] if not isinstance(e, int) else gate_up[e:e + 1, :, :]
                sp.dma_start(gu[j][:, :, :], src.rearrange("e (c p) n -> p c (e n)", p=P)).then_inc(loaded[j], 16)
                src = down[bass.ds(e, 1), :, :] if not isinstance(e, int) else down[e:e + 1, :, :]
                for f, q in enumerate(FEATURES):
                    sp.dma_start(dn[j][0:q, f, :], src[:, f * P:f * P + q, :].rearrange("e q n -> q (e n)")
                                 ).then_inc(loaded[j], 16)
            over(sp, body)

        def products(f):
            if small and f:
                return [(slice(2 * P, WIDTH), bank_u, g_written)]
            g = slice(f * P, (f + 1) * P)
            u = slice((FC - small) * P + f * P, (FC - small) * P + (f + 1) * P)
            return [(g, bank_g, g_written), (u, bank_u, u_written)]

        @block.tensor
        def _(pe):
            pe.sem_inc(d_written, 1)

            def body(e, j, pair, xt):
                def up(b):
                    for f in range(FC):
                        n = FC * b + f
                        for cols, bank, written in products(f):
                            pe.wait_ge(h_ready, UF * e + n + 1)
                            for c in range(KC):
                                last = nc.tensor.matmul(bank[f][0:cols.stop - cols.start, :], gu[j][:, c, cols],
                                                        xt[:, c, b * T:(b + 1) * T],
                                                        start=(c == 0), stop=(c == KC - 1))
                            last.then_inc(written, 1)

                def down_b(b):
                    pe.wait_ge(h_ready, UF * e + FC * (b + 1) + 2)
                    for g in range(2):
                        pe.wait_ge(d_drained, UDN * e + 2 * b + g + 1)
                        for i in range(2):
                            t = 2 * g + i
                            for f in range(FC):
                                q = FEATURES[f]
                                last = nc.tensor.matmul(bank_d[g][:, i, :], hT[b % 2][0:q, f, t * P:(t + 1) * P],
                                                        dn[j][0:q, f, :], start=(f == 0), stop=(f == FC - 1))
                        last.then_inc(d_written, 1)

                pe.wait_ge(loaded[j], LOADS * (pair + 1))
                for b in range(B + 1):
                    if b < B:
                        up(b)
                    if b >= 1:
                        down_b(b - 1)
            over(pe, body)

        @block.scalar
        def _(act):
            def body(e, j, pair, xt):
                for n in range(UF):
                    f = n % FC
                    act.wait_ge(g_written, UF * e + n + 1)
                    act.wait_ge(h_ready, UF * e + n + 1)
                    q = FEATURES[f]
                    src = bank_u[f][HALF:HALF + q, :] if small and f else bank_g[f][0:q, :]
                    nc.scalar.activation(sg[f][0:q, :], src, ACT.Silu).then_inc(silu_done, 1)
            over(act, body)

        @block.vector
        def _(dve):
            nc.vector.sem_inc(used, 2)
            nc.vector.sem_inc(h_ready, 2)
            nc.vector.sem_inc(d_drained, 2)

            def body(e, j, pair, xt):
                def take_down(b):
                    for g in range(2):
                        dve.wait_ge(d_written, 1 + UDN * e + 2 * b + g + 1)
                        for i in range(2):
                            t = 4 * b + 2 * g + i
                            wt = weights[:, e, t:t + 1] if isinstance(e, int) else \
                                weights[:, bass.ds(e, 1), t:t + 1].rearrange("p a b -> p (a b)")
                            last = nc.vector.scalar_tensor_tensor(X[:, t, :], bank_d[g][:, i, :], wt, X[:, t, :],
                                                                  ALU.mult, ALU.add)
                        last.then_inc(d_drained, 1)

                for b in range(B + 1):
                    if b < B:
                        for f in range(FC):
                            n = FC * b + f
                            if not (small and f):
                                dve.wait_ge(u_written, UU * e + (b if small else n) + 1)
                            dve.wait_ge(silu_done, UF * e + n + 1)
                            if b >= 2:
                                dve.wait_ge(d_written, 1 + UDN * e + 2 * (b - 1))
                            else:
                                dve.wait_ge(d_written, 1 + UDN * e)
                            q = FEATURES[f]
                            nc.vector.tensor_tensor(hT[b % 2][0:q, f, :], sg[f][0:q, :], bank_u[f][0:q, :],
                                                    ALU.mult).then_inc(h_ready, 1)
                    if b >= 1:
                        take_down(b - 1)
                nc.vector.sem_inc(used, 1)
            over(dve, body)


def alibi_block(nc, X, XT, ident, qk_dram, w, consts):
    SPLIT = ([0, 1, 2, 0, 1, 2, 0, 1], [0, 0, 0, 1, 1, 1, 2, 2])
    HG = P // DA
    QG = H // HG
    QU = HG * TPB
    LOADS = 16 * 2 * len(SPLIT[0])
    HQ = P // SLOT
    G = H // HQ
    GU = HQ * TPB
    TBL = 2 * T - P
    UNITS = TPB * H
    R = 4
    TURN, VALUE = 3, 3 + TPB
    SPREAD = VALUE + 3
    PV = TILES // 2
    FIRST = PV + 2 * QG
    PROJECT = [QU * g + 3 * TPB for g in range(QG)]
    RING = sorted([(PROJECT[g] + k, "qk"[k], g) for g in range(QG) for k in range(2)] +
                  [(GU * (g + 1) + SPREAD - 2, "sum", g) for g in range(G)])
    RING = [x[1:] for x in RING] + [("out", i) for i in range(TPB // 2)]
    with ExitStack() as ctx:
        sb, ps, sem = pools(nc, ctx)
        wq = sb("c_wq", [P, KC, D])
        wk = sb("c_wk", [P, KC, D])
        wv = sb("c_wv", [P, KC, D])
        wo = sb("c_wo", [P, G, D])
        bq = sb("c_bq", [P, QG])
        bk = sb("c_bk", [P, QG])
        bvr = sb("c_bv", [P, D])
        bor = sb("c_bo", [P, D])
        slopes = sb("c_slopes", [P, H])
        spread = sb("c_spread", [P, P])
        table = sb("c_table", [P, H, TBL])
        V = sb("c_V", [P, TILES, H, DA])
        Vb = sb("c_Vb", [P, TPB, H, SLOT])
        Q = sb("c_Q", [P, H, T], BF16)
        K = sb("c_K", [P, H, T], BF16)
        whole = [sb(f"c_whole{j}", [P, T]) for j in range(2)]
        parts = [sb(f"c_parts{j}", [P, 3, T], BF16) for j in range(2)]
        s = [sb(f"c_s{j}", [P, T]) for j in range(R)]
        pT = [sb(f"c_pT{j}", [P, TPB, T]) for j in range(2)]
        nmax = sb("c_nmax", [P, R])
        oraw = [sb(f"c_oraw{j}", [P, T]) for j in range(2)]
        oT = sb("c_oT", [P, G, T])
        bank_s = [ps(f"c_bank_s{j}", [P, T]) for j in range(2)]
        bank_t = [ps(f"c_bank_t{j}", [P, T]) for j in range(2)]
        bank_o = [ps(f"c_bank_o{j}", [P, T]) for j in range(2)]
        bank_p = [ps(f"c_bank_p{j}", [P, T]) for j in range(2)]
        proj_loaded, rest_loaded = sem("c_proj_loaded"), sem("c_rest_loaded")
        table_loaded = sem("c_table_loaded")
        ones_ready, x_biased = sem("c_ones_ready"), sem("c_x_biased")
        table_ready = sem("c_table_ready")
        p_written, p_drained = sem("c_p_written"), sem("c_p_drained")
        s_written, s_taken = sem("c_s_written"), sem("c_s_taken")
        exp_done = sem("c_exp_done")
        t_written = sem("c_t_written")
        t_taken = [sem(f"c_t_taken{j}") for j in range(2)]
        o_written, o_taken = sem("c_o_written"), sem("c_o_taken")
        oT_ready = sem("c_oT_ready")
        vb_ready = sem("c_vb_ready")
        dve_turn, sp_turn, pool_turn = (sem(f"c_{x}_turn") for x in ("dve", "sp", "pool"))
        cut = sem("c_cut")
        cut_done = sem("c_cut_done")
        stored = [sem(f"c_stored_{x}") for x in "qk"]
        qk_loaded = [sem(f"c_qk_loaded{g}") for g in range(QG)]
        block = ctx.enter_context(nc.Block())

        def unit(b, what, i, last):
            order = [x for x in RING if not last or x[0] in ("sum", "out")]
            n = order.index((what, i))
            return len(RING) * b + (FIRST + n), (FIRST + n) % 2

        @block.gpsimd
        def _(pool):
            nc.gpsimd.sem_inc(cut_done, 2)
            nc.gpsimd.memset(Vb[:, :, :, :], 1.0).then_inc(ones_ready, 1)

            def cut_parts(m, which, b, whole_ready):
                x, part = whole[which], parts[which]
                pool.wait_ge(p_drained, whole_ready)
                if not (isinstance(m, int) and m < 2):
                    pool.wait_ge(stored[which], 8 * m if isinstance(m, int) and which == 0 else
                                 8 * (m - which))
                nc.gpsimd.sem_inc(pool_turn, 1)
                nc.gpsimd.tensor_scalar(part[:, 0, :], x[:, :], 1.0, None, ALU.mult).then_inc(cut, 1)
                pool.wait_ge(cut, 3 * m + 1)
                nc.gpsimd.tensor_tensor(x[:, :], x[:, :], part[:, 0, :], ALU.subtract).then_inc(cut, 1)
                pool.wait_ge(cut, 3 * m + 2)
                nc.gpsimd.sem_inc(pool_turn, 1)
                nc.gpsimd.tensor_scalar(part[:, 1, :], x[:, :], 1.0, None, ALU.mult).then_inc(cut, 1)
                pool.wait_ge(cut, 3 * m + 3)
                nc.gpsimd.tensor_tensor(part[:, 2, :], x[:, :], part[:, 1, :], ALU.subtract).then_inc(cut_done, 1)

            def slope(h):
                nc.gpsimd.tensor_scalar(table[:, h, :], table[:, H - 1, :], slopes[:, h:h + 1], None,
                                        ALU.mult).then_inc(table_ready, 1)

            for g in range(QG):
                for which in range(2):
                    m = 2 * g + which
                    cut_parts(m, which, -1, m + 1 + 2)
                if g == 0:
                    pool.wait_ge(table_loaded, 16 * 3)
                    slope(0)
            for h in range(1, H):
                slope(h)
            nc.gpsimd.tensor_tensor(X[:, :, :], X[:, :, :], bor[:, :].unsqueeze(1).broadcast_to([P, TILES, D]),
                                    ALU.add).then_inc(x_biased, 1)

            def normalise(g, b, last_b):
                n, _ = unit(b, "sum", g, last_b)
                pool.wait_ge(p_drained, n + 1 + 2)
                nc.gpsimd.tensor_tensor(oT[:, g, :], oraw[g % 2][:, :], oT[:, g, :], ALU.mult).then_inc(oT_ready, 1)

            def sequence(b, last_b):
                for what, g in RING:
                    if what in ("q", "k") and not last_b:
                        n, _ = unit(b, what, g, last_b)
                        which = "qk".index(what)
                        cut_parts(2 * QG * b + (2 * QG + 2 * g + which), which, b, n + 1 + 2)
                    elif what == "sum":
                        normalise(g, b, last_b)

            with pool.Fori(0, B - 1) as b:
                sequence(b, False)
            sequence(B - 1, True)

        @block.sync
        def _(sp):
            chunks = "(c p) n -> p c n"
            for dst, src in ((wv[:, :, :], w["L1_attn_WvT"].rearrange(chunks, p=P)),
                             (bvr[:, :], rows(w["L1_attn_bv"])),
                             (wq[:, :, :], w["L1_attn_WqT"].rearrange(chunks, p=P)),
                             (bq[:, :], w["L1_attn_bq"]), (bk[:, :], w["L1_attn_bk"]),
                             (wk[:, :, :], w["L1_attn_WkT"].rearrange(chunks, p=P))):
                sp.dma_start(dst, src).then_inc(proj_loaded, 16)
            for dst, src in ((wo[:, :, :], w["L1_attn_WoT"].rearrange(chunks, p=P)),
                             (spread[:, :], consts["spread"])):
                sp.dma_start(dst, src).then_inc(rest_loaded, 16)
            sp.wait_ge(proj_loaded, 16 * 6)
            sp.wait_ge(rest_loaded, 16 * 2)

            def place(m, g, scores_done):
                for which in range(2):
                    sp.wait_ge(cut_done, m + which + 1 + 2)
                    sp.sem_inc(sp_turn, 1)
                    sp.dma_start(qk_dram[which, g].rearrange("a p n -> p a n"),
                                 parts[which][:, :, :]).then_inc(stored[which], 16)
                for which in range(2):
                    sp.wait_ge(stored[which], 8 * m + 16)
                    sp.sem_inc(sp_turn, 1)
                if scores_done is not None:
                    sp.wait_ge(s_written, scores_done)
                    sp.sem_inc(sp_turn, 1)
                for which in range(2):
                    for c, part in enumerate(SPLIT[which]):
                        sp.dma_start((Q, K)[which][c * DA:(c + 1) * DA, g * HG:(g + 1) * HG, :],
                                     qk_dram[which, g, part].rearrange("(h d) n -> d h n", d=DA)
                                     ).then_inc(qk_loaded[g], 16)

            for g in range(QG):
                place(2 * g, g, None)
            with sp.Fori(0, B - 1) as b:
                for g in range(QG):
                    place(2 * QG * b + (2 * QG + 2 * g), g, UNITS * b + (1 + QU * (g + 1)))
            for g in range(QG):
                sp.wait_ge(qk_loaded[g], LOADS * B)

        @block.tensor
        def _(pe):
            pe.sem_inc(s_written, 1)
            pe.sem_inc(t_written, R)
            pe.sem_inc(o_written, 1)

            def project_head_group(n, g, which, b):
                m = (wq, wk)[which]
                for c in range(KC):
                    last = nc.tensor.matmul(bank_p[n % 2][:, :], m[:, c, g * P:(g + 1) * P],
                                            XT[:, c, bass.ds(b * T, T)], start=(c == 0), stop=(c == KC - 1))
                last.then_inc(p_written, 1)

            pe.wait_ge(proj_loaded, 16 * 6)
            for n in range(2 * QG):
                pe.wait_ge(p_drained, n + 1)
                project_head_group(n, n // 2, n % 2, 0)
            for n in range(PV):
                pe.wait_ge(p_drained, 2 * QG + n + 1)
                for i in range(2):
                    t = 2 * n + i
                    for c in range(KC):
                        last = nc.tensor.matmul(bank_p[n % 2][:, i * D:(i + 1) * D], XT[:, c, t * P:(t + 1) * P],
                                                wv[:, c, :], start=(c == 0), stop=(c == KC - 1))
                last.then_inc(p_written, 1)
            pe.wait_ge(rest_loaded, 16 * 2)

            def scores(u, b):
                h, it = divmod(u, TPB)
                if u % QU == 0:
                    pe.wait_ge(qk_loaded[u // QU], LOADS * (b + 1))
                pe.wait_ge(s_taken, UNITS * b + u + 1)
                nc.tensor.matmul(bank_s[u % 2][:, :], Q[:, h, it * P:(it + 1) * P], K[:, h, :],
                                 start=True, stop=True).then_inc(s_written, 1)

            def turn(u, b):
                pe.wait_ge(exp_done, UNITS * b + u + 1)
                pe.wait_ge(t_taken[u % 2], UNITS // 2 * b + u // 2 + 1)
                for j in range(TPB):
                    last = nc.tensor.transpose(bank_t[u % 2][:, j * P:(j + 1) * P],
                                               s[u % R][:, j * P:(j + 1) * P], ident[:, :])
                last.then_inc(t_written, 1)

            def value(u, b):
                h, j = divmod(u, TPB)
                g, a = divmod(h, HQ)
                if j == 0:
                    for x in t_taken:
                        pe.wait_ge(x, UNITS // 2 * b + TPB // 2 * (h + 1) + 1)
                if u == 0:
                    pe.wait_ge(vb_ready, b + 1)
                if u % GU == 0:
                    pe.wait_ge(o_taken, G * b + g + 1)
                last = nc.tensor.matmul(bank_o[g % 2][a * SLOT:(a + 1) * SLOT, :], Vb[:, j, h, :],
                                        pT[h % 2][:, j, :], start=(j == 0), stop=(j == TPB - 1))
                if u % GU == GU - 1:
                    last.then_inc(o_written, 1)

            def sums(g, b, last_b):
                n, bank = unit(b, "sum", g, last_b)
                pe.wait_ge(o_taken, G * b + g + 1 + 2)
                pe.wait_ge(p_drained, n + 1)
                nc.tensor.matmul(bank_p[bank][:, :], spread[:, :], oraw[g % 2][:, :],
                                 start=True, stop=True).then_inc(p_written, 1)

            def sequence(b, last_b):
                for u in range(UNITS + SPREAD):
                    if u < UNITS:
                        scores(u, b)
                    if 0 <= u - TURN < UNITS:
                        turn(u - TURN, b)
                    if 0 <= u - VALUE < UNITS:
                        value(u - VALUE, b)
                    for g in range(QG):
                        if not last_b and u - PROJECT[g] in (0, 1):
                            which = u - PROJECT[g]
                            n, bank = unit(b, "qk"[which], g, last_b)
                            pe.wait_ge(p_drained, n + 1)
                            project_head_group(bank, g, which, b + 1)
                    v = u - SPREAD + 1
                    if v >= 0 and v % GU == GU - 1:
                        sums(v // GU, b, last_b)
                pe.wait_ge(oT_ready, G * b + G + 2)
                for i in range(TPB // 2):
                    n, bank = unit(b, "out", i, last_b)
                    pe.wait_ge(p_drained, n + 1)
                    for k in range(2):
                        t = 2 * i + k
                        for g in range(G):
                            last = nc.tensor.matmul(bank_p[bank][:, k * D:(k + 1) * D], oT[:, g, t * P:(t + 1) * P],
                                                    wo[:, g, :], start=(g == 0), stop=(g == G - 1))
                    last.then_inc(p_written, 1)

            with pe.Fori(0, B - 1) as b:
                sequence(b, False)
            sequence(B - 1, True)

        @block.scalar
        def _(act):
            for dst, src in ((table[:, H - 1, :], consts["dist"]), (slopes[:, :], rows(w["L1_attn_slopes"])),
                             (bor[:, :], rows(w["L1_attn_bo"]))):
                act.dma_start(dst, src).then_inc(table_loaded, 16)
            nc.scalar.sem_inc(o_taken, 2)

            def take_turn(u, b):
                h, it = divmod(u, TPB)
                act.wait_ge(t_written, UNITS * b + u + 1 + R)
                nc.scalar.activation(pT[h % 2][:, :, it * P:(it + 1) * P],
                                     bank_t[u % 2][:, :].rearrange("p (j q) -> p j q", q=P),
                                     ACT.Copy).then_inc(t_taken[u % 2], 1)

            def sequence(b):
                for u in range(UNITS + SPREAD - 1):
                    if u < UNITS:
                        act.wait_ge(s_taken, UNITS * b + u + 1 + 2)
                        nc.scalar.activation(s[u % R][:, :], s[u % R][:, :], ACT.Exp, scale=-1.0,
                                             bias=nmax[:, u % R:u % R + 1]).then_inc(exp_done, 1)
                    if 0 <= u - TURN < UNITS and (u - TURN) % 2:
                        take_turn(u - TURN, b)
                    if u == 1:
                        act.wait_ge(o_written, 1 + G * b)
                        nc.scalar.activation(Vb[:, :, :, 0:DA], V[:, bass.ds(b * TPB, TPB), :, :],
                                             ACT.Copy).then_inc(vb_ready, 1)
                    v = u - VALUE
                    if v >= 0 and v % GU == GU - 1:
                        g = v // GU
                        act.wait_ge(o_written, 1 + G * b + g + 1)
                        act.wait_ge(oT_ready, G * b + g + 1)
                        nc.scalar.activation(oraw[g % 2][:, :], bank_o[g % 2][:, :], ACT.Copy).then_inc(o_taken, 1)

            act.wait_ge(ones_ready, 1)
            act.wait_ge(p_drained, FIRST + 2)
            with act.Fori(0, B) as b:
                sequence(b)

        @block.vector
        def _(dve):
            nc.vector.sem_inc(p_drained, 2)
            nc.vector.sem_inc(s_taken, 2)
            for x in t_taken:
                nc.vector.sem_inc(x, 1)
            nc.vector.sem_inc(oT_ready, 2)

            def drain_head_group(bank, g, which, m):
                dve.wait_ge(cut_done, m + 1)
                nc.vector.tensor_scalar(whole[which][:, :], bank_p[bank][:, :], (bq, bk)[which][:, g:g + 1],
                                        1.0 if which else -float(DA) ** -0.5, ALU.add, ALU.mult).then_inc(p_drained, 1)

            dve.wait_ge(proj_loaded, 16 * 6)
            for n in range(2 * QG):
                dve.wait_ge(p_written, n + 1)
                drain_head_group(n % 2, n // 2, n % 2, n)
            for n in range(PV):
                dve.wait_ge(p_written, 2 * QG + n + 1)
                nc.vector.tensor_tensor(V[:, 2 * n:2 * n + 2, :, :].rearrange("p i h d -> p i (h d)"),
                                        bank_p[n % 2][:, :].rearrange("p (i n) -> p i n", n=D),
                                        bvr[:, :].unsqueeze(1).broadcast_to([P, 2, D]), ALU.add).then_inc(p_drained, 1)

            def take_scores(u, b):
                h, it = divmod(u, TPB)
                dve.wait_ge(s_written, 1 + UNITS * b + u + 1)
                dve.wait_ge(t_written, UNITS * b + u + 1)
                if it == 0:
                    dve.wait_ge(table_ready, h + 1)
                off = T - P - it * P
                nc.vector.sem_inc(dve_turn, 1)
                nc.vector.tensor_tensor_reduce(out=s[u % R][:, :], in0=bank_s[u % 2][:, :],
                                               in1=table[:, h, off:off + T], scale=1.0, scalar=3.0e38,
                                               op0=ALU.add, op1=ALU.min,
                                               accum_out=nmax[:, u % R:u % R + 1]).then_inc(s_taken, 1)

            def take_turn(u, b):
                h, it = divmod(u, TPB)
                dve.wait_ge(t_written, UNITS * b + u + 1 + R)
                nc.vector.tensor_copy(pT[h % 2][:, :, it * P:(it + 1) * P],
                                      bank_t[u % 2][:, :].rearrange("p (j q) -> p j q", q=P)
                                      ).then_inc(t_taken[u % 2], 1)

            def invert_sums(g, b, last_b, pieces):
                n, bank = unit(b, "sum", g, last_b)
                if pieces[0] == 0:
                    dve.wait_ge(p_written, n + 1)
                for i in pieces:
                    v = slice(i * P, (i + 1) * P)
                    last = nc.vector.reciprocal(oT[:, g, v], bank_p[bank][:, v])
                if pieces[-1] == TPB - 1:
                    last.then_inc(p_drained, 1)

            def sequence(b, last_b):
                for u in range(UNITS + SPREAD):
                    if u < UNITS:
                        take_scores(u, b)
                    if 0 <= u - TURN < UNITS and (u - TURN) % 2 == 0:
                        take_turn(u - TURN, b)
                    for g in range(QG):
                        if not last_b and u - PROJECT[g] in (0, 1):
                            which = u - PROJECT[g]
                            n, bank = unit(b, "qk"[which], g, last_b)
                            dve.wait_ge(p_written, n + 1)
                            drain_head_group(bank, g, which, 2 * QG * b + (2 * QG + 2 * g + which))
                    g, i = divmod(u - (GU + SPREAD - 2), GU)
                    if g >= 0 and i < (TPB if g < G - 1 else 1):
                        invert_sums(g, b, last_b, [i] if g < G - 1 else range(TPB))
                dve.wait_ge(x_biased, 1)
                for i in range(TPB // 2):
                    n, bank = unit(b, "out", i, last_b)
                    dve.wait_ge(p_written, n + 1)
                    x = X[:, bass.ds(b * TPB + 2 * i, 2), :]
                    nc.vector.tensor_tensor(x, bank_p[bank][:, :].rearrange("p (i n) -> p i n", n=D), x,
                                            ALU.add).then_inc(p_drained, 1)

            with dve.Fori(0, B - 1) as b:
                sequence(b, False)
            sequence(B - 1, True)


def latent_block(nc, X, XT, ident, w, consts):
    UNITS = TILES
    R = 4
    TURN, VALUE = 2, 3
    PROJ = 3 * B
    OUT = 2 * B
    STEPS = UNITS + VALUE + 2
    ring = {u: [] for u in range(STEPS)}
    for b in range(B):
        u = TPB * (b + 1)
        ring[u].append(("proj", b, 0))
        ring[u + 1].append(("proj", b, 1))
        ring[u + VALUE].append(("proj", b, 2))
        ring[u + VALUE + 1].append(("out", b, 0))
        ring[min(u + VALUE + 2, STEPS - 1)].append(("out", b, 1))
    with ExitStack() as ctx:
        sb, ps, sem = pools(nc, ctx)
        W = sb("l_W", [P, 3, KC, NOPE])
        wo = sb("l_wo", [P, D])
        Q = sb("l_Q", [P, N])
        K = sb("l_K", [P, N])
        V = sb("l_V", [P, TILES, VD])
        mask = sb("l_mask", [P, T])
        s = [sb(f"l_s{j}", [P, T]) for j in range(R)]
        pr = [sb(f"l_p{j}", [P, T]) for j in range(R)]
        pT = [sb(f"l_pT{j}", [P, T]) for j in range(2)]
        nmax = sb("l_nmax", [P, R])
        rsum = sb("l_rsum", [P, TILES])
        rinv = sb("l_rinv", [P, TILES])
        oT = sb("l_oT", [P, TILES, P])
        bank_p = [ps(f"l_bank_p{j}", [P, T]) for j in range(2)]
        bank_s = [ps(f"l_bank_s{j}", [P, T]) for j in range(2)]
        bank_t = [ps(f"l_bank_t{j}", [P, T]) for j in range(2)]
        bank_o = [ps(f"l_bank_o{j}", [P, TPB, P]) for j in range(2)]
        mask_loaded = sem("l_mask_loaded")
        w_loaded = [sem(f"l_w_loaded_{x}") for x in "qkvo"]
        sp_turn, dve_turn = sem("l_sp_turn"), sem("l_dve_turn")
        p_written = sem("l_p_written")
        copied, added = sem("l_copied"), sem("l_added")
        s_written, s_taken, exp_done = (sem("l_" + x) for x in ("s_written", "s_taken", "exp_done"))
        t_written, t_taken = sem("l_t_written"), sem("l_t_taken")
        o_written, o_taken = sem("l_o_written"), sem("l_o_taken")
        rinv_ready = sem("l_rinv_ready")
        block = ctx.enter_context(nc.Block())

        def order(last):
            return [x for u in range(STEPS) for x in ring[u] if not last or x[0] == "out"]

        def written(h, x, last):
            return (PROJ + OUT) * h + (PROJ + order(last).index(x) + 1)

        def bank_of(x, last):
            return bank_p[order(last).index(x) % 2]

        @block.sync
        def _(sp):
            def load(k, h):
                nm, first, step = (("q_wT", 0, QHD), ("kv_wT", 0, NOPE), ("kv_wT", H * NOPE, VD))[k]
                src = w["L1_ffn_" + nm].rearrange("(c p) n -> p c n", p=P)
                sp.dma_start(W[:, k, :, :], src[:, :, bass.ds(h * step + first, NOPE)]).then_inc(w_loaded[k], 16)

            def load_out(h):
                sp.dma_start(wo[:, :], w["L1_ffn_o_wT"][bass.ds(h * VD, VD), :]).then_inc(w_loaded[3], 16)

            for k in range(3):
                load(k, 0)
            sp.dma_start(mask[:, :], consts["causal"]).then_inc(mask_loaded, 16)
            sp.wait_ge(mask_loaded, 16)
            with sp.Fori(1, H) as h:
                for k in range(3):
                    sp.wait_ge(copied, PROJ * h + (k - 2))
                    sp.sem_inc(sp_turn, 1)
                    load(k, h)
                sp.wait_ge(added, OUT * h)
                sp.sem_inc(sp_turn, 1)
                load_out(h - 1)
            sp.wait_ge(added, OUT * H)
            load_out(H - 1)

        @block.tensor
        def _(pe):
            pe.sem_inc(t_written, R)
            pe.sem_inc(s_written, 1)
            pe.sem_inc(o_written, 1)

            def project(bank, b, k):
                if k < 2:
                    for c in range(KC):
                        last = nc.tensor.matmul(bank[:, :], W[:, k, c, :], XT[:, c, b * T:(b + 1) * T],
                                                start=(c == 0), stop=(c == KC - 1))
                else:
                    for i in range(TPB):
                        t = b * TPB + i
                        for c in range(KC):
                            last = nc.tensor.matmul(bank[:, i * VD:(i + 1) * VD], XT[:, c, t * P:(t + 1) * P],
                                                    W[:, k, c, :], start=(c == 0), stop=(c == KC - 1))
                last.then_inc(p_written, 1)

            for n in range(PROJ):
                b, k = divmod(n, 3)
                if b == 0:
                    pe.wait_ge(w_loaded[k], 16)
                if n >= 2:
                    pe.wait_ge(copied, n - 1)
                project(bank_p[n % 2], b, k)
            pe.wait_ge(copied, PROJ)

            def scores(u, h):
                b, it = divmod(u, TPB)
                if it == 0:
                    pe.wait_ge(copied, PROJ * h + 3 * b + 2)
                pe.wait_ge(s_taken, UNITS * h + u + 1)
                nc.tensor.matmul(bank_s[u % 2][:, 0:(it + 1) * P], Q[:, u * P:(u + 1) * P],
                                 K[:, b * T:b * T + (it + 1) * P], start=True, stop=True).then_inc(s_written, 1)

            def turn(u, h):
                pe.wait_ge(exp_done, UNITS * h + u + 1 + R)
                pe.wait_ge(t_taken, UNITS * h + u + 1)
                for j in range(u % TPB + 1):
                    last = nc.tensor.transpose(bank_t[u % 2][:, j * P:(j + 1) * P],
                                               pr[u % R][:, j * P:(j + 1) * P], ident[:, :])
                last.then_inc(t_written, 1)

            def value(u, h):
                b, it = divmod(u, TPB)
                if it == 0:
                    pe.wait_ge(copied, PROJ * h + 3 * b + 3)
                    pe.wait_ge(o_taken, B * h + b + 1)
                pe.wait_ge(t_taken, UNITS * h + u + 1 + 2)
                for j in range(it + 1):
                    last = nc.tensor.matmul(bank_o[b % 2][:, it, :], V[:, b * TPB + j, :],
                                            pT[u % 2][:, j * P:(j + 1) * P], start=(j == 0), stop=(j == it))
                if it == TPB - 1:
                    last.then_inc(o_written, 1)

            def wait_for_bank(x, h, last_h):
                units = order(last_h)
                n = units.index(x)
                if n >= 2 or not last_h:
                    kind, b, k = units[n - 2]
                else:
                    kind, b, k = order(False)[n - 2]
                before = 0 if n >= 2 else 1
                if kind == "proj":
                    pe.wait_ge(copied, PROJ * h + (PROJ * (1 - before) + 3 * b + k + 1))
                else:
                    pe.wait_ge(added, OUT * h + (OUT * (1 - before) + 2 * b + k + 1))

            def head(h, last_h):
                for u in range(STEPS):
                    if u < UNITS:
                        scores(u, h)
                    if 0 <= u - TURN < UNITS:
                        turn(u - TURN, h)
                    if 0 <= u - VALUE < UNITS:
                        value(u - VALUE, h)
                    for x in ring[u]:
                        kind, b, k = x
                        if last_h and kind == "proj":
                            continue
                        wait_for_bank(x, h, last_h)
                        bank = bank_of(x, last_h)
                        if kind == "proj":
                            if b == 0:
                                pe.wait_ge(w_loaded[k], 16 * h + 32)
                            project(bank, b, k)
                            continue
                        if (b, k) == (0, 0):
                            pe.wait_ge(w_loaded[3], 16 * h + 16)
                        if k == 0:
                            pe.wait_ge(o_taken, B * h + b + 1 + 2)
                        for i in range(2):
                            last = nc.tensor.matmul(bank[:, i * D:(i + 1) * D], oT[:, b * TPB + 2 * k + i, :],
                                                    wo[:, :], start=True, stop=True)
                        last.then_inc(p_written, 1)

            with pe.Fori(0, H - 1) as h:
                head(h, False)
            head(H - 1, True)

        @block.scalar
        def _(act):
            nc.scalar.sem_inc(exp_done, R)
            nc.scalar.sem_inc(o_taken, 2)

            def copy(bank, b, k):
                if k < 2:
                    nc.scalar.activation((Q, K)[k][:, b * T:(b + 1) * T], bank[:, :], ACT.Copy,
                                         scale=-float(QHD) ** -0.5 if k == 0 else 1.0).then_inc(copied, 1)
                else:
                    nc.scalar.activation(V[:, b * TPB:(b + 1) * TPB, :].rearrange("p t n -> p (t n)"),
                                         bank[:, :], ACT.Copy).then_inc(copied, 1)

            for n in range(PROJ):
                act.wait_ge(p_written, n + 1)
                copy(bank_p[n % 2], *divmod(n, 3))

            def head(h, last_h):
                for u in range(STEPS):
                    if u < UNITS:
                        w_ = (u % TPB + 1) * P
                        act.wait_ge(s_taken, UNITS * h + u + 1 + 2)
                        act.wait_ge(t_written, UNITS * h + u + 1)
                        if u % TPB == 0:
                            act.wait_ge(rinv_ready, B * h + u // TPB + 1)
                        nc.scalar.activation(pr[u % R][:, 0:w_], s[u % R][:, 0:w_], ACT.Exp, scale=-1.0,
                                             bias=nmax[:, u % R:u % R + 1],
                                             accum_out=rsum[:, u:u + 1]).then_inc(exp_done, 1)
                    v = u - VALUE
                    if v >= 0 and v % TPB == TPB - 1:
                        b = v // TPB
                        act.wait_ge(o_written, 1 + B * h + b + 1)
                        act.wait_ge(added, OUT * h + 2 * b + 2)
                        nc.scalar.activation(oT[:, b * TPB:(b + 1) * TPB, :], bank_o[b % 2][:, :, :],
                                             ACT.Copy).then_inc(o_taken, 1)
                    for x in ring[u]:
                        if x[0] == "proj" and not last_h:
                            act.wait_ge(p_written, written(h, x, last_h))
                            copy(bank_of(x, last_h), *x[1:])

            with act.Fori(0, H - 1) as h:
                head(h, False)
            head(H - 1, True)

        @block.vector
        def _(dve):
            nc.vector.sem_inc(added, OUT)
            nc.vector.sem_inc(rinv_ready, B)
            nc.vector.sem_inc(s_taken, 2)
            nc.vector.sem_inc(t_taken, 2)
            dve.wait_ge(mask_loaded, 16)

            def take_scores(u, h):
                w_ = (u % TPB + 1) * P
                dve.wait_ge(s_written, 1 + UNITS * h + u + 1)
                dve.wait_ge(exp_done, UNITS * h + u + 1)
                nc.vector.sem_inc(dve_turn, 1)
                nc.vector.tensor_tensor_reduce(out=s[u % R][:, 0:w_], in0=bank_s[u % 2][:, 0:w_],
                                               in1=mask[:, T - w_:T], scale=1.0, scalar=3.0e38,
                                               op0=ALU.add, op1=ALU.min,
                                               accum_out=nmax[:, u % R:u % R + 1]).then_inc(s_taken, 1)

            def take_turn(u, h):
                w_ = (u % TPB + 1) * P
                dve.wait_ge(t_written, UNITS * h + u + 1 + R)
                nc.vector.tensor_copy(pT[u % 2][:, 0:w_], bank_t[u % 2][:, 0:w_]).then_inc(t_taken, 1)

            def head(h, last_h):
                for u in range(STEPS):
                    if u < UNITS:
                        take_scores(u, h)
                    if 0 <= u - TURN < UNITS:
                        take_turn(u - TURN, h)
                    for x in ring[u]:
                        kind, b, k = x
                        if kind != "out":
                            continue
                        if k == 0:
                            dve.wait_ge(exp_done, UNITS * h + TPB * (b + 1) + R)
                            nc.vector.reciprocal(rinv[:, TPB * b:TPB * (b + 1)],
                                                 rsum[:, TPB * b:TPB * (b + 1)]).then_inc(rinv_ready, 1)
                            dve.wait_ge(rinv_ready, B * h + b + 1 + B)
                        dve.wait_ge(p_written, written(h, x, last_h))
                        for i in range(2):
                            t = b * TPB + 2 * k + i
                            last = nc.vector.scalar_tensor_tensor(X[:, t, :], bank_of(x, last_h)[:, i * D:(i + 1) * D],
                                                                  rinv[:, t:t + 1], X[:, t, :], ALU.mult, ALU.add)
                        last.then_inc(added, 1)

            with dve.Fori(0, H - 1) as h:
                head(h, False)
            head(H - 1, True)


def sum_block(nc, X, Y):
    with ExitStack() as ctx:
        block = ctx.enter_context(nc.Block())

        @block.vector
        def _(dve):
            nc.vector.tensor_tensor(X[:, :, :], X[:, :, :], Y[:, :, :], ALU.add)


def last_part(nc, X, HID, XT, ident, w, consts):
    norm_block(nc, "n4_", X, XT, ident, 1e-5, rms_weight=w["L1_ffn_ln1_w"], rows_out=HID, rms_eps=1e-6)
    latent_block(nc, HID, XT, ident, w, consts)
    norm_block(nc, "n6_", HID, XT, ident, 1e-6, rms_weight=w["L1_ffn_ln2_w"])
    with ExitStack() as part:
        weights = part.enter_context(nc.sbuf_tensor("e1_weights", [P, E1 + NSH, TILES], F32))
        router_block(nc, "r1_", XT, w["L1_ffn_gate_wT"], E1, consts["rank1"], weights)
        experts_block(nc, "e1_", HID, [(0, E1 + NSH, XT)], weights,
                      w["L1_ffn_gate_up"], w["L1_ffn_down"], I1 - P)
    sum_block(nc, X, HID)


def clear_block(nc):
    used = sorted(nc.released_uncleared_semaphores)
    assert used == list(range(used[0], used[-1] + 1))
    with ExitStack() as ctx:
        block = ctx.enter_context(nc.Block())

        @block.gpsimd
        def _(pool):
            pool.sem_clear(range(used[0], used[-1] + 1))


def store_block(nc, X, out):
    with ExitStack() as ctx:
        sb, ps, sem = pools(nc, ctx)
        stored = sem("x_stored")
        block = ctx.enter_context(nc.Block())

        @block.sync
        def _(sp):
            sp.dma_start(out[:, 0:TILES // 2, :], X[:, 0:TILES // 2, :]).then_inc(stored, 16)
            sp.wait_ge(stored, 32)

        @block.scalar
        def _(act):
            act.dma_start(out[:, TILES // 2:, :], X[:, TILES // 2:, :]).then_inc(stored, 16)


def network(nc, w, consts, decay_dram, qk_dram, out):
    with ExitStack() as ctx:
        sb, ps, sem = pools(nc, ctx)
        X = sb("X", [P, TILES, D])
        XT = sb("XT", [P, KC, N])
        ident = sb("ident", [P, P])
        as_tiles = "b (c p) d -> p (b c) d"
        load_block(nc, X, w["L0_attn_hidden_states"].rearrange(as_tiles, p=P), ident, consts["ident"])
        norm_block(nc, "n0_", X, XT, ident, 1e-5)
        with ExitStack() as part:
            beta = part.enter_context(nc.sbuf_tensor("beta", [P, H, TILES], F32))
            decay_block(nc, XT, beta, decay_dram, w)
            delta_block(nc, X, XT, beta, ident, decay_dram, w, consts)
        with ExitStack() as part:
            kept = [part.enter_context(nc.sbuf_tensor("kept_" + x, [P, TILES], F32)) for x in ("scale", "shift")]
            norm_block(nc, "n1_", X, XT, ident, 1e-5, kept=kept)
            weights = part.enter_context(nc.sbuf_tensor("e0_weights", [P, E0 + 1, TILES], F32))
            score = part.enter_context(nc.sbuf_tensor("score", [P, TILES], F32))
            XS = part.enter_context(nc.sbuf_tensor("XS", [P, KC, N], F32))
            router_block(nc, "r0_", XT, w["L0_ffn_router_w"], E0, consts["rank0"], weights, score)
            norm_block(nc, "n2_", X, XS, ident, 1e-5, scale_by=score, kept=kept)
            experts_block(nc, "e0_", X, [(0, E0, XS), (E0, 1, XT)], weights,
                          w["L0_ffn_gate_up"], w["L0_ffn_down"], F0 - P)
        clear_block(nc)
        norm_block(nc, "n3_", X, XT, ident, 1e-5)
        alibi_block(nc, X, XT, ident, qk_dram, w, consts)
        with ExitStack() as part:
            HID = part.enter_context(nc.sbuf_tensor("HID", [P, TILES, D], F32))
            last_part(nc, X, HID, XT, ident, w, consts)
        store_block(nc, X, out.rearrange(as_tiles, p=P))


def constants():
    p = np.arange(P)
    level = np.zeros((P, LEVELS, 4, HALF), np.float32)
    for l in range(LEVELS):
        s = 1 << l
        u = np.arange(HALF)
        level[:, l, :, :] = (((p[:, None] // s) % 2 == 0) & (p[:, None] // (2 * s) == u[None, :] // s))[:, None, :]
    dist = np.abs(np.arange(2 * T - P)[None, :] - (T - P) - p[:, None]).astype(np.float32)

    spread = (p[:, None] == SLOT * (p[None, :] // SLOT) + DA).astype(np.float32)

    def rank(E):
        return np.ascontiguousarray(np.broadcast_to((E - np.arange(E)).astype(np.float32), (P, TILES, E)))

    return {
        "ident": np.eye(P, dtype=np.float32),
        "level_mask": level.reshape(P, LEVELS, 4 * HALF),
        "dist": dist,
        "spread": spread,
        "causal": np.where(np.arange(T)[None, :] - (T - P) <= p[:, None], 0.0, -NEG).astype(np.float32),
        "rank0": rank(E0),
        "rank1": rank(E1),
    }


def packed(gate, up):
    if gate.shape[2] == 2 * P:
        return np.concatenate([gate, up], axis=2)
    second = gate.shape[2] - P
    pad = np.zeros(gate.shape[:2] + (HALF - second,), gate.dtype)
    return np.concatenate([gate[:, :, :P], up[:, :, :P], up[:, :, P:], pad, gate[:, :, P:]], axis=2)


def layouts(x):
    out = {k: x[k] for k in (
        "L0_attn_hidden_states", "L0_attn_Wq", "L0_attn_Wk", "L0_attn_Wv", "L0_attn_conv_q", "L0_attn_conv_k",
        "L0_attn_conv_v", "L0_attn_Wf1", "L0_attn_Wf2", "L0_attn_Wb", "L0_attn_A_log", "L0_attn_dt_bias",
        "L0_attn_Wg", "L0_attn_bg", "L0_attn_norm_w", "L0_attn_Wo", "L0_ffn_router_w", "L1_attn_bv", "L1_attn_bo", "L1_attn_slopes", "L1_ffn_ln1_w", "L1_ffn_ln2_w")}
    gate, up, down = (np.concatenate([x[f"L0_ffn_{part}_w"], x[f"L0_ffn_shared_{part}_w"][None]])
                      for part in ("gate", "up", "down"))
    out["L0_ffn_gate_up"], out["L0_ffn_down"] = packed(gate, up), down
    for m in ("Wq", "Wk", "Wv"):
        out[f"L1_attn_{m}T"] = x[f"L1_attn_{m}"].T
    wide = np.zeros((H, SLOT, D), x["L1_attn_Wo"].dtype)
    wide[:, :DA] = x["L1_attn_Wo"].T.reshape(H, DA, D)
    out["L1_attn_WoT"] = wide.reshape(H * SLOT, D)
    for m in ("bq", "bk"):
        out[f"L1_attn_{m}"] = x[f"L1_attn_{m}"].reshape(-1, P).T
    for m in ("q_w", "kv_w", "o_w", "gate_w"):
        out[f"L1_ffn_{m}T"] = x[f"L1_ffn_{m}"].T
    w1 = x["L1_ffn_w1"].reshape(E1, 2, I1, D)
    sh = x["L1_ffn_sh_gu_w"].reshape(2, NSH, I1, D)
    gate, up = (np.concatenate([w1[:, n], sh[n]]).transpose(0, 2, 1) for n in range(2))
    out["L1_ffn_gate_up"] = packed(gate, up)
    down = x["L1_ffn_sh_down_w"].reshape(D, NSH, I1).transpose(1, 2, 0)
    out["L1_ffn_down"] = np.concatenate([x["L1_ffn_w2"].transpose(0, 2, 1), down])
    return {k: np.ascontiguousarray(v) for k, v in out.items()}


def kernel(**inputs):
    import concourse.bacc as _bacc
    from concourse.bass_utils import run_bass_kernel_spmd as _run

    nc = _bacc.Bacc("TRN2", target_bir_lowering=False, num_devices=1)
    arrays = {}

    def dram(name, a):
        arrays[name] = a
        return nc.dram_tensor(name, a.shape, mybir.dt.from_np(a.dtype), kind="ExternalInput").ap()

    x = {k: np.asarray(v) for k, v in inputs.items()}
    w = {k: dram("in_" + k, v) for k, v in layouts(x).items()}
    consts = {k: dram("const_" + k, v) for k, v in constants().items()}
    decay_dram = nc.dram_tensor("decay", (LEVELS + 2, P, N), F32, kind="Internal").ap()
    out = nc.dram_tensor("out_0_dram", (B, T, D), F32, kind="ExternalOutput").ap()
    qk_dram = nc.dram_tensor("qk_parts", (2, 2, 3, P, T), BF16, kind="Internal").ap()
    network(nc, w, consts, decay_dram, qk_dram, out)
    r = _run(nc, [arrays], core_ids=[0])
    return r.results[0]["out_0_dram"]
```
